# Optimizing a Trainium2 kernel written in Bass

```python
import numpy as np
import jax
import jax.numpy as jnp

def _softmax(x, axis=-1):
    return jax.nn.softmax(x, axis=axis)

def _gelu(x):
    return jax.nn.gelu(x, approximate=True)

def _silu(x):
    return jax.nn.silu(x)

def _sigmoid(x):
    return jax.nn.sigmoid(x)

def _layernorm(x, axis=-1, eps=1e-05):
    m = jnp.mean(x, axis=axis, keepdims=True)
    v = jnp.var(x, axis=axis, keepdims=True)
    return (x - m) / jnp.sqrt(v + eps)

def _scatter_add(tgt, idx, src, axis=0):
    return tgt.at[idx].add(src)

def _segment_sum(src, seg, n):
    return jax.ops.segment_sum(src, seg, n)
kernel_name = 'mk_adaln_d1_jaxref_r8_9707ab'

def setup_inputs(seed: int=0):
    np.random.seed(seed)
    _w = jnp.asarray

    def _L0_attn_setup():
        import jax, jax.numpy as jnp
        import numpy as np
        B, S, DM = (2, 128, 256)
        H, HD, RD = (16, 128, 64)
        DQL, DKVL = (48, 64)
        THETA = 10000.0
        EPS = 1e-06

        def _rope_tables(seq, dim, theta):
            freqs = 1.0 / theta ** (jnp.arange(0, dim, 2, dtype=jnp.float32) / dim)
            t = jnp.arange(seq, dtype=jnp.float32)
            ang = jnp.outer(t, freqs)
            return (jnp.cos(ang), jnp.sin(ang))

        def _apply_rope(x, cos, sin):
            xr = x.reshape(x.shape[:-1] + (-1, 2))
            xe, xo = (xr[..., 0], xr[..., 1])
            c = cos[None, :, None, :]
            s = sin[None, :, None, :]
            return jnp.stack([xe * c - xo * s, xe * s + xo * c], axis=-1).reshape(x.shape)

        def _rmsnorm(x, w):
            return x * jax.lax.rsqrt(jnp.mean(x * x, axis=-1, keepdims=True) + EPS) * w

        def _reference_tuple_inner(x, Wq_down, q_norm_w, Wq_up, Wq_rope, Wkv_down, kv_norm_w, Wk_up, Wv_up, Wk_rope, Wout):
            b, s, _ = x.shape
            cos, sin = _rope_tables(s, RD, THETA)
            c_q = _rmsnorm(x @ Wq_down, q_norm_w)
            q = (c_q @ Wq_up).reshape(b, s, H, HD).transpose(0, 2, 1, 3)
            q_rope = _apply_rope((x @ Wq_rope).reshape(b, s, H, RD), cos, sin)
            q_rope = q_rope.transpose(0, 2, 1, 3)
            c_kv = _rmsnorm(x @ Wkv_down, kv_norm_w)
            k = (c_kv @ Wk_up).reshape(b, s, H, HD).transpose(0, 2, 1, 3)
            v = (c_kv @ Wv_up).reshape(b, s, H, HD).transpose(0, 2, 1, 3)
            k_rope = _apply_rope((x @ Wk_rope).reshape(b, s, H, RD), cos, sin)
            k_rope = k_rope.transpose(0, 2, 1, 3)
            scale = (HD + RD) ** (-0.5)
            scores = (jnp.einsum('bhqd,bhkd->bhqk', q, k) + jnp.einsum('bhqd,bhkd->bhqk', q_rope, k_rope)) * scale
            attn = jax.nn.softmax(scores, axis=-1)
            out = jnp.einsum('bhqk,bhkd->bhqd', attn, v)
            out = out.transpose(0, 2, 1, 3).reshape(b, s, H * HD) @ Wout
            return (out, attn)
        key = jax.random.key(seed)
        ks = jax.random.split(key, 9)
        sc = 0.02
        return {'x': jax.random.normal(ks[0], (B, S, DM), dtype=jnp.float32), 'Wq_down': jax.random.normal(ks[1], (DM, DQL), dtype=jnp.float32) * sc, 'q_norm_w': jnp.ones((DQL,), dtype=jnp.float32), 'Wq_up': jax.random.normal(ks[2], (DQL, H * HD), dtype=jnp.float32) * sc, 'Wq_rope': jax.random.normal(ks[3], (DM, H * RD), dtype=jnp.float32) * sc, 'Wkv_down': jax.random.normal(ks[4], (DM, DKVL), dtype=jnp.float32) * sc, 'kv_norm_w': jnp.ones((DKVL,), dtype=jnp.float32), 'Wk_up': jax.random.normal(ks[5], (DKVL, H * HD), dtype=jnp.float32) * sc, 'Wv_up': jax.random.normal(ks[6], (DKVL, H * HD), dtype=jnp.float32) * sc, 'Wk_rope': jax.random.normal(ks[7], (DM, H * RD), dtype=jnp.float32) * sc, 'Wout': jax.random.normal(ks[8], (H * HD, DM), dtype=jnp.float32) * sc}
    _L0_attn_in = _L0_attn_setup()

    def _L0_ffn_setup():
        import jax, jax.numpy as jnp
        import numpy as np
        N_GROUPS = 4
        TOPK_GROUPS = 2
        TOPK = 4
        ROUTE_SCALE = 1.0

        def _gate(xt, gate_w):
            T = xt.shape[0]
            E = gate_w.shape[0]
            scores = jax.nn.sigmoid(xt @ gate_w.T)
            original_scores = scores
            sg = scores.reshape(T, N_GROUPS, E // N_GROUPS)
            group_scores = sg.max(axis=-1)
            _, gidx = jax.lax.top_k(group_scores, TOPK_GROUPS)
            gmask = jax.nn.one_hot(gidx, N_GROUPS, dtype=scores.dtype).sum(axis=1)
            masked = (sg * gmask[:, :, None]).reshape(T, E)
            _, idx = jax.lax.top_k(masked, TOPK)
            w = jnp.take_along_axis(original_scores, idx, axis=-1)
            w = w / w.sum(axis=-1, keepdims=True) * ROUTE_SCALE
            return (w, idx)
        key = jax.random.key(seed)
        ks = jax.random.split(key, 8)
        B, S, D = (1, 256, 256)
        E, I = (16, 176)
        SH = 2 * I
        s = 0.02
        return {'x': jax.random.normal(ks[0], (B, S, D), dtype=jnp.float32), 'gate_w': jax.random.normal(ks[1], (E, D), dtype=jnp.float32) * s, 'W1': jax.random.normal(ks[2], (E, I, D), dtype=jnp.float32) * s, 'W2': jax.random.normal(ks[3], (E, D, I), dtype=jnp.float32) * s, 'W3': jax.random.normal(ks[4], (E, I, D), dtype=jnp.float32) * s, 'Ws1': jax.random.normal(ks[5], (SH, D), dtype=jnp.float32) * s, 'Ws2': jax.random.normal(ks[6], (D, SH), dtype=jnp.float32) * s, 'Ws3': jax.random.normal(ks[7], (SH, D), dtype=jnp.float32) * s}
    _L0_ffn_in = _L0_ffn_setup()
    _L0_c = _w((lambda *s: np.random.randn(*s).astype(np.float32) * 0.05)(4, 256))
    _L0_wmod = _w((lambda *s: np.random.randn(*s).astype(np.float32) * 0.05)(256, 6 * 256) * 256 ** (-0.5))
    _d = {'L0_attn_x': _L0_attn_in['x'], 'L0_attn_Wq_down': _L0_attn_in['Wq_down'], 'L0_attn_q_norm_w': _L0_attn_in['q_norm_w'], 'L0_attn_Wq_up': _L0_attn_in['Wq_up'], 'L0_attn_Wq_rope': _L0_attn_in['Wq_rope'], 'L0_attn_Wkv_down': _L0_attn_in['Wkv_down'], 'L0_attn_kv_norm_w': _L0_attn_in['kv_norm_w'], 'L0_attn_Wk_up': _L0_attn_in['Wk_up'], 'L0_attn_Wv_up': _L0_attn_in['Wv_up'], 'L0_attn_Wk_rope': _L0_attn_in['Wk_rope'], 'L0_attn_Wout': _L0_attn_in['Wout'], 'L0_ffn_gate_w': _L0_ffn_in['gate_w'], 'L0_ffn_W1': _L0_ffn_in['W1'], 'L0_ffn_W2': _L0_ffn_in['W2'], 'L0_ffn_W3': _L0_ffn_in['W3'], 'L0_ffn_Ws1': _L0_ffn_in['Ws1'], 'L0_ffn_Ws2': _L0_ffn_in['Ws2'], 'L0_ffn_Ws3': _L0_ffn_in['Ws3'], 'L0_c': _L0_c, 'L0_wmod': _L0_wmod}
    _x0 = _d['L0_attn_x']
    _d['L0_attn_x'] = jax.random.normal(jax.random.fold_in(jax.random.key(seed), 1), (4, 512, 256), dtype=_x0.dtype)
    del _x0
    return _d

def reference(L0_attn_x, L0_attn_Wq_down, L0_attn_q_norm_w, L0_attn_Wq_up, L0_attn_Wq_rope, L0_attn_Wkv_down, L0_attn_kv_norm_w, L0_attn_Wk_up, L0_attn_Wv_up, L0_attn_Wk_rope, L0_attn_Wout, L0_ffn_gate_w, L0_ffn_W1, L0_ffn_W2, L0_ffn_W3, L0_ffn_Ws1, L0_ffn_Ws2, L0_ffn_Ws3, L0_c, L0_wmod):

    def _L0_attn_ref(x, Wq_down, q_norm_w, Wq_up, Wq_rope, Wkv_down, kv_norm_w, Wk_up, Wv_up, Wk_rope, Wout):
        import jax, jax.numpy as jnp
        import numpy as np
        B, S, DM = (2, 128, 256)
        H, HD, RD = (16, 128, 64)
        DQL, DKVL = (48, 64)
        THETA = 10000.0
        EPS = 1e-06

        def _rope_tables(seq, dim, theta):
            freqs = 1.0 / theta ** (jnp.arange(0, dim, 2, dtype=jnp.float32) / dim)
            t = jnp.arange(seq, dtype=jnp.float32)
            ang = jnp.outer(t, freqs)
            return (jnp.cos(ang), jnp.sin(ang))

        def _apply_rope(x, cos, sin):
            xr = x.reshape(x.shape[:-1] + (-1, 2))
            xe, xo = (xr[..., 0], xr[..., 1])
            c = cos[None, :, None, :]
            s = sin[None, :, None, :]
            return jnp.stack([xe * c - xo * s, xe * s + xo * c], axis=-1).reshape(x.shape)

        def _rmsnorm(x, w):
            return x * jax.lax.rsqrt(jnp.mean(x * x, axis=-1, keepdims=True) + EPS) * w

        def _reference_tuple_inner(x, Wq_down, q_norm_w, Wq_up, Wq_rope, Wkv_down, kv_norm_w, Wk_up, Wv_up, Wk_rope, Wout):
            b, s, _ = x.shape
            cos, sin = _rope_tables(s, RD, THETA)
            c_q = _rmsnorm(x @ Wq_down, q_norm_w)
            q = (c_q @ Wq_up).reshape(b, s, H, HD).transpose(0, 2, 1, 3)
            q_rope = _apply_rope((x @ Wq_rope).reshape(b, s, H, RD), cos, sin)
            q_rope = q_rope.transpose(0, 2, 1, 3)
            c_kv = _rmsnorm(x @ Wkv_down, kv_norm_w)
            k = (c_kv @ Wk_up).reshape(b, s, H, HD).transpose(0, 2, 1, 3)
            v = (c_kv @ Wv_up).reshape(b, s, H, HD).transpose(0, 2, 1, 3)
            k_rope = _apply_rope((x @ Wk_rope).reshape(b, s, H, RD), cos, sin)
            k_rope = k_rope.transpose(0, 2, 1, 3)
            scale = (HD + RD) ** (-0.5)
            scores = (jnp.einsum('bhqd,bhkd->bhqk', q, k) + jnp.einsum('bhqd,bhkd->bhqk', q_rope, k_rope)) * scale
            attn = jax.nn.softmax(scores, axis=-1)
            out = jnp.einsum('bhqk,bhkd->bhqd', attn, v)
            out = out.transpose(0, 2, 1, 3).reshape(b, s, H * HD) @ Wout
            return (out, attn)
        return _reference_tuple_inner(x, Wq_down, q_norm_w, Wq_up, Wq_rope, Wkv_down, kv_norm_w, Wk_up, Wv_up, Wk_rope, Wout)[0]

    def _L0_ffn_ref(x, gate_w, W1, W2, W3, Ws1, Ws2, Ws3):
        import jax, jax.numpy as jnp
        import numpy as np
        N_GROUPS = 4
        TOPK_GROUPS = 2
        TOPK = 4
        ROUTE_SCALE = 1.0

        def _gate(xt, gate_w):
            T = xt.shape[0]
            E = gate_w.shape[0]
            scores = jax.nn.sigmoid(xt @ gate_w.T)
            original_scores = scores
            sg = scores.reshape(T, N_GROUPS, E // N_GROUPS)
            group_scores = sg.max(axis=-1)
            _, gidx = jax.lax.top_k(group_scores, TOPK_GROUPS)
            gmask = jax.nn.one_hot(gidx, N_GROUPS, dtype=scores.dtype).sum(axis=1)
            masked = (sg * gmask[:, :, None]).reshape(T, E)
            _, idx = jax.lax.top_k(masked, TOPK)
            w = jnp.take_along_axis(original_scores, idx, axis=-1)
            w = w / w.sum(axis=-1, keepdims=True) * ROUTE_SCALE
            return (w, idx)
        shape = x.shape
        D = shape[-1]
        xt = x.reshape(-1, D)
        E = W1.shape[0]
        weights, indices = _gate(xt, gate_w)
        combine = jnp.einsum('tk,tke->te', weights, jax.nn.one_hot(indices, E, dtype=weights.dtype))
        h1 = jnp.einsum('td,eid->tei', xt, W1)
        h3 = jnp.einsum('td,eid->tei', xt, W3)
        g = jax.nn.silu(h1) * h3 * combine[:, :, None]
        y = jnp.einsum('tei,edi->td', g, W2)
        z = jax.nn.silu(xt @ Ws1.T) * (xt @ Ws3.T) @ Ws2.T
        return (y + z).reshape(shape)
    x = L0_attn_x
    mod = (_silu(L0_c) @ L0_wmod).reshape(L0_c.shape[0], 6, 1, -1)
    sa, ca, ga, sb, cb, gb = (mod[:, 0], mod[:, 1], mod[:, 2], mod[:, 3], mod[:, 4], mod[:, 5])
    ga = (2 * (ga >= 0) - 1) * jnp.maximum(jnp.abs(ga), 0.25)
    gb = (2 * (gb >= 0) - 1) * jnp.maximum(jnp.abs(gb), 0.25)
    h = _layernorm(x, axis=-1) * (1 + ca) + sa
    x = x + ga * _L0_attn_ref(h, L0_attn_Wq_down, L0_attn_q_norm_w, L0_attn_Wq_up, L0_attn_Wq_rope, L0_attn_Wkv_down, L0_attn_kv_norm_w, L0_attn_Wk_up, L0_attn_Wv_up, L0_attn_Wk_rope, L0_attn_Wout)
    h = _layernorm(x, axis=-1) * (1 + cb) + sb
    x = x + gb * _L0_ffn_ref(h, L0_ffn_gate_w, L0_ffn_W1, L0_ffn_W2, L0_ffn_W3, L0_ffn_Ws1, L0_ffn_Ws2, L0_ffn_Ws3)
    return x

_drawn_inputs = setup_inputs


def setup_inputs(seed=0):
    import zlib

    import numpy as np

    out = dict(_drawn_inputs(seed))
    spreads = {'L0_attn_q_norm_w': (1.0, 0.6), 'L0_attn_kv_norm_w': (1.0, 0.6)}
    factors = {'L0_attn_Wq_down': 8.0,
     'L0_attn_Wq_up': 8.0,
     'L0_attn_Wq_rope': 8.0,
     'L0_attn_Wkv_down': 8.0,
     'L0_attn_Wk_up': 8.0,
     'L0_attn_Wv_up': 8.0,
     'L0_attn_Wk_rope': 8.0,
     'L0_attn_Wout': 8.0,
     'L0_ffn_gate_w': 8.0,
     'L0_ffn_W1': 8.0,
     'L0_ffn_W2': 8.0,
     'L0_ffn_W3': 8.0,
     'L0_ffn_Ws1': 8.0,
     'L0_ffn_Ws2': 8.0,
     'L0_ffn_Ws3': 8.0,
     'L0_c': 8.0,
     'L0_wmod': 8.0}
    for name, (base, spread) in spreads.items():
        noise = np.random.default_rng([zlib.crc32(name.encode()), seed]).standard_normal(out[name].shape)
        drawn = base * np.exp(spread * noise) if base else spread * noise
        out[name] = jnp.asarray(drawn.astype(out[name].dtype))
    for name, factor in factors.items():
        out[name] = (out[name] * factor).astype(out[name].dtype)
    return out
```

```python
import math
from contextlib import ExitStack

import numpy as np
import concourse.bass as bass
from concourse import mybir

F32 = mybir.dt.float32
F32R = mybir.dt.float32r
ALU = mybir.AluOpType
ACT = mybir.ActivationFunctionType
AX_X = mybir.AxisListType.X

P = 128
NB, SEQ, D = 4, 512, 256
TB = SEQ // P
NT = NB * TB
KD = D // P
H, HD, RD = 16, 128, 64
QL, KL = 48, 64
GH = 4
NG = H // GH
EPS_RMS, EPS_LN = 1e-6, 1e-5
SCALE = (HD + RD) ** -0.5
E, TOPK, EG, TOPG = 16, 4, 4, 2
FI = 176
FC = FI // 2
ES = E + 2

IT_HEADS = 2 * GH
UNITS = IT_HEADS * TB
ITERS = NB * H // IT_HEADS


def aux_plan():
    at = {u: [] for u in range(UNITS)}
    for s in range(1, IT_HEADS + 1):
        at[4 * s - 1].append(("tq", s + 1))
    for s in range(IT_HEADS):
        at[4 * s].append(("tk", s + 1))
    for par, start in ((1, 0), (0, 16)):
        for n, (p, a) in enumerate(((0, 1), (2, 3), (5, 6), (8, 9))):
            at[start + p].append(("pr", par, n))
            at[start + a].append(("ab", par, n))
    for par, a, b in ((1, (10, 10), (13, 14)), (0, (20, 21), (25, 26))):
        for n in range(2):
            at[a[n]].append(("ot", par, n))
            at[b[n]].append(("op", par, n))
    return at


AUX_FIRST = [("pr", 0, 0), ("ab", 0, 0), ("pr", 0, 1), ("ab", 0, 1), ("pr", 0, 2), ("ab", 0, 2),
             ("pr", 0, 3), ("ab", 0, 3), ("tq", 0), ("tk", 0), ("tq", 1)]
AUX_AT = aux_plan()
AUX_LIST = [t for u in range(UNITS) for t in AUX_AT[u]]
AUX_N = len(AUX_LIST)
assert AUX_N % 2 == 0


def program(nc, x, cT, wmod, wdn, wqup, wkup, wvup, wout, wrope, rope_tab, eye, qnw, kvw_bc, kvw2, wgate, w13, w2, earlier,
            out):
    ctx = ExitStack()
    with ctx:
        def sb(name, shape, dt=F32):
            return ctx.enter_context(nc.sbuf_tensor(name, shape, dt))

        def sem(name):
            return ctx.enter_context(nc.semaphore(name))

        bank = [ctx.enter_context(nc.psum_tensor(f"bank{i}", [P, 512], F32)) for i in range(8)]
        score_bank, pt_bank, out_bank, aux_bank = bank[0:2], bank[2:4], bank[4:6], bank[6:8]

        h_dram = nc.dram_tensor("h_dram", [NB, P, 2 * KD * SEQ], F32).ap()
        mod_dram = nc.dram_tensor("mod_dram", [NB, P, 2 * D], F32).ap()
        cq_dram = nc.dram_tensor("cq_dram", [NB, QL, 2 * SEQ], F32).ap()

        ident = sb("ident", [P, P])
        gate = sb("gate", [P, NB + 1, 2, D])
        xa = sb("xa", [P, (NB + 1) * TB, D])
        mhalf = sb("mhalf", [P, 2 * TB])
        idle = sb("idle", [P, 4])

        attention = ExitStack()

        def sb2(name, shape, dt=F32):
            return attention.enter_context(nc.sbuf_tensor(name, shape, dt))

        rope = sb2("rope", [P, TB, 2, 2, RD])
        wr_hi = sb2("wr_hi", [P, KD, NG, 512], F32R)
        wr_lo = sb2("wr_lo", [P, KD, NG, 512], F32R)
        ab_hi = sb2("ab_hi", [P, H * KL], F32R)
        ab_lo = sb2("ab_lo", [P, H * KL], F32R)
        mout = sb2("mout", [P, H // 2, D])
        modT = sb2("modT", [P, 4, KD, NB])
        ckv = sb2("ckv", [P, NT, KL])
        h_st = sb2("h_st", [P, 2, KD, SEQ], F32R)
        cq_st = sb2("cq_st", [P, 2, SEQ], F32R)
        qk_tok = sb2("qk_tok", [P, 2, TB, 2, GH, P])
        o_tok = sb2("o_tok", [P, 2, TB, GH * KL])

        wr_raw = qk_tok[:].rearrange("p a t q h c -> p a (t q h c)")[:, 0]
        wout_s = qk_tok[:].rearrange("p a t q h c -> p a (t q h c)")[:, 1].rearrange("p (h d) -> p h d", h=H)
        first = ExitStack()

        def sb1(name, shape, dt=F32):
            return first.enter_context(nc.sbuf_tensor(name, shape, dt))

        wmod_s = sb1("wmod_s", [P, KD, 6 * D])
        wdn_s = sb1("wdn_s", [P, KD, QL + KL])
        wqup_s = sb1("wqup_s", [P, H, QL])
        wkup_s = sb1("wkup_s", [P, H, KL])
        wvup_s = sb1("wvup_s", [P, H, KL])
        ab_f = sb1("ab_f", [QL, H * KL])
        qnw_s = sb1("qnw_s", [QL, 1])
        qnw_sc = sb1("qnw_sc", [QL, 1])
        kvwb_s = sb1("kvwb_s", [QL, KL])
        kvw2_s = sb1("kvw2_s", [P, 1])
        cT_s = sb1("cT_s", [P, KD, NB])
        cexp = sb1("cexp", [P, KD, NB])
        crec = sb1("crec", [P, KD, NB])
        csil = sb1("csil", [P, KD, NB])
        csil_bc = sb1("csil_bc", [P, KD, NB, P])
        gabs = sb1("gabs", [P, 2 * D])
        gsgn = sb1("gsgn", [P, 2 * D])
        mod_o = sb1("mod_o", [P, 2, D])
        bst = sb1("bst", [P, TB, 6])
        mv = sb1("mv", [P, TB, 2])
        ve = sb1("ve", [P, 3, TB])
        rstd = sb1("rstd", [P, TB])
        xn = sb1("xn", [P, TB, D])
        h_f = sb1("h_f", [P, KD, SEQ])
        h_hl = sb1("h_hl", [P, 2, KD, SEQ], F32R)
        dn = sb1("dn", [P, TB, QL + KL])
        dsq = sb1("dsq", [P, TB, QL + KL])
        ssq = sb1("ssq", [P, 2, TB])
        rms = sb1("rms", [P, 2, TB])
        ncq = sb1("ncq", [P, TB, QL])
        cq_hl = sb1("cq_hl", [QL, 2, SEQ], F32R)
        first.close()

        t_cos = sb2("t_cos", [P, 2, 2 * GH, RD])
        t_sin = sb2("t_sin", [P, 2, 2 * GH, RD])
        qT = sb2("qT", [P, 2, SEQ])
        kT = sb2("kT", [P, 2, SEQ])
        nmax = sb2("nmax", [P, 4])
        prob = sb2("prob", [P, 2, SEQ])
        rsum = sb2("rsum", [P, 2, TB])
        rinv = sb2("rinv", [P, 2, TB])
        probT = sb2("probT", [P, 2, SEQ])
        oT = sb2("oT", [P, 2, 2, SEQ])
        y_gate = sb2("y_gate", [P, 2, 2, D])

        attention.close()

        w_hi = sb("w_hi", [P, ES, KD, 2 * FI], F32R)
        w_lo = sb("w_lo", [P, ES, KD, 2 * FI], F32R)
        w_raw = sb("w_raw", [P, 2, KD, 2 * FI])
        w2_p = sb("w2_p", [P, ES, 2, D])
        w2_s = w2_p[0:FC]
        h2T = w2_p[:, 0:2].rearrange("p e c n -> p (e c n)").rearrange("p (k t) -> p k t", k=KD)
        modb = sb("modb", [P, 2, 2, D])
        gw_s = sb("gw_s", [P, KD, E])
        early_s = sb("early_s", [P, EG, EG])
        bst2 = sb("bst2", [P, TB, 6])
        mv2 = sb("mv2", [P, TB, 2])
        ve2 = sb("ve2", [P, TB])
        rstd2 = sb("rstd2", [P, TB])
        h2 = sb("h2", [P, NT, D])
        sg = sb("sg", [P, NT, E])
        gm = sb("gm", [P, NT, EG])
        gsel = sb("gsel", [P, NT, EG])
        msk = sb("msk", [P, NT, E])
        top = sb("top", [P, NT, 8])
        above = sb("above", [P, NT, E])
        equal = sb("equal", [P, NT, E])
        pre = sb("pre", [P, 2, NT, E])
        gtm = above[:].rearrange("p t (a b) -> p t a b", a=EG)
        gem = equal[:].rearrange("p t (a b) -> p t a b", a=EG)
        zg = pre[:].rearrange("p a t e -> p (a t e)")[:, 0:D]
        quota = sb("quota", [P, NT])
        den = sb("den", [P, NT])
        wts = sb("wts", [P, NT, ES])
        wt = sb("wt", [P, ES])
        xg = sb("xg", [P, D])
        xgT_hi = sb("xgT_hi", [P, KD, P], F32R)
        xgT_lo = sb("xgT_lo", [P, KD, P], F32R)
        sl = sb("sl", [P, 2, FI])
        g_s = sb("g_s", [P, 2, FI])
        gT = sb("gT", [FC, 2, 2, P])

        ld_a, ld_b, ld_c, ld_x = sem("ld_a"), sem("ld_b"), sem("ld_c"), sem("ld_x")
        dve_c, act_c, pool_c = sem("dve_c"), sem("act_c"), sem("pool_c")
        c_exp, c_sil, mod_mm, mod_ev = sem("c_exp"), sem("c_sil"), sem("mod_mm"), sem("mod_ev")
        ab_mm, ab_ev, ab_rd = sem("ab_mm"), sem("ab_ev"), sem("ab_rd")
        m_mm, m_ev, g_mm, g_ev = sem("m_mm"), sem("m_ev"), sem("g_mm"), sem("g_ev")
        wr_h, wr_l, ab_h, ab_l = sem("wr_h"), sem("wr_l"), sem("ab_h"), sem("ab_l")
        zeroed = sem("zeroed")
        p_stat, p_rstd, p_xn, p_tr, p_h, p_hhi, p_hlo = (sem(n) for n in
            ("p_stat", "p_rstd", "p_xn", "p_tr", "p_h", "p_hhi", "p_hlo"))
        p_dn, p_ssq, p_rms, p_ncq, p_ctr, p_chi, p_clo, p_st, p_cst = (sem(n) for n in
            ("p_dn", "p_ssq", "p_rms", "p_ncq", "p_ctr", "p_chi", "p_clo", "p_st", "p_cst"))
        p_dnev = sem("p_dnev")
        staged = sem("staged")
        s_score, s_max, s_exp, s_pt, s_ptc, s_pv, s_norm, s_rinv = (sem(n) for n in
            ("s_score", "s_max", "s_exp", "s_pt", "s_ptc", "s_pv", "s_norm", "s_rinv"))
        aux_done = sem("aux_done")
        s_sin, s_rope, s_ck, s_ab, s_qk, s_ot, s_yg, s_x = (sem(n) for n in
            ("s_sin", "s_rope", "s_ck", "s_ab", "s_qk", "s_ot", "s_yg", "s_x"))
        stored, mb_mm, mb_ev, mb_st, ld_f = (sem(n) for n in
            ("stored", "mb_mm", "mb_ev", "mb_st", "ld_f"))
        ld_w2 = sem("ld_w2")
        mb_ld = [sem("mb_ld0"), sem("mb_ld1")]
        ld_w = [sem("ld_w0"), sem("ld_w1")]
        w_h, w_l, f_stat, f_rstd, f_h2, f_tr, f_h2T, f_lg, f_sg, f_wts = (sem(n) for n in
            ("w_h", "w_l", "f_stat", "f_rstd", "f_h2", "f_tr", "f_h2T", "f_lg", "f_sg", "f_wts"))
        e_xg, e_wt, e_xt, e_hi, e_lo, e_h, e_sl, e_g, e_gt, e_gTc, e_y, e_zg, e_out = (sem(n) for n in
            ("e_xg", "e_wt", "e_xt", "e_hi", "e_lo", "e_h", "e_sl", "e_g", "e_gt", "e_gTc", "e_y", "e_zg", "e_out"))

        block = ctx.enter_context(nc.Block())

        def aux_count(i, k):
            return k + 1 if i is None else AUX_N * i + len(AUX_FIRST) + k + 1

        def aux_home(i, k):
            return aux_bank[(k if i is None else len(AUX_FIRST) + k) % 2]

        def read_out(i, t):
            if t[0] in ("tq", "tk"):
                return s_qk, (0 if i is None else 2 * IT_HEADS * i) + 2 * t[1] + (1 if t[0] == "tq" else 2)
            if t[0] in ("pr", "ab"):
                return s_sin if t[0] == "pr" else s_ab, pr_count(i, t[1], t[2]) + 1
            return s_ot if t[0] == "ot" else s_yg, 4 * i + (0 if t[1] else 2) + t[2] + 1

        def pr_count(i, par, n):
            return n if i is None else 2 * TB * i + (TB if par else 2 * TB) + n

        def aux_tasks():
            k = 0
            for u in range(UNITS):
                for t in AUX_AT[u]:
                    yield u, k, t
                    k += 1

        AUX_K = {u: [] for u in range(UNITS)}
        for u, k, t in aux_tasks():
            AUX_K[u].append((k, t))

        def it_batch(i):
            return i // 2

        def prep_batch(i, par):
            return i // 2 if par else ((i + 1) // 2) % NB

        def prep_group(i, par):
            return (i % 2) * 2 + 1 if par else ((i + 1) % 2) * 2

        def out_pair(i, par):
            return ((i + 1) % 2) * 4 + 2 if par else (i % 2) * 4

        def out_slot(i, par):
            return (i + 1) // 2 if par else i // 2 + 1

        LAST = [("ot", 1, 0), ("ot", 1, 1), ("op", 1, 0), ("op", 1, 1)]

        @block.sync
        def _(sp):
            sp.dma_start(cT_s[:], cT).then_inc(ld_a, 16)
            sp.dma_start(ident[:], eye).then_inc(ld_a, 16)
            sp.dma_start(xa[:, TB:, :], x.rearrange("(t p) d -> p t d", p=P)).then_inc(ld_x, 16)
            sp.dma_start(wmod_s[:], wmod).then_inc(ld_a, 16)
            sp.dma_start(wdn_s[:], wdn).then_inc(ld_a, 16)
            sp.dma_start(wr_raw, wrope).then_inc(ld_b, 16)
            sp.dma_start(rope[:], rope_tab).then_inc(ld_b, 16)
            sp.dma_start(wqup_s[:], wqup).then_inc(ld_c, 16)
            sp.dma_start(wkup_s[:], wkup).then_inc(ld_c, 16)
            sp.dma_start(wvup_s[:], wvup).then_inc(ld_c, 16)
            sp.dma_start(wout_s, wout).then_inc(ld_c, 16)
            sp.dma_start(qnw_s[:], qnw).then_inc(ld_c, 16)
            sp.dma_start(kvwb_s[:], kvw_bc).then_inc(ld_c, 16)
            sp.dma_start(kvw2_s[:], kvw2).then_inc(ld_c, 16)
            for b in range(NB):
                sp.wait_ge(mb_ev, b + 1)
                sp.dma_start(mod_dram[b], mod_o[:].rearrange("p a n -> p (a n)")).then_inc(mb_st, 16)
            sp.wait_ge(mb_st, 16 * NB)
            for b in range(NB):
                sp.wait_ge(p_hhi, b + 1)
                sp.wait_ge(p_hlo, b + 1)
                sp.dma_start(h_dram[b], h_hl[:].bitcast(F32).rearrange("p a k t -> p (a k t)")).then_inc(p_st, 16)
                sp.wait_ge(p_chi, b + 1)
                sp.wait_ge(p_clo, b + 1)
                sp.dma_start(cq_dram[b], cq_hl[:].bitcast(F32).rearrange("p a t -> p (a t)")).then_inc(p_cst, 16)
            sp.wait_ge(p_st, 16 * NB)
            sp.wait_ge(p_cst, 16 * NB)

            def stage(b):
                sp.dma_start(h_st[:].bitcast(F32).rearrange("p a k t -> p (a k t)"),
                             h_dram[bass.ds(b, 1)].rearrange("b p n -> (b p) n")).then_inc(staged, 16)
                sp.dma_start(cq_st[0:QL].bitcast(F32).rearrange("p a t -> p (a t)"),
                             cq_dram[bass.ds(b, 1)].rearrange("b p n -> (b p) n")).then_inc(staged, 16)

            sp.wait_ge(zeroed, 2)
            stage(0)
            last = max(k for u, k, t in aux_tasks() if t[0] in ("pr", "ab") and t[1] == 1)
            with sp.Fori(0, ITERS) as i:
                sp.wait_ge(aux_done, aux_count(i, last))
                stage(((i + 1) // 2) % NB)
            sp.wait_ge(staged, 32 * (ITERS + 1))
            sp.wait_ge(s_x, 4 * ITERS + 4)
            sp.dma_start(gw_s[:], wgate).then_inc(ld_f, 16)
            sp.dma_start(early_s[:], earlier).then_inc(ld_f, 16)
            for b in range(NB):
                if b >= 2:
                    sp.wait_ge(f_h2, b - 1)
                sp.dma_start(modb[:, b % 2].rearrange("p a n -> p (a n)"), mod_dram[b]).then_inc(mb_ld[b % 2], 16)
            for e in range(ES):
                if e >= 2:
                    sp.wait_ge(w_h, e - 1)
                    sp.wait_ge(w_l, e - 1)
                sp.dma_start(w_raw[:, e % 2], w13[:, e]).then_inc(ld_w[e % 2], 16)
                if e == 2:
                    sp.wait_ge(f_lg, NB)
                    sp.dma_start(w2_s, w2).then_inc(ld_w2, 16)
            sp.wait_ge(e_out, NT + 1)
            sp.dma_start(out.rearrange("(t p) d -> p t d", p=P), xa[:, TB:, :]).then_inc(stored, 16)
            sp.wait_ge(stored, 16)

        @block.tensor
        def _(pe):
            def mm3(dst, l_hi, l_lo, r_hi, r_lo, start, stop):
                pe.matmul(dst, l_hi, r_hi, start=start, stop=False)
                pe.matmul(dst, l_hi, r_lo, start=False, stop=False)
                return pe.matmul(dst, l_lo, r_hi, start=False, stop=stop)

            pe.wait_ge(ld_a, 64)
            pe.wait_ge(c_sil, 1)
            for w, chunk in enumerate((0, 1, 3, 4)):
                for c in range(KD):
                    for k in range(KD):
                        mm = pe.matmul(aux_bank[0][:, (w * KD + c) * NB:(w * KD + c + 1) * NB],
                                       wmod_s[:, k, chunk * D + c * P:chunk * D + (c + 1) * P],
                                       csil[:, k, :], start=(k == 0), stop=(k == KD - 1))
            mm.then_inc(mod_mm, 1)
            pe.wait_ge(c_sil, 2)
            for b in range(NB):
                for w in range(2):
                    for k in range(KD):
                        mm = pe.matmul(bank[b][:, w * D:(w + 1) * D], csil_bc[:, k, b, :],
                                       wmod_s[:, k, (3 * w + 2) * D:(3 * w + 3) * D],
                                       start=(k == 0), stop=(k == KD - 1))
                mm.then_inc(g_mm, 1)
            for b in range(NB):
                pe.wait_ge(g_ev, b + 1)
                for w in range(2):
                    for k in range(KD):
                        mm = pe.matmul(bank[b][:, w * D:(w + 1) * D], csil_bc[:, k, b, :],
                                       wmod_s[:, k, (3 + w) * D:(4 + w) * D],
                                       start=(k == 0), stop=(k == KD - 1))
                mm.then_inc(mb_mm, 1)

            pe.wait_ge(mod_ev, 1)
            for b in range(NB):
                pe.wait_ge(p_xn, b + 1)
                for k in range(KD):
                    if b > 0:
                        pe.wait_ge(p_h, KD * (b - 1) + k + 1)
                        if k == 0:
                            pe.wait_ge(p_clo, b)
                    for t in range(TB):
                        mm = pe.transpose(aux_bank[k][:, t * P:(t + 1) * P], xn[:, t, k * P:(k + 1) * P], ident[:])
                    mm.then_inc(p_tr, 1)
                if b > 0:
                    pe.wait_ge(p_dnev, b)
                pe.wait_ge(p_h, KD * (b + 1))
                for t in range(TB):
                    for k in range(KD):
                        mm = pe.matmul(out_bank[0][:, t * P:t * P + QL + KL], h_f[:, k, t * P:(t + 1) * P],
                                       wdn_s[:, k, :], start=(k == 0), stop=(k == KD - 1))
                mm.then_inc(p_dn, 1)
                pe.wait_ge(p_ncq, b + 1)
                for t in range(TB):
                    mm = pe.transpose(out_bank[1][0:QL, t * P:(t + 1) * P], ncq[:, t, :], ident[:])
                mm.then_inc(p_ctr, 1)

            pe.wait_ge(ld_c, 16 * 7)
            pe.wait_ge(p_dnev, NB)
            pe.wait_ge(p_clo, NB)
            for h in range(H):
                mm = pe.matmul(out_bank[h // 8][0:QL, (h % 8) * KL:(h % 8 + 1) * KL], wqup_s[:, h, :],
                               wkup_s[:, h, :], start=True, stop=True)
                if h % 8 == 7:
                    mm.then_inc(ab_mm, 1)
            for q in range(4):
                pe.wait_ge(mb_ev, q + 1)
                for pr in range(2 * q, 2 * q + 2):
                    for s in range(2):
                        mm = pe.matmul(bank[q][s * KL:(s + 1) * KL, (pr % 2) * D:(pr % 2 + 1) * D],
                                       wvup_s[:, 2 * pr + s, :], wout_s[:, 2 * pr + s, :], start=True, stop=True)
                mm.then_inc(m_mm, 1)

            def aux(i, k, t):
                dst = aux_home(i, k)
                if t[0] == "ab":
                    pe.wait_ge(ab_l, 1)
                if i is None and k >= 2:
                    pe.wait_ge(*read_out(None, AUX_FIRST[k - 2]))
                elif i is not None and k >= 2:
                    pe.wait_ge(*read_out(i, (LAST if isinstance(i, int) else AUX_LIST)[k - 2]))
                elif i is not None:
                    kind, s = AUX_LIST[AUX_N - 2 + k]
                    pe.wait_ge(*read_out(i, (kind, s - IT_HEADS)))
                if t[0] == "pr":
                    _, par, n = t
                    g = 0 if i is None else prep_group(i, par)
                    if n == 0 and (i is None or par == 0):
                        pe.wait_ge(staged, 32 if i is None else 32 * (i + 2))
                    for c in range(KD):
                        tok = slice(n * P, (n + 1) * P)
                        mm = mm3(dst[:], h_st[:, 0, c, tok], h_st[:, 1, c, tok],
                                 wr_hi[:, c, bass.ds(g, 1), :].rearrange("p a n -> p (a n)"),
                                 wr_lo[:, c, bass.ds(g, 1), :].rearrange("p a n -> p (a n)"),
                                 c == 0, c == KD - 1)
                elif t[0] == "ab":
                    _, par, n = t
                    g = 0 if i is None else prep_group(i, par)
                    tok = slice(n * P, (n + 1) * P)
                    mm = mm3(dst[:, 0:GH * KL], cq_st[:, 0, tok], cq_st[:, 1, tok],
                             ab_hi[:, bass.ds(g * (GH * KL), GH * KL)], ab_lo[:, bass.ds(g * (GH * KL), GH * KL)],
                             True, True)
                elif t[0] in ("tq", "tk"):
                    s = t[1]
                    par, hh = (s // GH) % 2, s % GH
                    if t[0] == "tq" and hh == 0:
                        n = pr_count(i, par, TB) if i is not None else TB
                        pe.wait_ge(s_rope, n)
                        pe.wait_ge(s_ab, n)
                        pe.wait_ge(s_ck, n)
                    for n in range(TB):
                        mm = pe.transpose(dst[:, n * P:(n + 1) * P], qk_tok[:, par, n, int(t[0] == "tk"), hh, :], ident[:])
                elif t[0] == "ot":
                    _, par, n = t
                    pe.wait_ge(s_norm, IT_HEADS * i + (0 if par else GH) + 1)
                    for q in range(TB):
                        mm = pe.transpose(dst[:, q * P:(q + 1) * P], o_tok[:, par, q, n * P:(n + 1) * P], ident[:])
                else:
                    _, par, n = t
                    if n == 0:
                        pe.wait_ge(s_ot, 4 * i + (2 if par else 4))
                    g2 = out_pair(i, par)
                    for q in range(2):
                        for pp in range(2):
                            mm = pe.matmul(dst[:, q * D:(q + 1) * D], oT[:, par, pp, (2 * n + q) * P:(2 * n + q + 1) * P],
                                           mout[:, bass.ds(g2 + pp, 1), :].rearrange("p a n -> p (a n)"),
                                           start=(pp == 0), stop=(pp == 1))
                mm.then_inc(aux_done, 1)

            def score(i, u):
                s, q = u // TB, u % TB
                if i is None:
                    if q == 0:
                        pe.wait_ge(s_qk, 2 * (s + 1))
                    if u >= 2:
                        pe.wait_ge(s_exp, u - 1)
                else:
                    if q == 0:
                        pe.wait_ge(s_qk, 2 * IT_HEADS * i + 2 * (s + 1))
                    pe.wait_ge(s_exp, UNITS * i + u - 1)
                pe.matmul(score_bank[u % 2][:], qT[:, s % 2, q * P:(q + 1) * P], kT[:, s % 2, :],
                          start=True, stop=True).then_inc(s_score, 1)

            def transpose_probs(i, u):
                base = 0 if i is None else UNITS * i
                pe.wait_ge(s_exp, base + u + 1)
                for c in range(TB):
                    mm = pe.transpose(pt_bank[u % 2][:, c * P:(c + 1) * P], prob[:, u % 2, c * P:(c + 1) * P], ident[:])
                mm.then_inc(s_pt, 1)

            def weigh_values(i, u):
                s, q = u // TB, u % TB
                pe.wait_ge(s_ptc, UNITS * i + u + 1)
                if q == 0 and s > 0:
                    pe.wait_ge(s_norm, IT_HEADS * i + s)
                for c in range(TB):
                    mm = pe.matmul(out_bank[s % 2][:, q * KL:(q + 1) * KL], probT[:, u % 2, c * P:(c + 1) * P],
                                   ckv[:, bass.ds(it_batch(i) * TB + c, 1), :].rearrange("p a n -> p (a n)"),
                                   start=(c == 0), stop=(c == TB - 1))
                mm.then_inc(s_pv, 1)

            pe.wait_ge(ab_ev, 2)
            pe.wait_ge(m_ev, 4)
            pe.wait_ge(wr_l, 1)
            pe.wait_ge(wr_h, 1)
            pe.wait_ge(ab_h, 1)
            pe.wait_ge(ab_l, 1)
            pe.wait_ge(zeroed, 2)
            for k, t in enumerate(AUX_FIRST):
                aux(None, k, t)
            score(None, 0)
            score(None, 1)
            transpose_probs(None, 0)
            with pe.Fori(0, ITERS) as i:
                for u in range(UNITS):
                    score(i, u + 2)
                    transpose_probs(i, u + 1)
                    weigh_values(i, u)
                    for k, t in AUX_K[u]:
                        aux(i, k, t)
            for k, t in enumerate(LAST):
                aux(ITERS, k, t)

            pe.wait_ge(s_x, 4 * ITERS + 4)
            pe.wait_ge(ld_f, 32)
            for b in range(NB):
                pe.wait_ge(f_h2, b + 1)
                for k in range(KD):
                    if b > 0:
                        pe.wait_ge(f_h2T, b)
                    for t in range(TB):
                        mm = pe.transpose(bank[k][:, t * P:(t + 1) * P], h2[:, b * TB + t, k * P:(k + 1) * P], ident[:])
                mm.then_inc(f_tr, 1)
                pe.wait_ge(f_h2T, b + 1)
                for t in range(TB):
                    for k in range(KD):
                        mm = pe.matmul(bank[2][:, (b * TB + t) * E:(b * TB + t + 1) * E], h2T[:, k, t * P:(t + 1) * P],
                                       gw_s[:, k, :], start=(k == 0), stop=(k == KD - 1))
                mm.then_inc(f_lg, 1)

            def inner(i, e):
                if e >= 2:
                    pe.wait_ge(e_g, ES * i + e - 1)
                if e == 0:
                    pe.wait_ge(e_hi, i + 1)
                    pe.wait_ge(e_lo, i + 1)
                for k in range(KD):
                    mm = mm3(bank[e % 2][:, 0:2 * FI], xgT_hi[:, k, :], xgT_lo[:, k, :], w_hi[:, e, k, :], w_lo[:, e, k, :],
                             k == 0, k == KD - 1)
                mm.then_inc(e_h, 1)

            def turn(i, e):
                pe.wait_ge(e_g, ES * i + e + 1)
                if e >= 2:
                    pe.wait_ge(e_gTc, ES * i + e - 1)
                for c in range(2):
                    mm = pe.transpose(bank[2 + e % 2][0:FC, c * P:(c + 1) * P], g_s[:, e % 2, c * FC:(c + 1) * FC], ident[:])
                mm.then_inc(e_gt, 1)

            def outer(i, e):
                pe.wait_ge(e_gTc, ES * i + e + 1)
                if e == 0:
                    pe.wait_ge(e_zg, i + 1)
                for c in range(2):
                    mm = pe.matmul(bank[4][:, 0:D], gT[:, e % 2, c, :], w2_s[:, e, c, :],
                                   start=(e == 0 and c == 0), stop=(e == ES - 1 and c == 1))
                if e == ES - 1:
                    mm.then_inc(e_y, 1)

            pe.wait_ge(w_h, ES)
            pe.wait_ge(w_l, ES)
            pe.wait_ge(ld_w2, 16)
            pe.wait_ge(f_sg, NB)
            with pe.Fori(0, NT) as i:
                pe.wait_ge(e_xg, i + 1)
                for k in range(KD):
                    mm = pe.transpose(bank[5][:, k * P:(k + 1) * P], xg[:, k * P:(k + 1) * P], ident[:])
                mm.then_inc(e_xt, 1)
                inner(i, 0)
                for e in range(ES):
                    if e + 1 < ES:
                        inner(i, e + 1)
                    turn(i, e)
                    if e > 0:
                        outer(i, e - 1)
                outer(i, ES - 1)

        @block.vector
        def _(dve):
            own = [0]

            def chain(ins):
                own[0] += 1
                ins.then_inc(dve_c, 1)
                dve.wait_ge(dve_c, own[0])

            dve.memset(o_tok[:, 1], 0.0).then_inc(s_norm, 1)
            dve.wait_ge(c_exp, 1)
            chain(dve.tensor_scalar(crec[:], cexp[:], 1.0, None, ALU.add))
            chain(dve.reciprocal(cexp[:], crec[:]))
            dve.tensor_tensor(csil[:], cT_s[:], cexp[:], ALU.mult).then_inc(c_sil, 1)
            dve.wait_ge(c_sil, 1)
            dve.tensor_copy(csil_bc[:].rearrange("p k b n -> p (k b) n"), csil[:].rearrange("p k b -> p (k b)")
                            .unsqueeze(2).to_broadcast([P, KD * NB, P])).then_inc(c_sil, 1)
            dve.wait_ge(mod_mm, 1)
            m4 = aux_bank[0][:, 0:4 * KD * NB].rearrange("p (w c b) -> p w c b", w=4, c=KD)
            for w in range(4):
                ins = dve.tensor_scalar(modT[:, w], m4[:, w], float(w % 2), None, ALU.add)
            ins.then_inc(mod_ev, 1)
            dve.wait_ge(mod_ev, 1)
            for b in range(NB):
                dve.wait_ge(g_mm, b + 1)
                dve.tensor_copy(gate[:, b + 1].rearrange("p w n -> p (w n)"), bank[b][:]).then_inc(g_ev, 1)
            for b in range(NB):
                dve.wait_ge(mb_mm, b + 1)
                if b > 0:
                    dve.wait_ge(mb_st, 16 * b)
                dve.tensor_copy(mod_o[:, 0], bank[b][:, 0:D])
                dve.tensor_scalar(mod_o[:, 1], bank[b][:, D:], 1.0, None, ALU.add).then_inc(mb_ev, 1)

            dve.wait_ge(ld_x, 16)
            for b in range(NB):
                xb = TB * (b + 1)
                for t in range(TB):
                    ins = dve.bn_stats(bst[:, t, :], xa[:, xb + t, :])
                chain(ins)
                for t in range(TB):
                    ins = dve.bn_aggr(mv[:, t, :], bst[:, t, :])
                ins.then_inc(p_stat, 1)
                dve.wait_ge(p_rstd, b + 1)
                if b > 0:
                    dve.wait_ge(p_tr, KD * b)
                for t in range(TB):
                    ins = dve.tensor_scalar(xn[:, t, :], xa[:, xb + t, :], mv[:, t, 0:1], rstd[:, t:t + 1],
                                            ALU.subtract, ALU.mult)
                ins.then_inc(p_xn, 1)
                if b > 0:
                    dve.wait_ge(p_hhi, b)
                    dve.wait_ge(p_hlo, b)
                for k in range(KD):
                    dve.wait_ge(p_tr, KD * b + k + 1)
                    dve.tensor_scalar(h_f[:, k, :], aux_bank[k][:], modT[:, 1, k, b:b + 1], modT[:, 0, k, b:b + 1],
                                      ALU.mult, ALU.add).then_inc(p_h, 1)
                dve.wait_ge(p_dn, b + 1)
                if b > 0:
                    dve.wait_ge(p_ncq, b)
                dve.tensor_copy(dn[:], out_bank[0][:].rearrange("p (t n) -> p t n", t=TB)[:, :, 0:QL + KL])\
                    .then_inc(p_dnev, 1)
                dve.wait_ge(p_dnev, b + 1)
                chain(dve.tensor_tensor(dsq[:], dn[:], dn[:], ALU.mult))
                dve.tensor_reduce(ssq[:, 0, :], dsq[:, :, 0:QL], AX_X, ALU.add)
                dve.tensor_reduce(ssq[:, 1, :], dsq[:, :, QL:], AX_X, ALU.add).then_inc(p_ssq, 1)
                dve.wait_ge(p_rms, b + 1)
                if b > 0:
                    dve.wait_ge(p_ctr, b)
                dve.tensor_tensor(ckv[:, b * TB:(b + 1) * TB, :], dn[:, :, QL:],
                                  rms[:, 1, :].unsqueeze(2).to_broadcast([P, TB, KL]), ALU.mult)
                dve.tensor_tensor(ncq[:], dn[:, :, 0:QL],
                                  rms[:, 0, :].unsqueeze(2).to_broadcast([P, TB, QL]), ALU.mult).then_inc(p_ncq, 1)
                dve.wait_ge(p_chi, b + 1)
                if b > 0:
                    dve.wait_ge(p_cst, 16 * b)
                dve.tensor_tensor(cq_hl[:, 1, :], out_bank[1][0:QL, :], cq_hl[:, 0, :].bitcast(F32),
                                  ALU.subtract).then_inc(p_clo, 1)

            dve.wait_ge(wr_h, 1)
            dve.tensor_tensor(wr_lo[:].rearrange("p k g n -> p (k g n)"), wr_raw,
                              wr_hi[:].bitcast(F32).rearrange("p k g n -> p (k g n)"), ALU.subtract).then_inc(wr_l, 1)
            dve.wait_ge(ld_c, 16 * 7)
            chain(dve.tensor_scalar(qnw_sc[:], qnw_s[:], SCALE, None, ALU.mult))
            for z in range(2):
                dve.wait_ge(ab_mm, z + 1)
                dve.scalar_tensor_tensor(
                    out=ab_f[:, z * 512:(z + 1) * 512].rearrange("p (h c) -> p h c", h=8),
                    in0=out_bank[z][0:QL, :].rearrange("p (h c) -> p h c", h=8), scalar=qnw_sc[:, 0:1],
                    in1=kvwb_s[:].unsqueeze(1).to_broadcast([QL, 8, KL]), op0=ALU.mult, op1=ALU.mult).then_inc(ab_ev, 1)
            dve.wait_ge(ab_h, 1)
            dve.tensor_tensor(ab_lo[0:QL], ab_f[:], ab_hi[0:QL].bitcast(F32), ALU.subtract).then_inc(ab_l, 1)
            for q in range(4):
                dve.wait_ge(m_mm, q + 1)
                dve.tensor_scalar(mout[:, 2 * q:2 * q + 2, :], bank[q][:].rearrange("p (a n) -> p a n", a=2),
                                  kvw2_s[:, 0:1], None, ALU.mult).then_inc(m_ev, 1)
            dve.wait_ge(g_ev, NB)
            for b in range(NB):
                g = gate[:, b + 1].rearrange("p w n -> p (w n)")
                dve.tensor_scalar(gsgn[:], g, 0.0, 0.5, ALU.is_ge, ALU.subtract)
                chain(dve.scalar_tensor_tensor(out=gabs[:], in0=g, scalar=-1.0, in1=g, op0=ALU.mult, op1=ALU.max))
                chain(dve.tensor_scalar(gabs[:], gabs[:], 0.25, 2.0, ALU.max, ALU.mult))
                chain(dve.tensor_tensor(g, gabs[:], gsgn[:], ALU.mult))

            def aux(i, k, t):
                src = aux_home(i, k)
                if t[0] == "pr":
                    _, par, n = t
                    dve.wait_ge(aux_done, aux_count(i, k))
                    if not (i is None and n < 2):
                        dve.wait_ge(s_rope, pr_count(i, par, n) - 1)
                    for dst, w in ((t_cos, 0), (t_sin, 1)):
                        ins = dve.tensor_tensor(dst[:, n % 2].rearrange("p (a h) c -> p a h c", a=2),
                                                src[:].rearrange("p (a h c) -> p a h c", a=2, h=GH),
                                                rope[:, n, w].unsqueeze(2).to_broadcast([P, 2, GH, RD]), ALU.mult)
                    ins.then_inc(s_sin, 1)
                elif t[0] == "ab":
                    _, par, n = t
                    dve.wait_ge(aux_done, aux_count(i, k))
                    dve.tensor_copy(qk_tok[:, par, n, 0, :, RD:], src[:, 0:GH * KL]
                                    .rearrange("p (h c) -> p h c", h=GH)).then_inc(s_ab, 1)
                elif t[0] == "op":
                    _, par, n = t
                    dve.wait_ge(aux_done, aux_count(i, k))
                    dve.wait_ge(s_x, 4 * i + (0 if par else 2) + n + 1)
                    dve.tensor_tensor(y_gate[:, n], src[:].rearrange("p (q n) -> p q n", q=2),
                                      gate[:, bass.ds(out_slot(i, par), 1), 0, :].to_broadcast([P, 2, D]),
                                      ALU.mult).then_inc(s_yg, 1)

            def row_max(i, u):
                dve.wait_ge(s_score, (0 if i is None else UNITS * i) + u + 1)
                dve.tensor_reduce(nmax[:, u % 4:u % 4 + 1], score_bank[u % 2][:], AX_X, ALU.max, negate=True)\
                    .then_inc(s_max, 1)

            def normalise(i, s):
                dve.wait_ge(s_pv, UNITS * i + TB * (s + 1))
                dve.reciprocal(rinv[:, s % 2, :], rsum[:, s % 2, :]).then_inc(s_rinv, 1)
                dve.wait_ge(s_rinv, IT_HEADS * i + s + 1)
                hh = s % GH
                dve.tensor_tensor(o_tok[:, s // GH, :, hh * KL:(hh + 1) * KL],
                                  out_bank[s % 2][:, 0:TB * KL].rearrange("p (q c) -> p q c", q=TB),
                                  rinv[:, s % 2, :].unsqueeze(2).to_broadcast([P, TB, KL]), ALU.mult).then_inc(s_norm, 1)

            for k, t in enumerate(AUX_FIRST):
                aux(None, k, t)
            row_max(None, 0)
            row_max(None, 1)
            with dve.Fori(0, ITERS) as i:
                for u in range(UNITS):
                    row_max(i, u + 2)
                    for k, t in AUX_K[u]:
                        aux(i, k, t)
                    if u % TB == TB - 1:
                        normalise(i, u // TB)
            for k, t in enumerate(LAST):
                aux(ITERS, k, t)

            dve.wait_ge(s_x, 4 * ITERS + 4)
            dve.wait_ge(s_norm, IT_HEADS * ITERS + 1)
            for b in range(NB):
                xb = TB * (b + 1)
                for t in range(TB):
                    ins = dve.bn_stats(bst2[:, t, :], xa[:, xb + t, :])
                chain(ins)
                if b > 0:
                    dve.wait_ge(f_rstd, b)
                for t in range(TB):
                    ins = dve.bn_aggr(mv2[:, t, :], bst2[:, t, :])
                ins.then_inc(f_stat, 1)
                dve.wait_ge(f_rstd, b + 1)
                dve.wait_ge(mb_ld[b % 2], 16 * (b // 2 + 1))
                rows = h2[:, b * TB:(b + 1) * TB, :]
                for t in range(TB):
                    ins = dve.tensor_scalar(h2[:, b * TB + t, :], xa[:, xb + t, :], mv2[:, t, 0:1], rstd2[:, t:t + 1],
                                            ALU.subtract, ALU.mult)
                chain(ins)
                chain(dve.tensor_tensor(rows, rows, modb[:, b % 2, 1:2, :].to_broadcast([P, TB, D]), ALU.mult))
                dve.tensor_tensor(rows, rows, modb[:, b % 2, 0:1, :].to_broadcast([P, TB, D]), ALU.add).then_inc(f_h2, 1)
            dve.wait_ge(f_sg, NB)
            dve.wait_ge(ld_f, 32)
            chain(dve.tensor_scalar(sg[:], sg[:], 1.0, None, ALU.add))
            chain(dve.reciprocal(sg[:], sg[:]))
            chain(dve.tensor_reduce(gm[:], sg[:].rearrange("p t (g e) -> p t g e", g=EG), AX_X, ALU.max))
            rival = gm[:].unsqueeze(2).to_broadcast([P, NT, EG, EG])
            me = gm[:].unsqueeze(3).to_broadcast([P, NT, EG, EG])
            dve.tensor_tensor(gtm, rival, me, ALU.is_gt)
            chain(dve.tensor_tensor(gem, rival, me, ALU.is_equal))
            chain(dve.tensor_tensor(gem.rearrange("p t a b -> p t (a b)"), gem.rearrange("p t a b -> p t (a b)"),
                                    early_s[:].rearrange("p a b -> p (a b)").unsqueeze(1).to_broadcast([P, NT, EG * EG]),
                                    ALU.mult))
            chain(dve.tensor_tensor(gtm, gtm, gem, ALU.add))
            chain(dve.tensor_reduce(gsel[:], gtm, AX_X, ALU.add))
            chain(dve.tensor_scalar(gsel[:], gsel[:], float(TOPG), None, ALU.is_lt))
            chain(dve.tensor_tensor(msk[:].rearrange("p t (g e) -> p (t g) e", g=EG), sg[:].rearrange("p t (g e) -> p (t g) e", g=EG),
                                    gsel[:].rearrange("p t g -> p (t g)").unsqueeze(2).to_broadcast([P, NT * EG, E // EG]),
                                    ALU.mult))
            for t in range(NT):
                ins = dve.max(top[:, t, :], msk[:, t, :])
            chain(ins)
            least = top[:, :, TOPK - 1:TOPK].to_broadcast([P, NT, E])
            dve.tensor_tensor(above[:], msk[:], least, ALU.is_gt)
            chain(dve.tensor_tensor(equal[:], msk[:], least, ALU.is_equal))
            chain(dve.tensor_reduce(quota[:], above[:], AX_X, ALU.add))
            chain(dve.tensor_scalar(quota[:], quota[:], -1.0, float(TOPK), ALU.mult, ALU.add))
            src, n, step = equal[:], 0, 1
            while step < E:
                dst = pre[:, n % 2]
                dve.tensor_copy(dst[:, :, 0:step], src[:, :, 0:step])
                chain(dve.tensor_tensor(dst[:, :, step:], src[:, :, step:], src[:, :, 0:E - step], ALU.add))
                src, n, step = dst, n + 1, 2 * step
            chain(dve.tensor_tensor(src, src, quota[:].unsqueeze(2).to_broadcast([P, NT, E]), ALU.is_le))
            chain(dve.tensor_tensor(src, src, equal[:], ALU.mult))
            chain(dve.tensor_tensor(src, src, above[:], ALU.add))
            chain(dve.tensor_tensor(wts[:, :, 0:E], src, sg[:], ALU.mult))
            chain(dve.tensor_reduce(den[:], wts[:, :, 0:E], AX_X, ALU.add))
            chain(dve.reciprocal(den[:], den[:]))
            dve.memset(wts[:, :, E:], 1.0).then_inc(e_zg, 1)
            chain(dve.tensor_tensor(wts[:, :, 0:E], wts[:, :, 0:E], den[:].unsqueeze(2).to_broadcast([P, NT, E]), ALU.mult))
            for e in range(ES):
                dve.wait_ge(w_h, e + 1)
                dve.tensor_tensor(w_lo[:, e], w_raw[:, e % 2], w_hi[:, e].bitcast(F32), ALU.subtract).then_inc(w_l, 1)

            def gated(i, e):
                dve.wait_ge(e_sl, ES * i + e + 1)
                if e >= 2:
                    dve.wait_ge(e_gt, ES * i + e - 1)
                dve.scalar_tensor_tensor(out=g_s[:, e % 2, :], in0=bank[e % 2][:, FI:2 * FI], scalar=wt[:, e:e + 1],
                                         in1=sl[:, e % 2, :], op0=ALU.mult, op1=ALU.mult).then_inc(e_g, 1)

            def turned(i, e):
                dve.wait_ge(e_gt, ES * i + e + 1)
                dve.tensor_copy(gT[:, e % 2].rearrange("p c t -> p (c t)"), bank[2 + e % 2][0:FC, 0:2 * P]).then_inc(e_gTc, 1)

            with dve.Fori(0, NT) as i:
                dve.tensor_copy(wt[:], wts[:, bass.ds(i, 1), :].rearrange("p a e -> p (a e)")).then_inc(e_wt, 1)
                dve.wait_ge(e_hi, i + 1)
                dve.tensor_tensor(xgT_lo[:].rearrange("p k t -> p (k t)"), bank[5][:, 0:D],
                                  xgT_hi[:].bitcast(F32).rearrange("p k t -> p (k t)"), ALU.subtract).then_inc(e_lo, 1)
                dve.wait_ge(e_wt, i + 1)
                for e in range(ES):
                    gated(i, e)
                    turned(i, e)
                dve.wait_ge(e_y, i + 1)
                dve.wait_ge(e_out, i + 1)
                dve.tensor_tensor(zg, bank[4][:, 0:D], gate[:, bass.ds(i // TB + 1, 1), 1, :]
                                  .rearrange("p a n -> p (a n)"), ALU.mult).then_inc(e_zg, 1)

        @block.scalar
        def _(act):
            act.wait_ge(ld_a, 64)
            act.activation(cexp[:], cT_s[:], ACT.Exp, scale=-1.0).then_inc(c_exp, 1)
            for b in range(NB):
                act.wait_ge(p_h, KD * (b + 1))
                if b > 0:
                    act.wait_ge(p_st, 16 * b)
                act.activation(h_hl[:, 0], h_f[:], ACT.Copy).then_inc(p_hhi, 1)
                act.wait_ge(p_ctr, b + 1)
                if b > 0:
                    act.wait_ge(p_cst, 16 * b)
                act.activation(cq_hl[:, 0], out_bank[1][0:QL, :], ACT.Copy).then_inc(p_chi, 1)
            act.wait_ge(ld_b, 32)
            act.activation(wr_hi[:].rearrange("p k g n -> p (k g n)"), wr_raw, ACT.Copy).then_inc(wr_h, 1)
            act.wait_ge(zeroed, 2)
            act.wait_ge(ab_ev, 2)
            act.activation(ab_hi[0:QL], ab_f[:], ACT.Copy).then_inc(ab_h, 1)

            def aux(i, k, t):
                if t[0] in ("tq", "tk"):
                    s = t[1]
                    act.wait_ge(aux_done, aux_count(i, k))
                    act.activation((qT if t[0] == "tq" else kT)[:, s % 2, :], aux_home(i, k)[:], ACT.Copy).then_inc(s_qk, 1)
                elif t[0] == "ot":
                    act.wait_ge(aux_done, aux_count(i, k))
                    act.activation(oT[:, t[1], t[2], :], aux_home(i, k)[:], ACT.Copy).then_inc(s_ot, 1)

            def exponentials(i, u):
                act.wait_ge(s_max, (0 if i is None else UNITS * i) + u + 1)
                s, q = (u // TB) % 2, u % TB
                act.activation(prob[:, u % 2, :], score_bank[u % 2][:], ACT.Exp, bias=nmax[:, u % 4:u % 4 + 1],
                               accum_out=rsum[:, s, q:q + 1]).then_inc(s_exp, 1)

            for k, t in enumerate(AUX_FIRST):
                aux(None, k, t)
            exponentials(None, 0)
            exponentials(None, 1)
            with act.Fori(0, ITERS) as i:
                for u in range(UNITS):
                    act.wait_ge(s_pt, UNITS * i + u + 1)
                    act.activation(probT[:, u % 2, :], pt_bank[u % 2][:], ACT.Copy).then_inc(s_ptc, 1)
                    exponentials(i, u + 2)
                    for k, t in AUX_K[u]:
                        aux(i, k, t)
            for k, t in enumerate(LAST):
                aux(ITERS, k, t)

            for b in range(NB):
                act.wait_ge(f_tr, b + 1)
                if b > 0:
                    act.wait_ge(f_lg, b)
                for k in range(KD):
                    ins = act.activation(h2T[:, k, :], bank[k][:], ACT.Copy)
                ins.then_inc(f_h2T, 1)
                act.wait_ge(f_lg, b + 1)
                act.activation(sg[:, b * TB:(b + 1) * TB, :], bank[2][:, b * TB * E:(b + 1) * TB * E]
                               .rearrange("p (t e) -> p t e", t=TB), ACT.Exp, scale=-1.0).then_inc(f_sg, 1)
            for e in range(ES):
                act.wait_ge(ld_w[e % 2], 16 * (e // 2 + 1))
                act.activation(w_hi[:, e], w_raw[:, e % 2], ACT.Copy).then_inc(w_h, 1)
            with act.Fori(0, NT) as i:
                act.activation(xg[:], h2[:, bass.ds(i, 1), :].rearrange("p a n -> p (a n)"), ACT.Copy).then_inc(e_xg, 1)
                act.wait_ge(e_xt, i + 1)
                act.activation(xgT_hi[:].rearrange("p k t -> p (k t)"), bank[5][:, 0:D], ACT.Copy).then_inc(e_hi, 1)
                for e in range(ES):
                    act.wait_ge(e_h, ES * i + e + 1)
                    if e >= 2:
                        act.wait_ge(e_g, ES * i + e - 1)
                    act.activation(sl[:, e % 2, :], bank[e % 2][:, 0:FI], ACT.Silu).then_inc(e_sl, 1)

        @block.gpsimd
        def _(pool):
            own = [0]

            def chain(ins):
                own[0] += 1
                ins.then_inc(pool_c, 1)
                pool.wait_ge(pool_c, own[0])

            pool.memset(xa[:, 0:TB, :], 0.0).then_inc(s_x, 1)
            pool.memset(idle[:, 0:1], 0.0).then_inc(s_x, 1)
            pool.memset(idle[:, 1:2], 0.0).then_inc(e_out, 1)
            pool.memset(gate[:, 0], 0.0).then_inc(zeroed, 1)
            chain(pool.memset(mhalf[:], -0.5))
            pool.memset(ab_hi[:].bitcast(F32), 0.0)
            pool.memset(ab_lo[:].bitcast(F32), 0.0)
            pool.memset(cq_st[:].bitcast(F32), 0.0).then_inc(zeroed, 1)
            for b in range(NB):
                pool.wait_ge(p_stat, b + 1)
                chain(pool.tensor_scalar(ve[:, 0, :], mv[:, :, 1], EPS_LN, None, ALU.add))
                pool.tensor_tensor(rstd[:], ve[:, 0, :], mhalf[:, 0:TB], ALU.pow).then_inc(p_rstd, 1)
                pool.wait_ge(p_ssq, b + 1)
                pool.tensor_scalar(ve[:, 1, :], ssq[:, 0, :], 1.0 / QL, EPS_RMS, ALU.mult, ALU.add)
                chain(pool.tensor_scalar(ve[:, 2, :], ssq[:, 1, :], 1.0 / KL, EPS_RMS, ALU.mult, ALU.add))
                pool.tensor_tensor(rms[:].rearrange("p a t -> p (a t)"), ve[:, 1:3, :].rearrange("p a t -> p (a t)"),
                                   mhalf[:], ALU.pow).then_inc(p_rms, 1)
                pool.wait_ge(p_hhi, b + 1)
                if b > 0:
                    pool.wait_ge(p_st, 16 * b)
                pool.tensor_tensor(h_hl[:, 1].rearrange("p k t -> p (k t)"), h_f[:].rearrange("p k t -> p (k t)"),
                                   h_hl[:, 0].bitcast(F32).rearrange("p k t -> p (k t)"), ALU.subtract).then_inc(p_hlo, 1)

            def aux(i, k, t):
                if t[0] == "pr":
                    _, par, n = t
                    pool.wait_ge(s_sin, pr_count(i, par, n) + 1)
                    dst = qk_tok[:, par, n].rearrange("p a h c -> p (a h) c")
                    half = RD // 2
                    pool.tensor_tensor(dst[:, :, 0:half], t_cos[:, n % 2, :, 0:half], t_sin[:, n % 2, :, half:],
                                       ALU.subtract)
                    pool.tensor_tensor(dst[:, :, half:RD], t_cos[:, n % 2, :, half:], t_sin[:, n % 2, :, 0:half],
                                       ALU.add).then_inc(s_rope, 1)
                    tile = n if i is None else prep_batch(i, par) * TB + n
                    pool.tensor_copy(qk_tok[:, par, n, 1, :, RD:],
                                     ckv[:, bass.ds(tile, 1), :].to_broadcast([P, GH, KL])).then_inc(s_ck, 1)
                elif t[0] == "op":
                    _, par, n = t
                    c = 4 * i + (0 if par else 2) + n
                    pool.wait_ge(s_yg, c + 1)
                    pool.wait_ge(s_x, c + 2)
                    rows = xa[:, bass.ds(out_slot(i, par) * TB + 2 * n, 2), :]
                    pool.tensor_tensor(rows, rows, y_gate[:, n], ALU.add).then_inc(s_x, 1)

            for k, t in enumerate(AUX_FIRST):
                aux(None, k, t)
            with pool.Fori(0, ITERS) as i:
                for u in range(UNITS):
                    for k, t in AUX_K[u]:
                        aux(i, k, t)
            for k, t in enumerate(LAST):
                aux(ITERS, k, t)

            for b in range(NB):
                pool.wait_ge(f_stat, b + 1)
                chain(pool.tensor_scalar(ve2[:], mv2[:, :, 1], EPS_LN, None, ALU.add))
                pool.tensor_tensor(rstd2[:], ve2[:], mhalf[:, 0:TB], ALU.pow).then_inc(f_rstd, 1)
            with pool.Fori(0, NT) as i:
                pool.wait_ge(e_zg, i + 2)
                row = xa[:, bass.ds(i + TB, 1), :].rearrange("p a n -> p (a n)")
                pool.tensor_tensor(row, row, zg, ALU.add).then_inc(e_out, 1)


def rope_constants():
    freqs = (1.0 / 10000.0 ** (np.arange(0, RD, 2, dtype=np.float32) / np.float32(RD))).astype(np.float32)
    ang = np.outer(np.arange(SEQ, dtype=np.float32), freqs).astype(np.float32)
    t = np.stack([np.cos(ang), np.sin(ang)]).astype(np.float32)
    t = np.concatenate([t, t], axis=-1)
    t = np.stack([t * np.float32(SCALE), t], axis=1)
    return np.ascontiguousarray(t.reshape(2, 2, TB, P, RD).transpose(3, 2, 0, 1, 4))


def lay_out(inputs):
    a = {k: np.asarray(v) for k, v in inputs.items()}

    def rows(w, n):
        return w.reshape(n, P, -1).transpose(1, 0, 2)

    def heads(w, r):
        return w.reshape(r, H, HD).transpose(2, 1, 0)

    def rotary(w):
        return w.reshape(D, NG, 1, GH, RD // 2, 2).transpose(0, 1, 2, 3, 5, 4)

    r = np.concatenate([rotary(a["L0_attn_Wq_rope"]), rotary(a["L0_attn_Wk_rope"])], axis=2).reshape(D, NG * 512)
    out = {
        "x": a["L0_attn_x"].reshape(NT * P, D),
        "cT": rows(a["L0_c"].T, KD),
        "wmod": rows(a["L0_wmod"], KD),
        "wdn": rows(np.concatenate([a["L0_attn_Wq_down"], a["L0_attn_Wkv_down"]], axis=1), KD),
        "wqup": heads(a["L0_attn_Wq_up"], QL),
        "wkup": heads(a["L0_attn_Wk_up"], KL),
        "wvup": heads(a["L0_attn_Wv_up"], KL),
        "wout": a["L0_attn_Wout"].reshape(H, HD, D).transpose(1, 0, 2),
        "wrope": rows(r, KD).reshape(P, -1),
        "rope_tab": rope_constants(),
        "eye": np.eye(P, dtype=np.float32),
        "qnw": a["L0_attn_q_norm_w"].reshape(QL, 1),
        "kvw_bc": np.broadcast_to(a["L0_attn_kv_norm_w"], (QL, KL)),
        "kvw2": np.concatenate([a["L0_attn_kv_norm_w"]] * 2).reshape(P, 1),
    }

    def experts(w, ws):
        return np.concatenate([w, ws.reshape(2, FI, D)]).transpose(0, 2, 1)

    w13 = np.concatenate([experts(a["L0_ffn_W1"], a["L0_ffn_Ws1"]), experts(a["L0_ffn_W3"], a["L0_ffn_Ws3"])], axis=2)
    w2 = np.concatenate([a["L0_ffn_W2"].transpose(0, 2, 1), a["L0_ffn_Ws2"].T.reshape(2, FI, D)])
    out["wgate"] = rows(a["L0_ffn_gate_w"].T, KD)
    out["w13"] = w13.reshape(ES, KD, P, 2 * FI).transpose(2, 0, 1, 3)
    out["w2"] = w2.reshape(ES, 2, FC, D).transpose(2, 0, 1, 3)
    out["earlier"] = np.broadcast_to(np.tril(np.ones((EG, EG), np.float32), -1), (P, EG, EG))
    return {k: np.ascontiguousarray(v) for k, v in out.items()}


def kernel(**inputs):
    import concourse.bacc as _bacc
    from concourse.bass_utils import run_bass_kernel_spmd as _run

    nc = _bacc.Bacc("TRN2", target_bir_lowering=False, num_devices=1)
    arrays = lay_out(inputs)
    args = {n: nc.dram_tensor(f"in_{n}", a.shape, mybir.dt.from_np(a.dtype), kind="ExternalInput").ap()
            for n, a in arrays.items()}
    args["out"] = nc.dram_tensor("out_x", (NT * P, D), F32, kind="ExternalOutput").ap()
    program(nc, **args)
    r = _run(nc, [{f"in_{n}": a for n, a in arrays.items()}], core_ids=[0])
    return r.results[0]["out_x"].reshape(NB, SEQ, D)
```

```python
import math
from contextlib import ExitStack

import numpy as np
import concourse.bass as bass
from concourse import mybir

F32 = mybir.dt.float32
F32R = mybir.dt.float32r
I32 = mybir.dt.int32
U32 = mybir.dt.uint32
ALU = mybir.AluOpType
ACT = mybir.ActivationFunctionType
AX_X = mybir.AxisListType.X

P = 128
NB, SEQ, D = 4, 512, 256
TB = SEQ // P
NT = NB * TB
KD = D // P
H, HD, RD = 16, 128, 64
QL, KL = 48, 64
GH = 4
NG = H // GH
EPS_RMS, EPS_LN = 1e-6, 1e-5
SCALE = (HD + RD) ** -0.5
E, TOPK, EG, TOPG = 16, 4, 4, 2
FI = 176
FC = FI // 2
ES = E + 2

SLOT_TILES = NT * P * TOPK // P + E
X_W = D
X_DEST = D + E
XW = D + 2 * E
NOWHERE = NT * P * TOPK
CYCLE = 4
assert SLOT_TILES % CYCLE == 0

R_EARLY, R_TRI = 0, EG * EG
R_FULL = R_TRI + P
R_TILE = R_FULL + NT
R_TOKEN = R_TILE + SLOT_TILES
R_ALL = R_TOKEN + NT

IT_HEADS = 2 * GH
UNITS = IT_HEADS * TB
ITERS = NB * H // IT_HEADS
AHEAD = 3


def aux_plan():
    at = {u: [] for u in range(UNITS)}
    for s in range(1, IT_HEADS + 1):
        at[4 * s - 2].append(("tq", s + 1))
        at[4 * s - 1].append(("tk", s + 1))
    for par, start in ((1, 0), (0, 16)):
        for n, (p, a) in enumerate(((0, 1), (2, 3), (5, 6), (8, 9))):
            at[start + p].append(("pr", par, n))
            at[start + a].append(("ab", par, n))
    for par, a, b in ((1, (10, 10), (13, 14)), (0, (20, 21), (25, 26))):
        for n in range(2):
            at[a[n]].append(("ot", par, n))
            at[b[n]].append(("op", par, n))
    return at


AUX_FIRST = [("pr", 0, 0), ("ab", 0, 0), ("pr", 0, 1), ("ab", 0, 1), ("pr", 0, 2), ("ab", 0, 2),
             ("pr", 0, 3), ("ab", 0, 3), ("tq", 0), ("tk", 0), ("tq", 1), ("tk", 1)]
AUX_AT = aux_plan()
AUX_LIST = [t for u in range(UNITS) for t in AUX_AT[u]]
AUX_N = len(AUX_LIST)
assert AUX_N % 2 == 0


PADS = SLOT_TILES // ITERS
assert PADS * ITERS == SLOT_TILES


def program(nc, x, cT, wmod, wdn, wqup, wkup, wvup, wout, wrope, rope_tab, eye, qnw, kvw_bc, kvw2, wgate, w13, w2,
            route, out):
    ctx = ExitStack()
    with ctx:
        def sb(name, shape, dt=F32):
            return ctx.enter_context(nc.sbuf_tensor(name, shape, dt))

        def sem(name):
            return ctx.enter_context(nc.semaphore(name))

        bank = [ctx.enter_context(nc.psum_tensor(f"bank{i}", [P, 512], F32)) for i in range(8)]
        score_bank, pt_bank, out_bank, aux_bank = bank[0:2], bank[2:4], bank[4:6], bank[6:8]

        h_dram = nc.dram_tensor("h_dram", [NB, P, 2 * KD * SEQ], F32).ap()
        mod_dram = nc.dram_tensor("mod_dram", [NB, P, 2 * D], F32).ap()
        slots = nc.dram_tensor("slots", [SLOT_TILES * P, XW], F32).ap()
        parts = nc.dram_tensor("parts", [NT * P * TOPK, D], F32).ap()
        cq_dram = nc.dram_tensor("cq_dram", [NB, QL, 2 * SEQ], F32).ap()

        ident = sb("ident", [P, P])
        gate = sb("gate", [P, NB + 1, 2, D])
        xa = sb("xa", [P, (NB + 1) * TB, D])
        mhalf = sb("mhalf", [P, NT])
        idle = sb("idle", [P, 4])

        attention = ExitStack()

        def sb2(name, shape, dt=F32):
            return attention.enter_context(nc.sbuf_tensor(name, shape, dt))

        rope = sb2("rope", [P, TB, 2, 2, RD])
        wr_hi = sb2("wr_hi", [P, KD, NG, 512], F32R)
        wr_lo = sb2("wr_lo", [P, KD, NG, 512], F32R)
        ab_hi = sb2("ab_hi", [P, H * KL], F32R)
        ab_lo = sb2("ab_lo", [P, H * KL], F32R)
        mout = sb2("mout", [P, H // 2, D])
        modT = sb2("modT", [P, 4, KD, NB])
        ckv = sb2("ckv", [P, NT, KL])
        h_st = sb2("h_st", [P, 2, KD, SEQ], F32R)
        cq_st = sb2("cq_st", [P, 2, SEQ], F32R)
        qk_tok = sb2("qk_tok", [P, 2, TB, 2, GH, P])
        o_tok = sb2("o_tok", [P, 2, TB, GH * KL])

        pad = sb2("pad", [P, XW])

        wr_raw = qk_tok[:].rearrange("p a t q h c -> p a (t q h c)")[:, 0]
        wout_s = qk_tok[:].rearrange("p a t q h c -> p a (t q h c)")[:, 1].rearrange("p (h d) -> p h d", h=H)
        first = ExitStack()

        def sb1(name, shape, dt=F32):
            return first.enter_context(nc.sbuf_tensor(name, shape, dt))

        wmod_s = sb1("wmod_s", [P, KD, 6 * D])
        wdn_s = sb1("wdn_s", [P, KD, QL + KL])
        wqup_s = sb1("wqup_s", [P, H, QL])
        wkup_s = sb1("wkup_s", [P, H, KL])
        ab_f = sb1("ab_f", [QL, H * KL])
        qnw_s = sb1("qnw_s", [QL, 1])
        qnw_sc = sb1("qnw_sc", [QL, 1])
        kvwb_s = sb1("kvwb_s", [QL, KL])
        cT_s = sb1("cT_s", [P, KD, NB])
        cexp = sb1("cexp", [P, KD, NB])
        crec = sb1("crec", [P, KD, NB])
        csil = sb1("csil", [P, KD, NB])
        csil_bc = sb1("csil_bc", [P, KD, NB, P])
        mod_o = sb1("mod_o", [P, 2, 2, D])
        bst = sb1("bst", [P, NT, 6])
        mv = sb1("mv", [P, NT, 2])
        ve = sb1("ve", [P, 2, 3, NT // 2])
        rstd = sb1("rstd", [P, 2, NT // 2])
        xn = o_tok[:].rearrange("p a q n -> p a (q n)").rearrange("p a (t d) -> p a t d", t=TB)
        h_f = sb1("h_f", [P, KD, SEQ])
        wvup_s = sb1("wvup_s", [P, H, KL])
        kvw2_s = sb1("kvw2_s", [P, 1])
        h_hl = sb1("h_hl", [P, 2, KD, SEQ], F32R)
        gabs, gsgn = h_f[:, 0, :], h_f[:, 1, :]
        dn = sb1("dn", [P, NT, QL + KL])
        dsq = mout[:].rearrange("p a n -> p (a n)")[:, 0:NT * (QL + KL)].rearrange("p (t n) -> p t n", t=NT)
        ssq = sb1("ssq", [P, 2, 2, NT // 2])
        rms = sb1("rms", [P, 2, 2, NT // 2])
        ncq = sb1("ncq", [P, NT, QL])
        cq_hl = h_hl[0:QL].rearrange("p a k t -> p (a k t)")[:, 0:2 * SEQ].rearrange("p (a t) -> p a t", a=2)
        first.close()

        t_cos = sb2("t_cos", [P, 2, 2 * GH, RD])
        t_sin = sb2("t_sin", [P, 2, 2 * GH, RD])
        qT = sb2("qT", [P, 2, 2, SEQ], F32R)
        kT = sb2("kT", [P, 2, 2, SEQ], F32R)
        nmax = sb2("nmax", [P, 4])
        prob = sb2("prob", [P, 2, SEQ])
        rsum = sb2("rsum", [P, 2, TB])
        rinv = sb2("rinv", [P, 2, TB])
        probT = sb2("probT", [P, 2, SEQ])
        oT = sb2("oT", [P, 2, 2, SEQ])
        y_gate = sb2("y_gate", [P, 2, 2, D])

        attention.close()

        w_hi = sb("w_hi", [P, ES, KD, 2 * FI], F32R)
        loaded = ExitStack()
        w_raw = loaded.enter_context(nc.sbuf_tensor("w_raw", [P, ES, KD, 2 * FI], F32))
        loaded.close()
        w_lo = sb("w_lo", [P, ES, KD, 2 * FI], F32R)
        w2_p = sb("w2_p", [P, ES, 2, D])
        w2_s = w2_p[0:FC]
        h2T = w2_p[:, 0:2].rearrange("p e c n -> p (e c n)").rearrange("p (k t) -> p k t", k=KD)
        own_i = sb("own_i", [P, SLOT_TILES], I32)
        gw_s = sb("gw_s", [P, KD, E])
        tab = sb("tab", [P, R_ALL])
        early_s = tab[:, R_EARLY:R_TRI].rearrange("p (a b) -> p a b", a=EG)
        tri_s = tab[:, R_TRI:R_FULL]
        full_s = tab[:, R_FULL:R_TILE]
        tile_s = tab[:, R_TILE:R_TOKEN]
        token_s = tab[:, R_TOKEN:R_ALL]
        bst2 = sb("bst2", [P, TB, 6])
        mv2 = sb("mv2", [P, TB, 2])
        ve2 = sb("ve2", [P, TB])
        rstd2 = sb("rstd2", [P, TB])
        h2 = sb("h2", [P, NT, XW])
        ones = sb("ones", [P, P])
        sg = sb("sg", [P, NT, E])
        gm = sb("gm", [P, NT, EG])
        gsel = sb("gsel", [P, NT, EG])
        msk = sb("msk", [P, NT, E])
        top = sb("top", [P, NT, 8])
        above = sb("above", [P, NT, E])
        equal = sb("equal", [P, NT, E])
        pre = sb("pre", [P, 2, NT, E])
        gtm = above[:].rearrange("p t (a b) -> p t a b", a=EG)
        gem = equal[:].rearrange("p t (a b) -> p t a b", a=EG)
        quota = sb("quota", [P, NT])
        den = sb("den", [P, NT])
        spare = xa[:, 0:TB, :].rearrange("p a n -> p (a n)")
        started = spare[:, 0:SLOT_TILES // 2 * (E + 1)].rearrange("p (s e) -> p s e", s=SLOT_TILES // 2)
        picked = spare.rearrange("p (t r e) -> p t r e", t=NT, r=TOPK)
        loads = sb("loads", [P, E])
        tiles_of = sb("tiles_of", [P, 2, E + 1])
        owner = sb("owner", [P, SLOT_TILES, E])
        own_f = sb("own_f", [P, SLOT_TILES])
        slot_f = sb("slot_f", [P, NT, TOPK])
        slot_i = sb("slot_i", [P, NT, TOPK], U32)
        x_hl = sb("x_hl", [P, 2, 2, KD * P], F32R)
        modb = x_hl[:].bitcast(F32).rearrange("p a b n -> p (a b n)").rearrange("p (b a n) -> p b a n", b=2, a=2)
        sl = sb("sl", [P, 2, FI])
        g_s = pre[:].rearrange("p a t e -> p (a t e)")[:, 0:2 * FI].rearrange("p (a n) -> p a n", a=2)
        gT = sb("gT", [FC, 2, 2, P])
        chosen_by = sb("chosen_by", [P, CYCLE, 2, E])
        x_now = sb("x_now", [P, D])
        sel = sb("sel", [P, CYCLE, 2])
        sel_i = sb("sel_i", [P, CYCLE], U32)
        h2_flat = h2[:].rearrange("p t n -> p (t n)")
        xs = h2_flat[:, 0:CYCLE * XW].rearrange("p (j n) -> p j n", j=CYCLE)
        ys = h2_flat[:, CYCLE * XW:CYCLE * (XW + D)].rearrange("p (j n) -> p j n", j=CYCLE)
        zg = msk[:].rearrange("p t e -> p (t e)")
        yb = w_hi[:].bitcast(F32).rearrange("p e k n -> p (e k n)")[:, 0:4 * TOPK * D].rearrange("p (j n) -> p j n", j=4)
        ysum = h2_flat[:, 0:2 * D].rearrange("p (j n) -> p j n", j=2)
        ygate = h2_flat[:, 2 * D:4 * D].rearrange("p (j n) -> p j n", j=2)

        ld_a, ld_b, ld_c, ld_d, ld_m, ld_v = (sem(n) for n in ("ld_a", "ld_b", "ld_c", "ld_d", "ld_m", "ld_v"))
        ld_x = [sem(f"ld_x{b}") for b in range(NB)]
        dve_c, act_c, pool_c = sem("dve_c"), sem("act_c"), sem("pool_c")
        c_exp, c_sil, mod_mm, mod_ev = sem("c_exp"), sem("c_sil"), sem("mod_mm"), sem("mod_ev")
        ab_mm, ab_ev, ab_rd = sem("ab_mm"), sem("ab_ev"), sem("ab_rd")
        m_mm, m_ev, g_mm, g_ev = sem("m_mm"), sem("m_ev"), sem("g_mm"), sem("g_ev")
        wr_h, wr_l, ab_h, ab_l = sem("wr_h"), sem("wr_l"), sem("ab_h"), sem("ab_l")
        zeroed = sem("zeroed")
        p_stat, p_rstd, p_xn, p_tr, p_h, p_hhi, p_hlo = (sem(n) for n in
            ("p_stat", "p_rstd", "p_xn", "p_tr", "p_h", "p_hhi", "p_hlo"))
        p_dn, p_ssq, p_rms, p_ncq, p_ctr, p_chi, p_clo, p_st, p_cst = (sem(n) for n in
            ("p_dn", "p_ssq", "p_rms", "p_ncq", "p_ctr", "p_chi", "p_clo", "p_st", "p_cst"))
        p_dnev = sem("p_dnev")
        staged = sem("staged")
        s_score, s_max, s_exp, s_pt, s_ptc, s_pv, s_norm, s_rinv = (sem(n) for n in
            ("s_score", "s_max", "s_exp", "s_pt", "s_ptc", "s_pv", "s_norm", "s_rinv"))
        aux_done = sem("aux_done")
        s_ql = sem("s_ql")
        s_sin, s_rope, s_ck, s_ab, s_qk, s_ot, s_yg, s_x = (sem(n) for n in
            ("s_sin", "s_rope", "s_ck", "s_ab", "s_qk", "s_ot", "s_yg", "s_x"))
        stored, mb_mm, mb_ev, ld_f = (sem(n) for n in
            ("stored", "mb_mm", "mb_ev", "ld_f"))
        ld_w2 = sem("ld_w2")
        padded, pad_set, sent, masked, counted, listed, indexed, extended = (sem(n) for n in
            ("padded", "pad_set", "sent", "masked", "counted", "listed", "indexed", "extended"))
        z_x, z_hi, z_lo, z_h, z_sl, z_g, z_gt, z_gTc, z_y, z_zg, z_out = (sem(n) for n in
            ("z_x", "z_hi", "z_lo", "z_h", "z_sl", "z_g", "z_gt", "z_gTc", "z_y", "z_zg", "z_out"))
        e_go = sem("e_go")
        z_now = sem("z_now")
        e_mul, e_sel, e_idx, e_yc = (sem(n) for n in ("e_mul", "e_sel", "e_idx", "e_yc"))
        ld_s = [sem(f"ld_s{j}") for j in range(CYCLE)]
        e_put = [sem(f"e_put{j}") for j in range(CYCLE)]
        ld_y = [sem(f"ld_y{j}") for j in range(4)]
        y_sum, y_gat, y_add = sem("y_sum"), sem("y_gat"), sem("y_add")
        mb_st = [sem("mb_st0"), sem("mb_st1")]
        mb_ld = [sem("mb_ld0"), sem("mb_ld1")]
        ld_ws, ld_ws2, ld_w = sem("ld_ws"), sem("ld_ws2"), sem("ld_w")
        w_h, w_l, f_stat, f_rstd, f_h2, f_tr, f_h2T, f_lg, f_sg, f_wts = (sem(n) for n in
            ("w_h", "w_l", "f_stat", "f_rstd", "f_h2", "f_tr", "f_h2T", "f_lg", "f_sg", "f_wts"))
        e_x, e_hi, e_lo, e_h, e_sl, e_g, e_gt, e_gTc, e_y = (sem(n) for n in
            ("e_x", "e_hi", "e_lo", "e_h", "e_sl", "e_g", "e_gt", "e_gTc", "e_y"))

        block = ctx.enter_context(nc.Block())

        def aux_count(i, k):
            return k + 1 if i is None else AUX_N * i + len(AUX_FIRST) + k + 1

        def aux_home(i, k):
            return aux_bank[(k if i is None else len(AUX_FIRST) + k) % 2]

        def read_out(i, t):
            if t[0] in ("tq", "tk"):
                return s_ql, (0 if i is None else 2 * IT_HEADS * i) + 2 * t[1] + (1 if t[0] == "tq" else 2)
            if t[0] in ("pr", "ab"):
                return s_sin if t[0] == "pr" else s_ab, pr_count(i, t[1], t[2]) + 1
            return s_ot if t[0] == "ot" else s_yg, 4 * i + (0 if t[1] else 2) + t[2] + 1

        def pr_count(i, par, n):
            return n if i is None else 2 * TB * i + (TB if par else 2 * TB) + n

        def aux_tasks():
            k = 0
            for u in range(UNITS):
                for t in AUX_AT[u]:
                    yield u, k, t
                    k += 1

        AUX_K = {u: [] for u in range(UNITS)}
        for u, k, t in aux_tasks():
            AUX_K[u].append((k, t))

        def it_batch(i):
            return i // 2

        def prep_batch(i, par):
            return i // 2 if par else ((i + 1) // 2) % NB

        def prep_group(i, par):
            return (i % 2) * 2 + 1 if par else ((i + 1) % 2) * 2

        def out_pair(i, par):
            return ((i + 1) % 2) * 4 + 2 if par else (i % 2) * 4

        def out_slot(i, par):
            return (i + 1) // 2 if par else i // 2 + 1

        Z_LOOP = range(2, NT - 4)
        E_LOOP = range(CYCLE, SLOT_TILES - CYCLE)

        def shared_steps(engine, step):
            for t in range(-2, Z_LOOP.start):
                step(t, t % 2)
            with engine.Fori(0, len(Z_LOOP) // 2) as i:
                for j in range(2):
                    step(i * 2 + (Z_LOOP.start + j), j)
            for t in range(Z_LOOP.stop, NT):
                step(t, t % 2)

        def expert_steps(engine, step, look_up=None):
            def ahead(first, count):
                return () if look_up is None else (look_up(first, count),)

            more = ahead(0, CYCLE + 2)
            for n in range(-3, E_LOOP.start):
                step(n, n % CYCLE, *more)
            with engine.Fori(0, len(E_LOOP) // CYCLE) as i:
                more = ahead(i * CYCLE + E_LOOP.start, CYCLE + 2)
                for j in range(CYCLE):
                    step(i * CYCLE + (E_LOOP.start + j), j, *more)
            more = ahead(E_LOOP.stop, CYCLE)
            for n in range(E_LOOP.stop, SLOT_TILES):
                step(n, n % CYCLE, *more)

        def static(n):
            return isinstance(n, int)

        def within(n, limit):
            return not static(n) or 0 <= n < limit

        def over(n, d):
            return n // d

        LAST = [("ot", 1, 0), ("ot", 1, 1), ("op", 1, 0), ("op", 1, 1)]

        @block.sync
        def _(sp):
            sp.dma_start(cT_s[:], cT).then_inc(ld_a, 16)
            sp.dma_start(wmod_s[:, :, 0:2 * D], wmod[:, :, 0:2 * D]).then_inc(ld_a, 16)
            sp.dma_start(ident[:], eye).then_inc(ld_a, 16)
            for b in range(NB):
                sp.dma_start(xa[:, TB * (b + 1):TB * (b + 2), :],
                             x[SEQ * b:SEQ * (b + 1)].rearrange("(t p) d -> p t d", p=P)).then_inc(ld_x[b], 16)
            sp.dma_start(wdn_s[:], wdn).then_inc(ld_d, 16)
            sp.dma_start(wr_raw, wrope).then_inc(ld_b, 16)
            sp.dma_start(rope[:], rope_tab).then_inc(ld_b, 16)
            sp.dma_start(wqup_s[:], wqup).then_inc(ld_c, 16)
            sp.dma_start(wkup_s[:], wkup).then_inc(ld_c, 16)
            sp.dma_start(qnw_s[:], qnw).then_inc(ld_c, 16)
            sp.dma_start(kvwb_s[:], kvw_bc).then_inc(ld_c, 16)
            sp.dma_start(wmod_s[:, :, 2 * D:], wmod[:, :, 2 * D:]).then_inc(ld_m, 16)
            sp.dma_start(wvup_s[:], wvup).then_inc(ld_v, 16)
            sp.dma_start(wout_s, wout).then_inc(ld_v, 16)
            sp.dma_start(kvw2_s[:], kvw2).then_inc(ld_v, 16)
            def stage(b):
                sp.dma_start(h_st[:].bitcast(F32).rearrange("p a k t -> p (a k t)"),
                             h_dram[bass.ds(b, 1)].rearrange("b p n -> (b p) n")).then_inc(staged, 16)
                sp.dma_start(cq_st[0:QL].bitcast(F32).rearrange("p a t -> p (a t)"),
                             cq_dram[bass.ds(b, 1)].rearrange("b p n -> (b p) n")).then_inc(staged, 16)

            for b in range(NB):
                sp.wait_ge(p_hhi, b + 1)
                sp.wait_ge(p_hlo, b + 1)
                sp.dma_start(h_dram[b], h_hl[:].bitcast(F32).rearrange("p a k t -> p (a k t)")).then_inc(p_st, 16)
            for b in range(NB):
                sp.wait_ge(p_chi, b + 1)
                sp.wait_ge(p_clo, b + 1)
                sp.dma_start(cq_dram[b], cq_hl.bitcast(F32).rearrange("p a t -> p (a t)")).then_inc(p_cst, 16)
                if b == 0:
                    sp.wait_ge(p_st, 16 * NB)
                    sp.wait_ge(p_cst, 16)
                    sp.wait_ge(zeroed, 2)
                    stage(0)
            sp.wait_ge(p_cst, 16 * NB)

            for b in range(NB):
                sp.wait_ge(mb_ev, b + 1)
                sp.dma_start(mod_dram[b], mod_o[:, b % 2].rearrange("p a n -> p (a n)")).then_inc(mb_st[b % 2], 16)
            for q in mb_st:
                sp.wait_ge(q, 32)
            last = max(k for u, k, t in aux_tasks() if t[0] in ("pr", "ab") and t[1] == 1)
            sp.wait_ge(pad_set, 3)
            with sp.Fori(0, ITERS) as i:
                sp.wait_ge(aux_done, aux_count(i, last))
                stage(((i + 1) // 2) % NB)
                sp.dma_start(slots[bass.ds(i * (PADS * P), PADS * P)].rearrange("(s p) n -> p s n", p=P),
                             pad[:].unsqueeze(1).to_broadcast([P, PADS, XW])).then_inc(padded, 16)
            sp.wait_ge(staged, 32 * (ITERS + 1))
            sp.wait_ge(s_x, 4 * ITERS + 4)
            for b in range(NB):
                if b >= 2:
                    sp.wait_ge(f_h2, b - 1)
                sp.dma_start(modb[:, b % 2].rearrange("p a n -> p (a n)"), mod_dram[b]).then_inc(mb_ld[b % 2], 16)
                if b == 0:
                    sp.wait_ge(padded, 16 * ITERS)
                    sp.dma_start(gw_s[:], wgate).then_inc(ld_f, 16)
                    sp.dma_start(tab[:], route).then_inc(ld_f, 16)
                if b == 1:
                    sp.dma_start(w_raw[:, E:], w13[:, E:]).then_inc(ld_ws, 16)
                    sp.dma_start(w2_s[:, E:], w2[:, E:]).then_inc(ld_ws2, 16)
            for e in range(0, E, 4):
                sp.dma_start(w_raw[:, e:e + 4], w13[:, e:e + 4]).then_inc(ld_w, 16)
            sp.wait_ge(f_lg, NB)
            sp.dma_start(w2_s[:, 0:E], w2[:, 0:E]).then_inc(ld_w2, 16)

            sp.wait_ge(sent, 16 * NT * TOPK)
            sp.wait_ge(z_x, NT)

            def load_slots(n, j):
                if not within(n + 3, SLOT_TILES):
                    return
                m, jm = n + 3, (j + 3) % CYCLE
                if not (static(n) and m < CYCLE):
                    sp.wait_ge(e_x, m - CYCLE + 1)
                    sp.wait_ge(e_mul, m - CYCLE + 1)
                sp.dma_start(xs[:, jm], slots[bass.ds(m * P, P)] if not static(m) else slots[m * P:(m + 1) * P])\
                    .then_inc(ld_s[jm], 16)

            expert_steps(sp, load_slots)

            for j in range(CYCLE):
                sp.wait_ge(e_put[j], 16 * (SLOT_TILES // CYCLE))
            sp.wait_ge(e_g, SLOT_TILES)
            own_parts = parts.rearrange("(t p r) d -> t p (r d)", t=NT, r=TOPK)
            for t in range(4):
                sp.dma_start(yb[:, t], own_parts[t]).then_inc(ld_y[t], 16)
            for b in range(NB):
                if b + 1 < NB:
                    for j in range(4):
                        sp.wait_ge(y_sum, 4 * b + j + 1)
                        sp.dma_start(yb[:, j], own_parts[4 * b + j + 4]).then_inc(ld_y[j], 16)
                sp.wait_ge(y_add, 4 * (b + 1))
                sp.dma_start(out[SEQ * b:SEQ * (b + 1)].rearrange("(t p) d -> p t d", p=P),
                             xa[:, TB * (b + 1):TB * (b + 2), :]).then_inc(stored, 16)
            sp.wait_ge(stored, 16 * NB)

        @block.tensor
        def _(pe):
            def mm3(dst, l_hi, l_lo, r_hi, r_lo, start, stop):
                pe.matmul(dst, l_hi, r_hi, start=start, stop=False)
                pe.matmul(dst, l_hi, r_lo, start=False, stop=False)
                return pe.matmul(dst, l_lo, r_hi, start=False, stop=stop)

            pe.wait_ge(ld_a, 48)
            pe.wait_ge(c_sil, 1)
            for w in range(2):
                for c in range(KD):
                    for k in range(KD):
                        mm = pe.matmul(aux_bank[0][:, (w * KD + c) * NB:(w * KD + c + 1) * NB],
                                       wmod_s[:, k, w * D + c * P:w * D + (c + 1) * P],
                                       csil[:, k, :], start=(k == 0), stop=(k == KD - 1))
            mm.then_inc(mod_mm, 1)

            def down(b):
                pe.wait_ge(p_h, KD * (b + 1))
                if b >= 2:
                    pe.wait_ge(p_dnev, b - 1)
                for t in range(TB):
                    for k in range(KD):
                        mm = pe.matmul(out_bank[b % 2][:, t * P:t * P + QL + KL], h_f[:, k, t * P:(t + 1) * P],
                                       wdn_s[:, k, :], start=(k == 0), stop=(k == KD - 1))
                mm.then_inc(p_dn, 1)

            def turn_latents(b):
                pe.wait_ge(p_ncq, b // 2 + 1)
                if b >= 2:
                    pe.wait_ge(p_clo, b - 1)
                for t in range(TB):
                    mm = pe.transpose(pt_bank[b % 2][0:QL, t * P:(t + 1) * P], ncq[:, b * TB + t, :], ident[:])
                mm.then_inc(p_ctr, 1)

            pe.wait_ge(mod_ev, 1)
            for b in range(NB):
                pe.wait_ge(p_xn, b + 1)
                for k in range(KD):
                    if b > 0:
                        pe.wait_ge(p_h, KD * (b - 1) + k + 1)
                    for t in range(TB):
                        mm = pe.transpose(aux_bank[k][:, t * P:(t + 1) * P], xn[:, b % 2, t, k * P:(k + 1) * P], ident[:])
                    mm.then_inc(p_tr, 1)
                if b == 0:
                    pe.wait_ge(ld_d, 16)
                down(b)
            turn_latents(0)
            turn_latents(1)

            pe.wait_ge(ld_c, 16 * 4)
            pe.wait_ge(p_dnev, NB)
            for h in range(H):
                mm = pe.matmul(out_bank[h // 8][0:QL, (h % 8) * KL:(h % 8 + 1) * KL], wqup_s[:, h, :],
                               wkup_s[:, h, :], start=True, stop=True)
                if h % 8 == 7:
                    mm.then_inc(ab_mm, 1)
            turn_latents(2)
            turn_latents(3)
            pe.wait_ge(ld_m, 16)
            pe.wait_ge(c_sil, 2)
            for n, (b, chunks) in enumerate([(b, c) for c in ((2, 5), (3, 4)) for b in range(NB)]):
                if n >= 2:
                    if n - 2 < NB:
                        pe.wait_ge(g_ev, n - 1)
                    else:
                        pe.wait_ge(mb_ev, n - 1 - NB)
                for w in range(2):
                    for k in range(KD):
                        mm = pe.matmul(score_bank[n % 2][:, w * D:(w + 1) * D], csil_bc[:, k, b, :],
                                       wmod_s[:, k, chunks[w] * D:(chunks[w] + 1) * D],
                                       start=(k == 0), stop=(k == KD - 1))
                mm.then_inc(g_mm if n < NB else mb_mm, 1)

            def aux(i, k, t):
                dst = aux_home(i, k)
                if t[0] == "ab":
                    pe.wait_ge(ab_l, 1)
                if i is None and k >= 2:
                    pe.wait_ge(*read_out(None, AUX_FIRST[k - 2]))
                elif i is not None and k >= 2:
                    pe.wait_ge(*read_out(i, (LAST if isinstance(i, int) else AUX_LIST)[k - 2]))
                elif i is not None:
                    kind, s = AUX_LIST[AUX_N - 2 + k]
                    pe.wait_ge(*read_out(i, (kind, s - IT_HEADS)))
                if t[0] == "pr":
                    _, par, n = t
                    g = 0 if i is None else prep_group(i, par)
                    if n == 0 and (i is None or par == 0):
                        pe.wait_ge(staged, 32 if i is None else 32 * (i + 2))
                    for c in range(KD):
                        tok = slice(n * P, (n + 1) * P)
                        mm = mm3(dst[:], h_st[:, 0, c, tok], h_st[:, 1, c, tok],
                                 wr_hi[:, c, bass.ds(g, 1), :].rearrange("p a n -> p (a n)"),
                                 wr_lo[:, c, bass.ds(g, 1), :].rearrange("p a n -> p (a n)"),
                                 c == 0, c == KD - 1)
                elif t[0] == "ab":
                    _, par, n = t
                    g = 0 if i is None else prep_group(i, par)
                    tok = slice(n * P, (n + 1) * P)
                    mm = mm3(dst[:, 0:GH * KL], cq_st[:, 0, tok], cq_st[:, 1, tok],
                             ab_hi[:, bass.ds(g * (GH * KL), GH * KL)], ab_lo[:, bass.ds(g * (GH * KL), GH * KL)],
                             True, True)
                elif t[0] in ("tq", "tk"):
                    s = t[1]
                    par, hh = (s // GH) % 2, s % GH
                    if t[0] == "tq" and hh == 0:
                        n = pr_count(i, par, TB) if i is not None else TB
                        pe.wait_ge(s_rope, n)
                        pe.wait_ge(s_ab, n)
                        pe.wait_ge(s_ck, n)
                    for n in range(TB):
                        mm = pe.transpose(dst[:, n * P:(n + 1) * P], qk_tok[:, par, n, int(t[0] == "tk"), hh, :], ident[:])
                elif t[0] == "ot":
                    _, par, n = t
                    pe.wait_ge(s_norm, IT_HEADS * i + (0 if par else GH) + 1)
                    for q in range(TB):
                        mm = pe.transpose(dst[:, q * P:(q + 1) * P], o_tok[:, par, q, n * P:(n + 1) * P], ident[:])
                else:
                    _, par, n = t
                    if n == 0:
                        pe.wait_ge(s_ot, 4 * i + (2 if par else 4))
                    g2 = out_pair(i, par)
                    for q in range(2):
                        for pp in range(2):
                            mm = pe.matmul(dst[:, q * D:(q + 1) * D], oT[:, par, pp, (2 * n + q) * P:(2 * n + q + 1) * P],
                                           mout[:, bass.ds(g2 + pp, 1), :].rearrange("p a n -> p (a n)"),
                                           start=(pp == 0), stop=(pp == 1))
                mm.then_inc(aux_done, 1)

            def score(i, u):
                s, q = u // TB, u % TB
                if i is None:
                    if q == 0:
                        pe.wait_ge(s_ql, 2 * (s + 1))
                    if u >= 2:
                        pe.wait_ge(s_exp, u - 1)
                else:
                    if q == 0:
                        pe.wait_ge(s_ql, 2 * IT_HEADS * i + 2 * (s + 1))
                    pe.wait_ge(s_exp, UNITS * i + u - 1)
                tok = slice(q * P, (q + 1) * P)
                mm3(score_bank[u % 2][:], qT[:, s % 2, 0, tok], qT[:, s % 2, 1, tok], kT[:, s % 2, 0, :], kT[:, s % 2, 1, :],
                    True, True).then_inc(s_score, 1)

            def transpose_probs(i, u):
                base = 0 if i is None else UNITS * i
                if i is None:
                    pe.wait_ge(s_exp, u + 1)
                for c in range(TB):
                    mm = pe.transpose(pt_bank[u % 2][:, c * P:(c + 1) * P], prob[:, u % 2, c * P:(c + 1) * P], ident[:])
                mm.then_inc(s_pt, 1)

            def weigh_values(i, u):
                s, q = u // TB, u % TB
                pe.wait_ge(s_ptc, UNITS * i + u + 1)
                if q == 0 and s > 0:
                    pe.wait_ge(s_norm, IT_HEADS * i + s)
                for c in range(TB):
                    mm = pe.matmul(out_bank[s % 2][:, q * KL:(q + 1) * KL], probT[:, u % 2, c * P:(c + 1) * P],
                                   ckv[:, bass.ds(it_batch(i) * TB + c, 1), :].rearrange("p a n -> p (a n)"),
                                   start=(c == 0), stop=(c == TB - 1))
                mm.then_inc(s_pv, 1)

            pe.wait_ge(ab_ev, 2)
            pe.wait_ge(p_clo, NB)
            pe.wait_ge(mb_ev, NB)
            pe.wait_ge(wr_l, 1)
            pe.wait_ge(wr_h, 1)
            pe.wait_ge(ab_h, 1)
            pe.wait_ge(ab_l, 1)
            pe.wait_ge(zeroed, 2)
            for k, t in enumerate(AUX_FIRST):
                aux(None, k, t)
            for u in range(AHEAD):
                score(None, u)
            transpose_probs(None, 0)
            pe.wait_ge(ld_v, 48)
            for q in range(4):
                if q >= 2:
                    pe.wait_ge(m_ev, q - 1)
                for pr in range(2 * q, 2 * q + 2):
                    for s in range(2):
                        mm = pe.matmul(out_bank[q % 2][s * KL:(s + 1) * KL, (pr % 2) * D:(pr % 2 + 1) * D],
                                       wvup_s[:, 2 * pr + s, :], wout_s[:, 2 * pr + s, :], start=True, stop=True)
                mm.then_inc(m_mm, 1)
            pe.wait_ge(m_ev, 4)
            with pe.Fori(0, ITERS) as i:
                for u in range(UNITS):
                    score(i, u + AHEAD)
                    transpose_probs(i, u + 1)
                    weigh_values(i, u)
                    for k, t in AUX_K[u]:
                        aux(i, k, t)
            for k, t in enumerate(LAST):
                aux(ITERS, k, t)

            pe.wait_ge(s_x, 4 * ITERS + 4)
            pe.wait_ge(ld_f, 32)
            for b in range(NB):
                pe.wait_ge(f_h2, b + 1)
                for k in range(KD):
                    if b > 0:
                        pe.wait_ge(f_h2T, b)
                    for t in range(TB):
                        mm = pe.transpose(bank[k][:, t * P:(t + 1) * P], h2[:, b * TB + t, k * P:(k + 1) * P], ident[:])
                mm.then_inc(f_tr, 1)
                pe.wait_ge(f_h2T, b + 1)
                for t in range(TB):
                    for k in range(KD):
                        mm = pe.matmul(bank[2][:, (b * TB + t) * E:(b * TB + t + 1) * E], h2T[:, k, t * P:(t + 1) * P],
                                       gw_s[:, k, :], start=(k == 0), stop=(k == KD - 1))
                mm.then_inc(f_lg, 1)

            x_bank, h_bank, g_bank, y_bank = bank[0:2], bank[2:4], bank[4:6], bank[6:8]

            def inner_products(par, h_par, w_hi_e, w_lo_e):
                for k in range(KD):
                    tok = slice(k * P, (k + 1) * P)
                    mm = mm3(h_bank[h_par][:, 0:2 * FI], x_hl[:, par, 0, tok], x_hl[:, par, 1, tok],
                             w_hi_e(k), w_lo_e(k), k == 0, k == KD - 1)
                return mm

            def turn_gated(par):
                for c in range(2):
                    mm = pe.transpose(g_bank[par][0:FC, c * P:(c + 1) * P], g_s[:, par, c * FC:(c + 1) * FC], ident[:])
                return mm

            def shared_position(t, par):
                def inner(c):
                    if not within(t + 1, NT):
                        return
                    if c == 0:
                        pe.wait_ge(z_lo, t + 2)
                    if not (static(t) and t + 1 == 0):
                        pe.wait_ge(z_g, 2 * (t + 1) + c - 1)
                    inner_products((par + 1) % 2, c, lambda k: w_hi[:, E + c, k, :], lambda k: w_lo[:, E + c, k, :])\
                        .then_inc(z_h, 1)

                def turn(u, c):
                    if not within(u, NT):
                        return
                    pe.wait_ge(z_g, 2 * u + c + 1)
                    if not (static(u) and u == 0):
                        pe.wait_ge(z_gTc, 2 * u + c - 1)
                    turn_gated(c).then_inc(z_gt, 1)

                def outer(c):
                    if not within(t, NT):
                        return
                    pe.wait_ge(z_gTc, 2 * t + c + 1)
                    if c == 0 and not (static(t) and t < 2):
                        pe.wait_ge(z_zg, t - 1)
                    for h in range(2):
                        mm = pe.matmul(y_bank[par][:, 0:D], gT[:, c, h, :], w2_s[:, E + c, h, :],
                                       start=(c == 0 and h == 0), stop=(c == 1 and h == 1))
                    if c == 1:
                        mm.then_inc(z_y, 1)

                if within(t + 2, NT):
                    pe.wait_ge(z_now, t + 3)
                    if not (static(t) and t < 0):
                        pe.wait_ge(z_lo, t + 1)
                    for k in range(KD):
                        mm = pe.transpose(x_bank[par][:, k * P:(k + 1) * P], x_now[:, k * P:(k + 1) * P], ident[:])
                    mm.then_inc(z_x, 1)
                inner(0)
                turn(t, 1)
                outer(0)
                inner(1)
                turn(t + 1, 0)
                outer(1)

            pe.wait_ge(f_sg, NB)
            pe.wait_ge(f_lg, NB)
            pe.wait_ge(w_h, 1)
            pe.wait_ge(w_l, 1)
            for t in range(-2, -1):
                shared_position(t, t % 2)
            pe.wait_ge(masked, 1)
            pe.matmul(bank[6][:, 0:NT * E], tri_s, above[:].rearrange("p t e -> p (t e)"), start=True, stop=True)
            pe.matmul(bank[6][:, NT * E:], ones[:], above[:].rearrange("p t e -> p (t e)"), start=True, stop=True)\
                .then_inc(counted, 1)
            pe.wait_ge(indexed, 1)
            pe.wait_ge(ld_ws2, 16)
            for t in range(-1, Z_LOOP.start):
                shared_position(t, t % 2)
            with pe.Fori(0, len(Z_LOOP) // 2) as i:
                for j in range(2):
                    shared_position(i * 2 + (Z_LOOP.start + j), j)
            for t in range(Z_LOOP.stop, NT):
                shared_position(t, t % 2)

            pe.wait_ge(listed, 1)
            pe.wait_ge(w_h, 1 + E)
            pe.wait_ge(w_l, 1 + E)
            pe.wait_ge(ld_w2, 16)

            def expert_numbers(first, count):
                return nc.values_load_multi_w_load_instructions(
                    own_i[0:1, bass.ds(first, count)], engines=(mybir.EngineType.PE,), min_val=0, max_val=E - 1)[1]

            def expert_position(n, j, experts):
                at = (lambda d: n + d) if static(n) and n < E_LOOP.start else (lambda d: j + d)
                if within(n + 3, SLOT_TILES):
                    m, jm = n + 3, (j + 3) % CYCLE
                    pe.wait_ge(ld_s[jm], 16 * (over(m, CYCLE) + 1))
                    if static(m) and m < 2:
                        pe.wait_ge(z_lo, NT)
                    else:
                        pe.wait_ge(e_lo, m - 1)
                    for k in range(KD):
                        mm = pe.transpose(x_bank[jm % 2][:, k * P:(k + 1) * P], xs[:, jm, k * P:(k + 1) * P], ident[:])
                    mm.then_inc(e_x, 1)
                if within(n + 2, SLOT_TILES):
                    m, par = n + 2, j % 2
                    expert = experts[at(2)]
                    pe.wait_ge(e_lo, m + 1)
                    if static(m) and m < 2:
                        pe.wait_ge(z_g, 2 * NT)
                    else:
                        pe.wait_ge(e_g, m - 1)
                    inner_products(par, par, lambda k: w_hi[:, bass.ds(expert, 1), k, :].rearrange("p a n -> p (a n)"),
                                   lambda k: w_lo[:, bass.ds(expert, 1), k, :].rearrange("p a n -> p (a n)")).then_inc(e_h, 1)
                if within(n + 1, SLOT_TILES):
                    m, par = n + 1, (j + 1) % 2
                    pe.wait_ge(e_g, m + 1)
                    if static(m) and m < 2:
                        pe.wait_ge(z_gTc, 2 * NT)
                    else:
                        pe.wait_ge(e_gTc, m - 1)
                    turn_gated(par).then_inc(e_gt, 1)
                if within(n, SLOT_TILES):
                    expert = experts[at(0)]
                    pe.wait_ge(e_gTc, n + 1)
                    if static(n) and n < 2:
                        pe.wait_ge(z_zg, NT)
                    else:
                        pe.wait_ge(e_yc, n - 1)
                    for h in range(2):
                        mm = pe.matmul(y_bank[j % 2][:, 0:D], gT[:, j % 2, h, :],
                                       w2_s[:, bass.ds(expert, 1), h, :].rearrange("p a n -> p (a n)"),
                                       start=(h == 0), stop=(h == 1))
                    mm.then_inc(e_y, 1)

            expert_steps(pe, expert_position, expert_numbers)

        @block.vector
        def _(dve):
            own = [0]

            def chain(ins):
                own[0] += 1
                ins.then_inc(dve_c, 1)
                dve.wait_ge(dve_c, own[0])

            dve.wait_ge(c_exp, 1)
            chain(dve.tensor_scalar(crec[:], cexp[:], 1.0, None, ALU.add))
            chain(dve.reciprocal(cexp[:], crec[:]))
            dve.tensor_tensor(csil[:], cT_s[:], cexp[:], ALU.mult).then_inc(c_sil, 1)

            def statistics(half):
                for b in (2 * half, 2 * half + 1):
                    dve.wait_ge(ld_x[b], 16)
                    for t in range(b * TB, (b + 1) * TB):
                        ins = dve.bn_stats(bst[:, t, :], xa[:, TB + t, :])
                chain(ins)
                for t in range(2 * half * TB, 2 * (half + 1) * TB):
                    ins = dve.bn_aggr(mv[:, t, :], bst[:, t, :])
                ins.then_inc(p_stat, 1)

            def centre(b):
                if b % 2 == 0:
                    dve.wait_ge(p_rstd, b // 2 + 1)
                if b >= 2:
                    dve.wait_ge(p_tr, KD * (b - 1))
                for t in range(b * TB, (b + 1) * TB):
                    ins = dve.tensor_scalar(xn[:, b % 2, t % TB, :], xa[:, TB + t, :], mv[:, t, 0:1],
                                            rstd[:, b // 2, t % (2 * TB):t % (2 * TB) + 1], ALU.subtract, ALU.mult)
                ins.then_inc(p_xn, 1)

            def modulate(b):
                if b > 0:
                    dve.wait_ge(p_hhi, b)
                    dve.wait_ge(p_hlo, b)
                    dve.wait_ge(p_dn, b)
                for k in range(KD):
                    dve.wait_ge(p_tr, KD * b + k + 1)
                    dve.tensor_scalar(h_f[:, k, :], aux_bank[k][:], modT[:, 1, k, b:b + 1], modT[:, 0, k, b:b + 1],
                                      ALU.mult, ALU.add).then_inc(p_h, 1)

            def latents(b):
                dve.wait_ge(p_dn, b + 1)
                dve.tensor_copy(dn[:, b * TB:(b + 1) * TB, :],
                                out_bank[b % 2][:].rearrange("p (t n) -> p t n", t=TB)[:, :, 0:QL + KL]).then_inc(p_dnev, 1)

            def squares(half):
                t = slice(half * 2 * TB, (half + 1) * 2 * TB)
                dve.wait_ge(p_dnev, 2 * half + 2)
                chain(dve.tensor_tensor(dsq[:, t, :], dn[:, t, :], dn[:, t, :], ALU.mult))
                dve.tensor_reduce(ssq[:, half, 0, :], dsq[:, t, 0:QL], AX_X, ALU.add)
                dve.tensor_reduce(ssq[:, half, 1, :], dsq[:, t, QL:], AX_X, ALU.add).then_inc(p_ssq, 1)

            def norm_latents(half):
                t = slice(half * 2 * TB, (half + 1) * 2 * TB)
                dve.wait_ge(p_rms, half + 1)
                dve.tensor_tensor(ckv[:, t, :], dn[:, t, QL:],
                                  rms[:, half, 1, :].unsqueeze(2).to_broadcast([P, 2 * TB, KL]), ALU.mult)
                dve.tensor_tensor(ncq[:, t, :], dn[:, t, 0:QL],
                                  rms[:, half, 0, :].unsqueeze(2).to_broadcast([P, 2 * TB, QL]), ALU.mult).then_inc(p_ncq, 1)

            def split_latents(b):
                dve.wait_ge(p_chi, b + 1)
                if b > 0:
                    dve.wait_ge(p_cst, 16 * b)
                dve.tensor_tensor(cq_hl[:, 1, :], pt_bank[b % 2][0:QL, :], cq_hl[:, 0, :].bitcast(F32),
                                  ALU.subtract).then_inc(p_clo, 1)

            statistics(0)
            dve.wait_ge(mod_mm, 1)
            m2 = aux_bank[0][:, 0:2 * KD * NB].rearrange("p (w c b) -> p w c b", w=2, c=KD)
            for w in range(2):
                ins = dve.tensor_scalar(modT[:, w], m2[:, w], float(w), None, ALU.add)
            ins.then_inc(mod_ev, 1)
            dve.wait_ge(mod_ev, 1)
            centre(0)
            centre(1)
            modulate(0)
            statistics(1)
            latents(0)
            modulate(1)
            latents(1)
            squares(0)
            centre(2)
            modulate(2)
            centre(3)
            norm_latents(0)
            latents(2)
            modulate(3)
            split_latents(0)
            latents(3)
            squares(1)
            dve.wait_ge(c_sil, 1)
            dve.tensor_copy(csil_bc[:].rearrange("p k b n -> p (k b) n"), csil[:].rearrange("p k b -> p (k b)")
                            .unsqueeze(2).to_broadcast([P, KD * NB, P])).then_inc(c_sil, 1)
            split_latents(1)
            dve.wait_ge(wr_h, 1)
            dve.tensor_tensor(wr_lo[:].rearrange("p k g n -> p (k g n)"), wr_raw,
                              wr_hi[:].bitcast(F32).rearrange("p k g n -> p (k g n)"), ALU.subtract).then_inc(wr_l, 1)
            norm_latents(1)
            dve.wait_ge(ld_c, 16 * 4)
            chain(dve.tensor_scalar(qnw_sc[:], qnw_s[:], SCALE, None, ALU.mult))
            for z in range(2):
                dve.wait_ge(ab_mm, z + 1)
                dve.scalar_tensor_tensor(
                    out=ab_f[:, z * 512:(z + 1) * 512].rearrange("p (h c) -> p h c", h=8),
                    in0=out_bank[z][0:QL, :].rearrange("p (h c) -> p h c", h=8), scalar=qnw_sc[:, 0:1],
                    in1=kvwb_s[:].unsqueeze(1).to_broadcast([QL, 8, KL]), op0=ALU.mult, op1=ALU.mult).then_inc(ab_ev, 1)
            dve.wait_ge(ab_h, 1)
            dve.tensor_tensor(ab_lo[0:QL], ab_f[:], ab_hi[0:QL].bitcast(F32), ALU.subtract).then_inc(ab_l, 1)
            split_latents(2)
            split_latents(3)
            for b in range(NB):
                dve.wait_ge(g_mm, b + 1)
                dve.tensor_copy(gate[:, b + 1].rearrange("p w n -> p (w n)"), score_bank[b % 2][:]).then_inc(g_ev, 1)
            for b in range(NB):
                dve.wait_ge(mb_mm, b + 1)
                if b >= 2:
                    dve.wait_ge(mb_st[b % 2], 16)
                dve.tensor_copy(mod_o[:, b % 2, 0], score_bank[b % 2][:, 0:D])
                dve.tensor_scalar(mod_o[:, b % 2, 1], score_bank[b % 2][:, D:], 1.0, None, ALU.add).then_inc(mb_ev, 1)

            def set_gates():
                dve.wait_ge(g_ev, NB)
                dve.wait_ge(p_hhi, NB)
                dve.wait_ge(p_hlo, NB)
                for b in range(NB):
                    g = gate[:, b + 1].rearrange("p w n -> p (w n)")
                    dve.tensor_scalar(gsgn, g, 0.0, 0.5, ALU.is_ge, ALU.subtract)
                    chain(dve.scalar_tensor_tensor(out=gabs, in0=g, scalar=-1.0, in1=g, op0=ALU.mult, op1=ALU.max))
                    chain(dve.tensor_scalar(gabs, gabs, 0.25, 2.0, ALU.max, ALU.mult))
                    chain(dve.tensor_tensor(g, gabs, gsgn, ALU.mult))

            def value_weights():
                for q in range(4):
                    dve.wait_ge(m_mm, q + 1)
                    dve.tensor_scalar(mout[:, 2 * q:2 * q + 2, :], out_bank[q % 2][:].rearrange("p (a n) -> p a n", a=2),
                                      kvw2_s[:, 0:1], None, ALU.mult).then_inc(m_ev, 1)

            set_gates()
            dve.memset(o_tok[:, 1], 0.0).then_inc(s_norm, 1)

            def aux(i, k, t):
                src = aux_home(i, k)
                if t[0] == "pr":
                    _, par, n = t
                    dve.wait_ge(aux_done, aux_count(i, k))
                    if not (i is None and n < 2):
                        dve.wait_ge(s_rope, pr_count(i, par, n) - 1)
                    for dst, w in ((t_cos, 0), (t_sin, 1)):
                        ins = dve.tensor_tensor(dst[:, n % 2].rearrange("p (a h) c -> p a h c", a=2),
                                                src[:].rearrange("p (a h c) -> p a h c", a=2, h=GH),
                                                rope[:, n, w].unsqueeze(2).to_broadcast([P, 2, GH, RD]), ALU.mult)
                    ins.then_inc(s_sin, 1)
                elif t[0] in ("tq", "tk"):
                    s, n = t[1], (0 if i is None else 2 * IT_HEADS * i) + 2 * t[1] + (1 if t[0] == "tq" else 2)
                    dve.wait_ge(s_qk, n)
                    hl = (qT if t[0] == "tq" else kT)[:, s % 2]
                    dve.tensor_tensor(hl[:, 1, :], src[:], hl[:, 0, :].bitcast(F32), ALU.subtract).then_inc(s_ql, 1)
                elif t[0] == "ab":
                    _, par, n = t
                    dve.wait_ge(aux_done, aux_count(i, k))
                    dve.tensor_copy(qk_tok[:, par, n, 0, :, RD:], src[:, 0:GH * KL]
                                    .rearrange("p (h c) -> p h c", h=GH)).then_inc(s_ab, 1)
                elif t[0] == "op":
                    _, par, n = t
                    dve.wait_ge(aux_done, aux_count(i, k))
                    dve.wait_ge(s_x, 4 * i + (0 if par else 2) + n + 1)
                    dve.tensor_tensor(y_gate[:, n], src[:].rearrange("p (q n) -> p q n", q=2),
                                      gate[:, bass.ds(out_slot(i, par), 1), 0, :].to_broadcast([P, 2, D]),
                                      ALU.mult).then_inc(s_yg, 1)

            def row_max(i, u):
                dve.wait_ge(s_score, (0 if i is None else UNITS * i) + u + 1)
                dve.tensor_reduce(nmax[:, u % 4:u % 4 + 1], score_bank[u % 2][:], AX_X, ALU.max, negate=True)\
                    .then_inc(s_max, 1)

            def normalise(i, s):
                dve.wait_ge(s_pv, UNITS * i + TB * (s + 1))
                dve.reciprocal(rinv[:, s % 2, :], rsum[:, s % 2, :]).then_inc(s_rinv, 1)
                dve.wait_ge(s_rinv, IT_HEADS * i + s + 1)
                hh = s % GH
                dve.tensor_tensor(o_tok[:, s // GH, :, hh * KL:(hh + 1) * KL],
                                  out_bank[s % 2][:, 0:TB * KL].rearrange("p (q c) -> p q c", q=TB),
                                  rinv[:, s % 2, :].unsqueeze(2).to_broadcast([P, TB, KL]), ALU.mult).then_inc(s_norm, 1)

            for k, t in enumerate(AUX_FIRST):
                aux(None, k, t)
            for u in range(AHEAD):
                row_max(None, u)
            value_weights()
            for q in mb_st:
                dve.wait_ge(q, 32)
            with dve.Fori(0, ITERS) as i:
                for u in range(UNITS):
                    row_max(i, u + AHEAD)
                    for k, t in AUX_K[u]:
                        aux(i, k, t)
                    if u % TB == TB - 1:
                        normalise(i, u // TB)
            for k, t in enumerate(LAST):
                aux(ITERS, k, t)

            dve.wait_ge(s_x, 4 * ITERS + 4)
            dve.wait_ge(s_norm, IT_HEADS * ITERS + 1)
            for b in range(NB):
                xb = TB * (b + 1)
                for t in range(TB):
                    ins = dve.bn_stats(bst2[:, t, :], xa[:, xb + t, :])
                chain(ins)
                if b > 0:
                    dve.wait_ge(f_rstd, b)
                for t in range(TB):
                    ins = dve.bn_aggr(mv2[:, t, :], bst2[:, t, :])
                ins.then_inc(f_stat, 1)
                dve.wait_ge(f_rstd, b + 1)
                dve.wait_ge(mb_ld[b % 2], 16 * (b // 2 + 1))
                rows = h2[:, b * TB:(b + 1) * TB, 0:D]
                for t in range(TB):
                    ins = dve.tensor_scalar(h2[:, b * TB + t, 0:D], xa[:, xb + t, :], mv2[:, t, 0:1], rstd2[:, t:t + 1],
                                            ALU.subtract, ALU.mult)
                chain(ins)
                chain(dve.tensor_tensor(rows, rows, modb[:, b % 2, 1:2, :].to_broadcast([P, TB, D]), ALU.mult))
                dve.tensor_tensor(rows, rows, modb[:, b % 2, 0:1, :].to_broadcast([P, TB, D]), ALU.add).then_inc(f_h2, 1)
            dve.wait_ge(w_h, 1)
            dve.tensor_tensor(w_lo[:, E:], w_raw[:, E:], w_hi[:, E:].bitcast(F32), ALU.subtract).then_inc(w_l, 1)

            dve.wait_ge(f_sg, NB)
            chain(dve.tensor_scalar(sg[:], sg[:], 1.0, None, ALU.add))
            chain(dve.reciprocal(sg[:], sg[:]))
            chain(dve.tensor_reduce(gm[:], sg[:].rearrange("p t (g e) -> p t g e", g=EG), AX_X, ALU.max))
            rival = gm[:].unsqueeze(2).to_broadcast([P, NT, EG, EG])
            me = gm[:].unsqueeze(3).to_broadcast([P, NT, EG, EG])
            dve.tensor_tensor(gtm, rival, me, ALU.is_gt)
            chain(dve.tensor_tensor(gem, rival, me, ALU.is_equal))
            chain(dve.tensor_tensor(gem.rearrange("p t a b -> p t (a b)"), gem.rearrange("p t a b -> p t (a b)"),
                                    early_s[:].rearrange("p a b -> p (a b)").unsqueeze(1).to_broadcast([P, NT, EG * EG]),
                                    ALU.mult))
            chain(dve.tensor_tensor(gtm, gtm, gem, ALU.add))
            chain(dve.tensor_reduce(gsel[:], gtm, AX_X, ALU.add))
            chain(dve.tensor_scalar(gsel[:], gsel[:], float(TOPG), None, ALU.is_lt))
            chain(dve.tensor_tensor(msk[:].rearrange("p t (g e) -> p (t g) e", g=EG), sg[:].rearrange("p t (g e) -> p (t g) e", g=EG),
                                    gsel[:].rearrange("p t g -> p (t g)").unsqueeze(2).to_broadcast([P, NT * EG, E // EG]),
                                    ALU.mult))
            for t in range(NT):
                ins = dve.max(top[:, t, :], msk[:, t, :])
            chain(ins)
            least = top[:, :, TOPK - 1:TOPK].to_broadcast([P, NT, E])
            dve.tensor_tensor(above[:], msk[:], least, ALU.is_gt)
            chain(dve.tensor_tensor(equal[:], msk[:], least, ALU.is_equal))
            chain(dve.tensor_reduce(quota[:], above[:], AX_X, ALU.add))
            chain(dve.tensor_scalar(quota[:], quota[:], -1.0, float(TOPK), ALU.mult, ALU.add))
            src, n, step = equal[:], 0, 1
            while step < E:
                dst = pre[:, n % 2]
                dve.tensor_copy(dst[:, :, 0:step], src[:, :, 0:step])
                chain(dve.tensor_tensor(dst[:, :, step:], src[:, :, step:], src[:, :, 0:E - step], ALU.add))
                src, n, step = dst, n + 1, 2 * step
            chain(dve.tensor_tensor(src, src, quota[:].unsqueeze(2).to_broadcast([P, NT, E]), ALU.is_le))
            chain(dve.tensor_tensor(src, src, equal[:], ALU.mult))
            chain(dve.tensor_tensor(above[:], src, above[:], ALU.add))
            chosen = above[:]
            dve.memset(ones[:], 1.0).then_inc(masked, 1)
            weights = h2[:, :, X_W:X_W + E]
            chain(dve.tensor_tensor(equal[:], chosen, sg[:], ALU.mult))
            chain(dve.tensor_reduce(den[:], equal[:], AX_X, ALU.add))
            chain(dve.reciprocal(den[:], den[:]))
            dve.tensor_tensor(weights, equal[:], den[:].unsqueeze(2).to_broadcast([P, NT, E]), ALU.mult)
            src, n, step = chosen, 0, 1
            while step < E:
                dst = pre[:, n % 2]
                dve.tensor_copy(dst[:, :, 0:step], src[:, :, 0:step])
                chain(dve.tensor_tensor(dst[:, :, step:], src[:, :, step:], src[:, :, 0:E - step], ALU.add))
                src, n, step = dst, n + 1, 2 * step
            chain(dve.tensor_tensor(msk[:], src, chosen, ALU.mult))
            chain(dve.tensor_scalar(msk[:], msk[:], -1.0, None, ALU.add))
            rank = msk[:]
            dve.tensor_tensor(h2[:, :, X_DEST:], rank, token_s.unsqueeze(2).to_broadcast([P, NT, E]), ALU.add).then_inc(extended, 1)
            dve.wait_ge(counted, 1)
            within_tile = bank[6][:, 0:NT * E].rearrange("p (t e) -> p t e", t=NT)
            in_tile = bank[6][:, NT * E:].rearrange("p (t e) -> p t e", t=NT)
            dve.memset(pre[:, 0, 0:1, :], 0.0)
            chain(dve.tensor_copy(pre[:, 0, 1:, :], in_tile[:, 0:NT - 1, :]))
            src, n, step = pre[:, 0], 1, 1
            while step < NT:
                dst = pre[:, n % 2]
                dve.tensor_copy(dst[:, 0:step, :], src[:, 0:step, :])
                chain(dve.tensor_tensor(dst[:, step:, :], src[:, step:, :], src[:, 0:NT - step, :], ALU.add))
                src, n, step = dst, n + 1, 2 * step
            before, other = src, pre[:, n % 2]
            chain(dve.tensor_tensor(loads[:].unsqueeze(1), before[:, NT - 1:NT, :], in_tile[:, NT - 1:NT, :], ALU.add))
            chain(dve.tensor_tensor(other, loads[:].unsqueeze(2).to_broadcast([P, E, NT]),
                                    full_s.unsqueeze(1).to_broadcast([P, E, NT]), ALU.is_gt))
            dve.memset(tiles_of[:, 0, 0:1], 0.0)
            chain(dve.tensor_reduce(tiles_of[:, 0, 1:], other, AX_X, ALU.add))
            n, step = 0, 1
            while step < E:
                a, z = tiles_of[:, n % 2], tiles_of[:, (n + 1) % 2]
                dve.tensor_copy(z[:, 0:step], a[:, 0:step])
                chain(dve.tensor_tensor(z[:, step:], a[:, step:], a[:, 0:E + 1 - step], ALU.add))
                n, step = n + 1, 2 * step
            first_tile = tiles_of[:, n % 2]
            scaled = tiles_of[:, (n + 1) % 2]
            chain(dve.tensor_scalar(scaled, first_tile, float(P), None, ALU.mult))
            chain(dve.tensor_tensor(other, before, within_tile, ALU.add))
            chain(dve.tensor_tensor(other, other, scaled[:, 0:E].unsqueeze(1).to_broadcast([P, NT, E]), ALU.add))
            for r in range(TOPK):
                ins = dve.scalar_tensor_tensor(out=picked[:, :, r, :], in0=rank, scalar=float(r), in1=other,
                                               op0=ALU.is_equal, op1=ALU.mult)
            chain(ins)
            chain(dve.tensor_reduce(slot_f[:], picked, AX_X, ALU.add))
            dve.tensor_copy(slot_i[:], slot_f[:]).then_inc(indexed, 1)
            chain(dve.memset(first_tile[:, E:], float(2 * SLOT_TILES)))
            half = SLOT_TILES // 2
            for z in range(2):
                part = slice(z * half, (z + 1) * half)
                chain(dve.tensor_tensor(started, first_tile.unsqueeze(1).to_broadcast([P, half, E + 1]),
                                        tile_s[:, part].unsqueeze(2).to_broadcast([P, half, E + 1]), ALU.is_le))
                dve.tensor_tensor(owner[:, part, :], started[:, :, 0:E], started[:, :, 1:], ALU.subtract)
                chain(dve.tensor_reduce(own_f[:, part], started[:, :, 0:E], AX_X, ALU.add))
            dve.tensor_scalar(own_i[:], own_f[:], -1.0, None, ALU.add).then_inc(listed, 1)

            x_bank, h_bank, g_bank, y_bank = bank[0:2], bank[2:4], bank[4:6], bank[6:8]

            def what_rounding_leaves(par, hi_done, x_lo_done):
                dve.tensor_tensor(x_hl[:, par, 1, :], x_bank[par][:, 0:D], x_hl[:, par, 0, :].bitcast(F32),
                                  ALU.subtract).then_inc(x_lo_done, 1)

            def shared_position(t, par):
                if within(t + 2, NT):
                    dve.wait_ge(z_hi, t + 3)
                    if not (static(t) and t < 0):
                        dve.wait_ge(z_h, 2 * (t + 1))
                    dve.tensor_tensor(x_hl[:, par, 1, :], x_bank[par][:, 0:D], x_hl[:, par, 0, :].bitcast(F32),
                                      ALU.subtract).then_inc(z_lo, 1)

                def gate_half(c):
                    if not within(t + 1, NT):
                        return
                    dve.wait_ge(z_sl, 2 * (t + 1) + c + 1)
                    if not (static(t) and t + 1 == 0):
                        dve.wait_ge(z_gt, 2 * (t + 1) + c - 1)
                    dve.tensor_tensor(g_s[:, c, :], h_bank[c][:, FI:2 * FI], sl[:, c, :], ALU.mult).then_inc(z_g, 1)

                def copy_turned(u, c):
                    if not within(u, NT):
                        return
                    dve.wait_ge(z_gt, 2 * u + c + 1)
                    if c == 0:
                        pass
                    dve.tensor_copy(gT[:, c].rearrange("p c t -> p (c t)"), g_bank[c][0:FC, 0:2 * P]).then_inc(z_gTc, 1)

                gate_half(0)
                copy_turned(t, 1)
                gate_half(1)
                copy_turned(t + 1, 0)
                if within(t, NT):
                    dve.wait_ge(z_y, t + 1)
                    slot = t // TB + 1
                    g2 = gate[:, slot, 1, :] if static(t) else gate[:, bass.ds(slot, 1), 1, :].rearrange("p a n -> p (a n)")
                    dve.tensor_tensor(zg, y_bank[par][:, 0:D], g2, ALU.mult).then_inc(z_zg, 1)
                    dve.wait_ge(w_h, t + 2)
                    dve.tensor_tensor(w_lo[:, bass.ds(t, 1)].rearrange("p a k n -> p (a k n)"),
                                      w_raw[:, bass.ds(t, 1)].rearrange("p a k n -> p (a k n)"),
                                      w_hi[:, bass.ds(t, 1)].bitcast(F32).rearrange("p a k n -> p (a k n)"),
                                      ALU.subtract).then_inc(w_l, 1)
                    dve.wait_ge(z_zg, t + 1)
                    row = xa[:, bass.ds(t + TB, 1), :].rearrange("p a n -> p (a n)")
                    dve.tensor_tensor(row, row, zg, ALU.add).then_inc(z_out, 1)

            shared_steps(dve, shared_position)

            def expert_position(n, j):
                if within(n + 3, SLOT_TILES):
                    m, jm = n + 3, (j + 3) % CYCLE
                    dve.wait_ge(ld_s[jm], 16 * (over(m, CYCLE) + 1))
                    dve.tensor_tensor(chosen_by[:, jm], xs[:, jm, X_W:].rearrange("p (a e) -> p a e", a=2),
                                      owner[:, bass.ds(m, 1), :].to_broadcast([P, 2, E]), ALU.mult).then_inc(e_mul, 1)
                    dve.wait_ge(e_hi, m + 1)
                    if not (static(m) and m < 2):
                        dve.wait_ge(e_h, m - 1)
                    dve.tensor_tensor(x_hl[:, jm % 2, 1, :], x_bank[jm % 2][:, 0:D], x_hl[:, jm % 2, 0, :].bitcast(F32),
                                      ALU.subtract).then_inc(e_lo, 1)
                    dve.wait_ge(e_mul, m + 1)
                    dve.tensor_reduce(sel[:, jm], chosen_by[:, jm], AX_X, ALU.add).then_inc(e_sel, 1)
                if within(n + 2, SLOT_TILES):
                    m, jm, par = n + 2, (j + 2) % CYCLE, j % 2
                    dve.wait_ge(e_sl, m + 1)
                    if static(m) and m < 2:
                        dve.wait_ge(z_gt, 2 * NT)
                    else:
                        dve.wait_ge(e_gt, m - 1)
                    dve.wait_ge(e_sel, m + 1)
                    dve.scalar_tensor_tensor(out=g_s[:, par, :], in0=h_bank[par][:, FI:2 * FI], scalar=sel[:, jm, 0:1],
                                             in1=sl[:, par, :], op0=ALU.mult, op1=ALU.mult).then_inc(e_g, 1)
                    if not (static(m) and m < CYCLE):
                        dve.wait_ge(e_put[jm], 16 * over(m, CYCLE))
                    dve.tensor_copy(sel_i[:, jm:jm + 1], sel[:, jm, 1:2]).then_inc(e_idx, 1)
                if within(n + 1, SLOT_TILES):
                    m, par = n + 1, (j + 1) % 2
                    dve.wait_ge(e_gt, m + 1)
                    if not (static(m) and m < 2):
                        dve.wait_ge(e_y, m - 1)
                    dve.tensor_copy(gT[:, par].rearrange("p c t -> p (c t)"), g_bank[par][0:FC, 0:2 * P]).then_inc(e_gTc, 1)

            expert_steps(dve, expert_position)

            for t in range(NT):
                dve.wait_ge(ld_y[t % 4], 16 * (t // 4 + 1))
                if t >= 2:
                    dve.wait_ge(y_gat, t - 1)
                dve.tensor_reduce(ysum[:, t % 2], yb[:, t % 4].rearrange("p (r d) -> p d r", r=TOPK), AX_X, ALU.add)\
                    .then_inc(y_sum, 1)
                dve.wait_ge(y_sum, t + 1)
                if t >= 2:
                    dve.wait_ge(y_add, t - 1)
                dve.tensor_tensor(ygate[:, t % 2], ysum[:, t % 2], gate[:, t // TB + 1, 1, :], ALU.mult).then_inc(y_gat, 1)

        @block.scalar
        def _(act):
            act.wait_ge(ld_a, 48)
            act.activation(cexp[:], cT_s[:], ACT.Exp, scale=-1.0).then_inc(c_exp, 1)
            def split_latents(b):
                act.wait_ge(p_ctr, b + 1)
                if b > 0:
                    act.wait_ge(p_cst, 16 * b)
                act.activation(cq_hl[:, 0], pt_bank[b % 2][0:QL, :], ACT.Copy).then_inc(p_chi, 1)

            for b in range(NB):
                act.wait_ge(p_h, KD * (b + 1))
                if b > 0:
                    act.wait_ge(p_st, 16 * b)
                act.activation(h_hl[:, 0], h_f[:], ACT.Copy).then_inc(p_hhi, 1)
            act.wait_ge(p_st, 16 * NB)
            split_latents(0)
            act.wait_ge(ld_b, 32)
            act.activation(wr_hi[:].rearrange("p k g n -> p (k g n)"), wr_raw, ACT.Copy).then_inc(wr_h, 1)
            split_latents(1)
            act.wait_ge(zeroed, 2)
            act.wait_ge(ab_ev, 2)
            act.activation(ab_hi[0:QL], ab_f[:], ACT.Copy).then_inc(ab_h, 1)
            split_latents(2)
            split_latents(3)

            def aux(i, k, t):
                if t[0] in ("tq", "tk"):
                    s = t[1]
                    act.wait_ge(aux_done, aux_count(i, k))
                    act.activation((qT if t[0] == "tq" else kT)[:, s % 2, 0, :], aux_home(i, k)[:], ACT.Copy).then_inc(s_qk, 1)
                elif t[0] == "ot":
                    act.wait_ge(aux_done, aux_count(i, k))
                    act.activation(oT[:, t[1], t[2], :], aux_home(i, k)[:], ACT.Copy).then_inc(s_ot, 1)

            def copy_probs(i, u):
                act.wait_ge(s_pt, (0 if i is None else UNITS * i) + u + 1)
                act.activation(probT[:, u % 2, :], pt_bank[u % 2][:], ACT.Copy).then_inc(s_ptc, 1)

            def exponentials(i, u):
                act.wait_ge(s_max, (0 if i is None else UNITS * i) + u + 1)
                s, q = (u // TB) % 2, u % TB
                act.activation(prob[:, u % 2, :], score_bank[u % 2][:], ACT.Exp, bias=nmax[:, u % 4:u % 4 + 1],
                               accum_out=rsum[:, s, q:q + 1]).then_inc(s_exp, 1)

            for k, t in enumerate(AUX_FIRST):
                aux(None, k, t)
            for u in range(2):
                exponentials(None, u)
            for q in mb_st:
                act.wait_ge(q, 32)
            copy_probs(None, 0)
            exponentials(None, 2)
            with act.Fori(0, ITERS) as i:
                for u in range(UNITS):
                    copy_probs(i, u + 1)
                    exponentials(i, u + AHEAD)
                    for k, t in AUX_K[u]:
                        aux(i, k, t)
            for k, t in enumerate(LAST):
                aux(ITERS, k, t)

            for b in range(NB):
                act.wait_ge(f_tr, b + 1)
                if b > 0:
                    act.wait_ge(f_lg, b)
                for k in range(KD):
                    ins = act.activation(h2T[:, k, :], bank[k][:], ACT.Copy)
                ins.then_inc(f_h2T, 1)
                act.wait_ge(f_lg, b + 1)
                act.activation(sg[:, b * TB:(b + 1) * TB, :], bank[2][:, b * TB * E:(b + 1) * TB * E]
                               .rearrange("p (t e) -> p t e", t=TB), ACT.Exp, scale=-1.0).then_inc(f_sg, 1)
            act.wait_ge(ld_ws, 16)
            act.activation(w_hi[:, E:], w_raw[:, E:], ACT.Copy).then_inc(w_h, 1)

            x_bank, h_bank, g_bank, y_bank = bank[0:2], bank[2:4], bank[4:6], bank[6:8]

            act.wait_ge(f_h2, NB)

            def fetch(t):
                act.activation(x_now[:], h2[:, bass.ds(t, 1), 0:D].rearrange("p a n -> p (a n)"), ACT.Copy).then_inc(z_now, 1)

            fetch(0)

            def shared_position(t, par):
                if within(t + 2, NT):
                    act.wait_ge(z_x, t + 3)
                    if not (static(t) and t < 0):
                        act.wait_ge(z_h, 2 * (t + 1))
                    act.activation(x_hl[:, par, 0, :], x_bank[par][:, 0:D], ACT.Copy).then_inc(z_hi, 1)
                if within(t + 3, NT):
                    fetch(t + 3)
                if within(t + 1, NT):
                    for c in range(2):
                        act.wait_ge(z_h, 2 * (t + 1) + c + 1)
                        if not (static(t) and t + 1 == 0):
                            act.wait_ge(z_g, 2 * (t + 1) + c - 1)
                        act.activation(sl[:, c, :], h_bank[c][:, 0:FI], ACT.Silu).then_inc(z_sl, 1)
                if within(t, NT):
                    if static(t) and t == 0:
                        act.wait_ge(ld_w, 64)
                    act.activation(w_hi[:, bass.ds(t, 1)].rearrange("p a k n -> p (a k n)"),
                                   w_raw[:, bass.ds(t, 1)].rearrange("p a k n -> p (a k n)"), ACT.Copy).then_inc(w_h, 1)

            shared_steps(act, shared_position)

            def expert_position(n, j):
                if within(n + 3, SLOT_TILES):
                    m, par = n + 3, (j + 3) % 2
                    act.wait_ge(e_x, m + 1)
                    if static(m) and m < 2:
                        act.wait_ge(z_h, 2 * NT)
                    else:
                        act.wait_ge(e_h, m - 1)
                    act.activation(x_hl[:, par, 0, :], x_bank[par][:, 0:D], ACT.Copy).then_inc(e_hi, 1)
                if within(n + 2, SLOT_TILES):
                    m, par = n + 2, j % 2
                    act.wait_ge(e_h, m + 1)
                    if static(m) and m < 2:
                        act.wait_ge(z_g, 2 * NT)
                    else:
                        act.wait_ge(e_g, m - 1)
                    act.activation(sl[:, par, :], h_bank[par][:, 0:FI], ACT.Silu).then_inc(e_sl, 1)
                if within(n, SLOT_TILES):
                    act.wait_ge(e_y, n + 1)
                    if not (static(n) and n < CYCLE):
                        act.wait_ge(e_put[j], 16 * over(n, CYCLE))
                    act.activation(ys[:, j], y_bank[j % 2][:, 0:D], ACT.Copy).then_inc(e_yc, 1)

            expert_steps(act, expert_position)

        @block.gpsimd
        def _(pool):
            own = [0]

            def chain(ins):
                own[0] += 1
                ins.then_inc(pool_c, 1)
                pool.wait_ge(pool_c, own[0])

            pool.memset(xa[:, 0:TB, :], 0.0).then_inc(s_x, 1)
            pool.memset(idle[:, 0:1], 0.0).then_inc(s_x, 1)
            pool.memset(pad[:, 0:X_W], 0.0).then_inc(pad_set, 1)
            pool.memset(pad[:, X_W:X_DEST], 0.0).then_inc(pad_set, 1)
            pool.memset(pad[:, X_DEST:], float(NOWHERE)).then_inc(pad_set, 1)
            pool.memset(gate[:, 0], 0.0).then_inc(zeroed, 1)
            chain(pool.memset(mhalf[:], -0.5))
            pool.memset(ab_hi[:].bitcast(F32), 0.0)
            pool.memset(ab_lo[:].bitcast(F32), 0.0)
            pool.memset(cq_st[:].bitcast(F32), 0.0).then_inc(zeroed, 1)
            def inverse_deviations(half):
                pool.wait_ge(p_stat, half + 1)
                chain(pool.tensor_scalar(ve[:, half, 0, :], mv[:, half * 2 * TB:(half + 1) * 2 * TB, 1], EPS_LN, None, ALU.add))
                pool.tensor_tensor(rstd[:, half], ve[:, half, 0, :], mhalf[:, 0:2 * TB], ALU.pow).then_inc(p_rstd, 1)

            def split_inputs(b):
                pool.wait_ge(p_hhi, b + 1)
                if b > 0:
                    pool.wait_ge(p_st, 16 * b)
                pool.tensor_tensor(h_hl[:, 1].rearrange("p k t -> p (k t)"), h_f[:].rearrange("p k t -> p (k t)"),
                                   h_hl[:, 0].bitcast(F32).rearrange("p k t -> p (k t)"), ALU.subtract).then_inc(p_hlo, 1)

            def inverse_norms(half):
                pool.wait_ge(p_ssq, half + 1)
                pool.tensor_scalar(ve[:, half, 1, :], ssq[:, half, 0, :], 1.0 / QL, EPS_RMS, ALU.mult, ALU.add)
                chain(pool.tensor_scalar(ve[:, half, 2, :], ssq[:, half, 1, :], 1.0 / KL, EPS_RMS, ALU.mult, ALU.add))
                pool.tensor_tensor(rms[:, half].rearrange("p a t -> p (a t)"), ve[:, half, 1:3, :].rearrange("p a t -> p (a t)"),
                                   mhalf[:], ALU.pow).then_inc(p_rms, 1)

            inverse_deviations(0)
            split_inputs(0)
            inverse_deviations(1)
            split_inputs(1)
            inverse_norms(0)
            split_inputs(2)
            split_inputs(3)
            inverse_norms(1)

            def aux(i, k, t):
                if t[0] == "pr":
                    _, par, n = t
                    pool.wait_ge(s_sin, pr_count(i, par, n) + 1)
                    dst = qk_tok[:, par, n].rearrange("p a h c -> p (a h) c")
                    half = RD // 2
                    pool.tensor_tensor(dst[:, :, 0:half], t_cos[:, n % 2, :, 0:half], t_sin[:, n % 2, :, half:],
                                       ALU.subtract)
                    pool.tensor_tensor(dst[:, :, half:RD], t_cos[:, n % 2, :, half:], t_sin[:, n % 2, :, 0:half],
                                       ALU.add).then_inc(s_rope, 1)
                    tile = n if i is None else prep_batch(i, par) * TB + n
                    pool.tensor_copy(qk_tok[:, par, n, 1, :, RD:],
                                     ckv[:, bass.ds(tile, 1), :].to_broadcast([P, GH, KL])).then_inc(s_ck, 1)
                elif t[0] == "op":
                    _, par, n = t
                    c = 4 * i + (0 if par else 2) + n
                    pool.wait_ge(s_yg, c + 1)
                    pool.wait_ge(s_x, c + 2)
                    rows = xa[:, bass.ds(out_slot(i, par) * TB + 2 * n, 2), :]
                    pool.tensor_tensor(rows, rows, y_gate[:, n], ALU.add).then_inc(s_x, 1)

            for k, t in enumerate(AUX_FIRST):
                aux(None, k, t)
            with pool.Fori(0, ITERS) as i:
                for u in range(UNITS):
                    for k, t in AUX_K[u]:
                        aux(i, k, t)
            for k, t in enumerate(LAST):
                aux(ITERS, k, t)

            for b in range(NB):
                pool.wait_ge(f_stat, b + 1)
                chain(pool.tensor_scalar(ve2[:], mv2[:, :, 1], EPS_LN, None, ALU.add))
                pool.tensor_tensor(rstd2[:], ve2[:], mhalf[:, 0:TB], ALU.pow).then_inc(f_rstd, 1)
            pool.wait_ge(padded, 16 * ITERS)
            pool.wait_ge(indexed, 1)
            pool.wait_ge(extended, 1)
            pool.wait_ge(f_h2, NB)
            for t in range(NT):
                for r in range(TOPK):
                    pool.indirect_dma_start(slots, bass.IndirectOffsetOnAxis(ap=slot_i[:, t, r:r + 1], axis=0),
                                            h2[:, t, :], None).then_inc(sent, 16)

            last_part = pool.to_reg(NOWHERE - 1)

            def expert_position(n, j):
                if within(n, SLOT_TILES):
                    pool.wait_ge(e_yc, n + 1)
                    pool.wait_ge(e_idx, n + 1)
                    if not (static(n) and n == 0):
                        pool.wait_ge(e_go, n)
                    pool.tensor_tensor(idle[:, 1:2], mhalf[:, 0:1], mhalf[:, 0:1], ALU.add).then_inc(e_go, 1)
                    pool.indirect_dma_start(parts, bass.IndirectOffsetOnAxis(ap=sel_i[:, j:j + 1], axis=0),
                                            ys[:, j], None, bounds_check=last_part, oob_is_err=False).then_inc(e_put[j], 16)

            expert_steps(pool, expert_position)

            for t in range(NT):
                pool.wait_ge(y_gat, t + 1)
                row = xa[:, t + TB, :]
                pool.tensor_tensor(row, row, ygate[:, t % 2], ALU.add).then_inc(y_add, 1)


def route_constants():
    tab = np.zeros((P, R_ALL), np.float32)
    tab[:, R_EARLY:R_TRI] = np.tril(np.ones((EG, EG), np.float32), -1).reshape(1, -1)
    tab[:, R_TRI:R_FULL] = np.triu(np.ones((P, P), np.float32), 1)
    tab[:, R_FULL:R_TILE] = P * np.arange(NT, dtype=np.float32)
    tab[:, R_TILE:R_TOKEN] = np.arange(SLOT_TILES, dtype=np.float32)
    tab[:, R_TOKEN:R_ALL] = TOPK * np.arange(NT * P, dtype=np.float32).reshape(NT, P).T
    return tab


def rope_constants():
    freqs = (1.0 / 10000.0 ** (np.arange(0, RD, 2, dtype=np.float32) / np.float32(RD))).astype(np.float32)
    ang = np.outer(np.arange(SEQ, dtype=np.float32), freqs).astype(np.float32)
    t = np.stack([np.cos(ang), np.sin(ang)]).astype(np.float32)
    t = np.concatenate([t, t], axis=-1)
    t = np.stack([t * np.float32(SCALE), t], axis=1)
    return np.ascontiguousarray(t.reshape(2, 2, TB, P, RD).transpose(3, 2, 0, 1, 4))


def lay_out(inputs):
    a = {k: np.asarray(v) for k, v in inputs.items()}

    def rows(w, n):
        return w.reshape(n, P, -1).transpose(1, 0, 2)

    def heads(w, r):
        return w.reshape(r, H, HD).transpose(2, 1, 0)

    def rotary(w):
        return w.reshape(D, NG, 1, GH, RD // 2, 2).transpose(0, 1, 2, 3, 5, 4)

    r = np.concatenate([rotary(a["L0_attn_Wq_rope"]), rotary(a["L0_attn_Wk_rope"])], axis=2).reshape(D, NG * 512)
    out = {
        "x": a["L0_attn_x"].reshape(NT * P, D),
        "cT": rows(a["L0_c"].T, KD),
        "wmod": rows(a["L0_wmod"], KD),
        "wdn": rows(np.concatenate([a["L0_attn_Wq_down"], a["L0_attn_Wkv_down"]], axis=1), KD),
        "wqup": heads(a["L0_attn_Wq_up"], QL),
        "wkup": heads(a["L0_attn_Wk_up"], KL),
        "wvup": heads(a["L0_attn_Wv_up"], KL),
        "wout": a["L0_attn_Wout"].reshape(H, HD, D).transpose(1, 0, 2),
        "wrope": rows(r, KD).reshape(P, -1),
        "rope_tab": rope_constants(),
        "eye": np.eye(P, dtype=np.float32),
        "qnw": a["L0_attn_q_norm_w"].reshape(QL, 1),
        "kvw_bc": np.broadcast_to(a["L0_attn_kv_norm_w"], (QL, KL)),
        "kvw2": np.concatenate([a["L0_attn_kv_norm_w"]] * 2).reshape(P, 1),
    }

    def experts(w, ws):
        return np.concatenate([w, ws.reshape(2, FI, D)]).transpose(0, 2, 1)

    w13 = np.concatenate([experts(a["L0_ffn_W1"], a["L0_ffn_Ws1"]), experts(a["L0_ffn_W3"], a["L0_ffn_Ws3"])], axis=2)
    w2 = np.concatenate([a["L0_ffn_W2"].transpose(0, 2, 1), a["L0_ffn_Ws2"].T.reshape(2, FI, D)])
    out["wgate"] = rows(a["L0_ffn_gate_w"].T, KD)
    out["w13"] = w13.reshape(ES, KD, P, 2 * FI).transpose(2, 0, 1, 3)
    out["w2"] = w2.reshape(ES, 2, FC, D).transpose(2, 0, 1, 3)
    out["route"] = route_constants()
    return {k: np.ascontiguousarray(v) for k, v in out.items()}


def kernel(**inputs):
    import concourse.bacc as _bacc
    from concourse.bass_utils import run_bass_kernel_spmd as _run

    nc = _bacc.Bacc("TRN2", target_bir_lowering=False, num_devices=1)
    arrays = lay_out(inputs)
    args = {n: nc.dram_tensor(f"in_{n}", a.shape, mybir.dt.from_np(a.dtype), kind="ExternalInput").ap()
            for n, a in arrays.items()}
    args["out"] = nc.dram_tensor("out_x", (NT * P, D), F32, kind="ExternalOutput").ap()
    program(nc, **args)
    r = _run(nc, [{f"in_{n}": a for n, a in arrays.items()}], core_ids=[0])
    return r.results[0]["out_x"].reshape(NB, SEQ, D)
```

```python
from contextlib import ExitStack

import numpy as np
import concourse.bass as bass
from concourse import mybir

F32 = mybir.dt.float32
F32R = mybir.dt.float32r
I32 = mybir.dt.int32
U32 = mybir.dt.uint32
ALU = mybir.AluOpType
ACT = mybir.ActivationFunctionType
AX_X = mybir.AxisListType.X

P = 128
NB, SEQ, D = 4, 512, 256
TB = SEQ // P
NT = NB * TB
KD = D // P
H, HD, RD = 16, 128, 64
QL, KL = 48, 64
GH = 4
NG = H // GH
EPS_RMS, EPS_LN = 1e-6, 1e-5
SCALE = (HD + RD) ** -0.5
E, TOPK, EG, TOPG = 16, 4, 4, 2
FI = 176
FC = FI // 2
ES = E + 2

SLOT_TILES = NT * P * TOPK // P + E
X_W = D
X_DEST = D + E
XW = D + 2 * E
NOWHERE = NT * P * TOPK
CYCLE = 4
PACK = CYCLE + 2
assert SLOT_TILES % CYCLE == 0 and E ** PACK <= 2 ** 24

R_EARLY, R_TRI = 0, EG * EG
R_FULL = R_TRI + P
R_TILE = R_FULL + NT
R_TOKEN = R_TILE + SLOT_TILES
R_ALL = R_TOKEN + NT

IT_HEADS = 2 * GH
UNITS = IT_HEADS * TB
ITERS = NB * H // IT_HEADS
AHEAD = 3


def aux_plan():
    at = {u: [] for u in range(UNITS)}
    for s in range(1, IT_HEADS + 1):
        at[4 * s - 2].append(("tq", s + 1))
        at[4 * s - 1].append(("tk", s + 1))
    for par, start in ((1, 0), (0, 16)):
        for n, (p, a) in enumerate(((0, 1), (2, 3), (5, 6), (8, 9))):
            at[start + p].append(("pr", par, n))
            at[start + a].append(("ab", par, n))
    for par, a, b in ((1, (10, 10), (13, 14)), (0, (20, 21), (25, 26))):
        for n in range(2):
            at[a[n]].append(("ot", par, n))
            at[b[n]].append(("op", par, n))
    return at


AUX_FIRST = [("pr", 0, 0), ("ab", 0, 0), ("pr", 0, 1), ("ab", 0, 1), ("pr", 0, 2), ("ab", 0, 2),
             ("pr", 0, 3), ("ab", 0, 3), ("tq", 0), ("tk", 0), ("tq", 1), ("tk", 1)]
AUX_AT = aux_plan()
AUX_LIST = [t for u in range(UNITS) for t in AUX_AT[u]]
AUX_N = len(AUX_LIST)
assert AUX_N % 2 == 0


ASIDE = 1
LOGIT_ORDER = [b for b in range(NB) if b != ASIDE] + [ASIDE]
PADS = SLOT_TILES // ITERS
assert PADS * ITERS == SLOT_TILES


def program(nc, x, cT, wmod, wdn, wqup, wkup, wvup, wout, wrope, rope_tab, eye, qnw, kvw_bc, kvw2, wgate, w13, w2,
            route, out):
    ctx = ExitStack()
    with ctx:
        def sb(name, shape, dt=F32):
            return ctx.enter_context(nc.sbuf_tensor(name, shape, dt))

        def sem(name):
            return ctx.enter_context(nc.semaphore(name))

        bank = [ctx.enter_context(nc.psum_tensor(f"bank{i}", [P, 512], F32)) for i in range(8)]
        score_bank, pt_bank, out_bank, aux_bank = bank[0:2], bank[2:4], bank[4:6], bank[6:8]

        h_dram = nc.dram_tensor("h_dram", [NB, P, 2 * KD * SEQ], F32).ap()
        mod_dram = nc.dram_tensor("mod_dram", [NB, P, 2 * D], F32).ap()
        slots = nc.dram_tensor("slots", [SLOT_TILES * P, XW], F32).ap()
        parts = nc.dram_tensor("parts", [NT * P * TOPK, D], F32).ap()
        cq_dram = nc.dram_tensor("cq_dram", [NB, QL, 2 * SEQ], F32).ap()

        ident = sb("ident", [P, P])
        gate = sb("gate", [P, NB + 1, 2, D])
        xa = sb("xa", [P, (NB + 1) * TB, D])
        mhalf = sb("mhalf", [P, NT])
        idle = sb("idle", [P, 4])
        bst2 = sb("bst2", [P, NT, 6])
        mv2 = sb("mv2", [P, NT, 2])
        ve2 = sb("ve2", [P, NT])
        rstd2 = sb("rstd2", [P, NT])

        attention = ExitStack()

        def sb2(name, shape, dt=F32):
            return attention.enter_context(nc.sbuf_tensor(name, shape, dt))

        rope = sb2("rope", [P, TB, 2, 2, RD])
        wr_hi = sb2("wr_hi", [P, KD, NG, 512], F32R)
        wr_lo = sb2("wr_lo", [P, KD, NG, 512], F32R)
        ab_hi = sb2("ab_hi", [P, H * KL], F32R)
        ab_lo = sb2("ab_lo", [P, H * KL], F32R)
        early = ExitStack()
        mod_o = early.enter_context(nc.sbuf_tensor("mod_o", [P, 2, 2, D], F32))
        early.close()
        mout = sb2("mout", [P, 2, H // 2, D], F32R)
        modT = sb2("modT", [P, 2, KD, NB])
        ckv = sb2("ckv", [P, NT, KL])
        h_st = sb2("h_st", [P, 2, KD, SEQ], F32R)
        cq_st = sb2("cq_st", [P, 2, SEQ], F32R)
        qk_tok = sb2("qk_tok", [P, 2, TB, 2, GH, P])
        o_tok = sb2("o_tok", [P, 2, TB, GH * KL])

        pad = sb2("pad", [P, XW])

        wr_raw = qk_tok[:].rearrange("p a t q h c -> p a (t q h c)")[:, 0]
        wout_s = qk_tok[:].rearrange("p a t q h c -> p a (t q h c)")[:, 1].rearrange("p (h d) -> p h d", h=H)
        first = ExitStack()

        def sb1(name, shape, dt=F32):
            return first.enter_context(nc.sbuf_tensor(name, shape, dt))

        wdn_s = sb1("wdn_s", [P, KD, QL + KL])
        wqup_s = sb1("wqup_s", [P, H, QL])
        wkup_s = sb1("wkup_s", [P, H, KL])
        ab_f = sb1("ab_f", [QL, H * KL])
        qnw_s = sb1("qnw_s", [QL, 1])
        qnw_sc = sb1("qnw_sc", [QL, 1])
        kvwb_s = sb1("kvwb_s", [QL, KL])
        h_hl = sb1("h_hl", [P, 2, KD, SEQ], F32R)
        cq_hl = h_hl[0:QL].rearrange("p a k t -> p (a k t)")[:, 0:2 * SEQ].rearrange("p (a t) -> p a t", a=2)
        dn = sb1("dn", [P, NT, QL + KL])
        ncq = sb1("ncq", [P, NT, QL])
        bst = sb1("bst", [P, NT, 6])
        mv = sb1("mv", [P, NT, 2])
        ve = sb1("ve", [P, 2, 3, NT // 2])
        rstd = sb1("rstd", [P, 2, NT // 2])
        ssq = sb1("ssq", [P, 2, 2, NT // 2])
        rms = sb1("rms", [P, 2, 2, NT // 2])
        cT_s = sb1("cT_s", [P, KD, NB])
        cexp = sb1("cexp", [P, KD, NB])
        crec = sb1("crec", [P, KD, NB])
        csil = sb1("csil", [P, KD, NB])
        wmod_s = sb1("wmod_s", [P, KD, 6 * D])
        csil_bc = sb1("csil_bc", [P, KD, NB, P])
        h_f = sb1("h_f", [P, KD, SEQ])
        gabs, gsgn = h_f[:, 0, :], h_f[:, 1, :]
        wvup_s = sb1("wvup_s", [P, H, KL])
        kvw2_s = sb1("kvw2_s", [P, 1])
        xn = o_tok[:].rearrange("p a q n -> p a (q n)").rearrange("p a (t d) -> p a t d", t=TB)
        dsq = mod_o[:].rearrange("p a w n -> p (a w n)")[:, 0:2 * TB * (QL + KL)].rearrange("p (t n) -> p t n", t=2 * TB)
        def h_slot(b):
            return h_st if b == 0 else h_hl

        def cq_slot(b):
            return cq_st[0:QL] if b == 0 else cq_hl

        first.close()

        t_cos = sb2("t_cos", [P, 2, 2 * GH, RD])
        t_sin = sb2("t_sin", [P, 2, 2 * GH, RD])
        qT = sb2("qT", [P, 2, 2, SEQ], F32R)
        kT = sb2("kT", [P, 2, 2, SEQ], F32R)
        nmax = sb2("nmax", [P, 4])
        prob = sb2("prob", [P, 2, SEQ])
        rsum = sb2("rsum", [P, 2, TB])
        rinv = sb2("rinv", [P, 2, TB])
        probT = sb2("probT", [P, 2, SEQ])
        oT = sb2("oT", [P, 2, 2, 2, SEQ], F32R)
        y_gate = sb2("y_gate", [P, 2, 2, D])

        attention.close()

        w_hi = sb("w_hi", [P, ES, KD, 2 * FI], F32R)
        loaded = ExitStack()
        w_raw = loaded.enter_context(nc.sbuf_tensor("w_raw", [P, ES, KD, 2 * FI], F32))
        loaded.close()
        w_lo = sb("w_lo", [P, ES, KD, 2 * FI], F32R)
        w2_p = sb("w2_p", [P, ES, 2, D])
        w2_s = w2_p[0:FC]
        h2T = w2_p[:, 0:4].rearrange("p e c n -> p (e c n)").rearrange("p (a k t) -> p a k t", a=2, k=KD)
        own_i = sb("own_i", [P, SLOT_TILES], I32)
        gw_s = sb("gw_s", [P, KD, E])
        tab = sb("tab", [P, R_ALL])
        early_s = tab[:, R_EARLY:R_TRI].rearrange("p (a b) -> p a b", a=EG)
        tri_s = tab[:, R_TRI:R_FULL]
        full_s = tab[:, R_FULL:R_TILE]
        tile_s = tab[:, R_TILE:R_TOKEN]
        token_s = tab[:, R_TOKEN:R_ALL]
        h2 = sb("h2", [P, NT, XW])
        ones = sb("ones", [P, P])
        sg = sb("sg", [P, NT, E])
        gm = sb("gm", [P, NT, EG])
        gsel = sb("gsel", [P, NT, EG])
        msk = sb("msk", [P, NT, E])
        top = sb("top", [P, NT, 8])
        above = sb("above", [P, NT, E])
        equal = sb("equal", [P, NT, E])
        pre = sb("pre", [P, 2, NT, E])
        gtm = above[:].rearrange("p t (a b) -> p t a b", a=EG)
        gem = equal[:].rearrange("p t (a b) -> p t a b", a=EG)
        quota = sb("quota", [P, NT])
        den = quota
        spare = xa[:, 0:TB, :].rearrange("p a n -> p (a n)")
        started = spare[:, 0:SLOT_TILES // 2 * (E + 1)].rearrange("p (s e) -> p s e", s=SLOT_TILES // 2)
        picked = spare.rearrange("p (t r e) -> p t r e", t=NT, r=TOPK)
        loads = ve2
        tiles_of = sb("tiles_of", [P, 2, E + 1])
        owner = sb("owner", [P, SLOT_TILES, E])
        after_started = SLOT_TILES // 2 * (E + 1)
        own_f = spare[:, after_started:after_started + SLOT_TILES]
        packed_f = spare[:, after_started + SLOT_TILES:after_started + SLOT_TILES + 2 * (SLOT_TILES - PACK + 1)]\
            .rearrange("p (a n) -> p a n", a=2)
        slot_f = sb("slot_f", [P, NT, TOPK])
        slot_i = sb("slot_i", [P, NT, TOPK], U32)
        x_hl = sb("x_hl", [P, 2, 2, KD * P], F32R)
        modb = x_hl[:].bitcast(F32).rearrange("p a b n -> p (a b n)").rearrange("p (b a n) -> p b a n", b=2, a=2)
        sl = sb("sl", [P, 2, FI])
        g_s = pre[:].rearrange("p a t e -> p (a t e)")[:, 0:2 * FI].rearrange("p (a n) -> p a n", a=2)
        gT = sb("gT", [FC, 2, 2, P])
        chosen_by = sb("chosen_by", [P, CYCLE, 2, E])
        x_now = sb("x_now", [P, D])
        sel = sb("sel", [P, CYCLE, 2])
        sel_i = sb("sel_i", [P, CYCLE], U32)
        h2_flat = h2[:].rearrange("p t n -> p (t n)")
        xs = h2_flat[:, 0:CYCLE * XW].rearrange("p (j n) -> p j n", j=CYCLE)
        ys = h2_flat[:, CYCLE * XW:CYCLE * (XW + D)].rearrange("p (j n) -> p j n", j=CYCLE)
        zg = msk[:].rearrange("p t e -> p (t e)")
        yb = w_hi[:].bitcast(F32).rearrange("p e k n -> p (e k n)")[:, 0:4 * TOPK * D].rearrange("p (j n) -> p j n", j=4)
        ysum = h2_flat[:, 0:2 * D].rearrange("p (j n) -> p j n", j=2)
        ygate = h2_flat[:, 2 * D:4 * D].rearrange("p (j n) -> p j n", j=2)

        ld_a, ld_b, ld_c, ld_d, ld_m, ld_v = (sem(n) for n in ("ld_a", "ld_b", "ld_c", "ld_d", "ld_m", "ld_v"))
        ld_x = [sem(f"ld_x{b}") for b in range(NB)]
        dve_c, pool_c = sem("dve_c"), sem("pool_c")
        c_exp, c_sil, mod_mm, mod_ev = sem("c_exp"), sem("c_sil"), sem("mod_mm"), sem("mod_ev")
        ab_mm, ab_ev = sem("ab_mm"), sem("ab_ev")
        m_mm, m_ev, g_mm, g_ev = sem("m_mm"), sem("m_ev"), sem("g_mm"), sem("g_ev")
        wr_h, wr_l, ab_h, ab_l = sem("wr_h"), sem("wr_l"), sem("ab_h"), sem("ab_l")
        zeroed = sem("zeroed")
        p_stat, p_rstd, p_xn, p_tr, p_h, p_hhi, p_hlo = (sem(n) for n in
            ("p_stat", "p_rstd", "p_xn", "p_tr", "p_h", "p_hhi", "p_hlo"))
        p_dn, p_ssq, p_rms, p_ncq, p_ctr, p_chi, p_clo, p_st, p_cst = (sem(n) for n in
            ("p_dn", "p_ssq", "p_rms", "p_ncq", "p_ctr", "p_chi", "p_clo", "p_st", "p_cst"))
        p_dnev = sem("p_dnev")
        staged, p_st0 = sem("staged"), sem("p_st0")
        s_score, s_max, s_exp, s_pt, s_ptc, s_pv, s_norm, s_rinv = (sem(n) for n in
            ("s_score", "s_max", "s_exp", "s_pt", "s_ptc", "s_pv", "s_norm", "s_rinv"))
        aux_done = sem("aux_done")
        s_ql, s_ol, m_h = sem("s_ql"), sem("s_ol"), sem("m_h")
        s_sin, s_rope, s_ck, s_ab, s_qk, s_ot, s_yg, s_x = (sem(n) for n in
            ("s_sin", "s_rope", "s_ck", "s_ab", "s_qk", "s_ot", "s_yg", "s_x"))
        stored, mb_mm, mb_ev, ld_f = (sem(n) for n in
            ("stored", "mb_mm", "mb_ev", "ld_f"))
        ld_w2 = sem("ld_w2")
        padded, pad_set, sent, masked, counted, listed, indexed, extended = (sem(n) for n in
            ("padded", "pad_set", "sent", "masked", "counted", "listed", "indexed", "extended"))
        z_x, z_hi, z_lo, z_h, z_sl, z_g, z_gt, z_gTc, z_y, z_zg = (sem(n) for n in
            ("z_x", "z_hi", "z_lo", "z_h", "z_sl", "z_g", "z_gt", "z_gTc", "z_y", "z_zg"))
        e_go, f_centred, f_h2p = sem("e_go"), sem("f_centred"), sem("f_h2p")
        z_now = sem("z_now")
        e_mul, e_sel, e_idx, e_yc = (sem(n) for n in ("e_mul", "e_sel", "e_idx", "e_yc"))
        ld_s = [sem(f"ld_s{j}") for j in range(CYCLE)]
        e_put = [sem(f"e_put{j}") for j in range(CYCLE)]
        ld_y = [sem(f"ld_y{j}") for j in range(4)]
        y_sum, y_gat, y_add = sem("y_sum"), sem("y_gat"), sem("y_add")
        mb_st = [sem("mb_st0"), sem("mb_st1")]
        mb_ld = [sem("mb_ld0"), sem("mb_ld1")]
        ld_ws, ld_ws2, ld_w = sem("ld_ws"), sem("ld_ws2"), sem("ld_w")
        w_h, w_l, f_stat, f_rstd, f_h2, f_tr, f_h2T, f_lg, f_sg = (sem(n) for n in
            ("w_h", "w_l", "f_stat", "f_rstd", "f_h2", "f_tr", "f_h2T", "f_lg", "f_sg"))
        e_x, e_hi, e_lo, e_h, e_sl, e_g, e_gt, e_gTc, e_y = (sem(n) for n in
            ("e_x", "e_hi", "e_lo", "e_h", "e_sl", "e_g", "e_gt", "e_gTc", "e_y"))

        block = ctx.enter_context(nc.Block())

        def aux_count(i, k):
            return k + 1 if i is None else AUX_N * i + len(AUX_FIRST) + k + 1

        def aux_home(i, k):
            return aux_bank[(k if i is None else len(AUX_FIRST) + k) % 2]

        def read_out(i, t):
            if t[0] in ("tq", "tk"):
                return s_ql, (0 if i is None else 2 * IT_HEADS * i) + 2 * t[1] + (1 if t[0] == "tq" else 2)
            if t[0] in ("pr", "ab"):
                return s_sin if t[0] == "pr" else s_ab, pr_count(i, t[1], t[2]) + 1
            return s_ol if t[0] == "ot" else s_yg, 4 * i + (0 if t[1] else 2) + t[2] + 1

        def pr_count(i, par, n):
            return n if i is None else 2 * TB * i + (TB if par else 2 * TB) + n

        def aux_tasks():
            k = 0
            for u in range(UNITS):
                for t in AUX_AT[u]:
                    yield u, k, t
                    k += 1

        AUX_K = {u: [] for u in range(UNITS)}
        for u, k, t in aux_tasks():
            AUX_K[u].append((k, t))

        def it_batch(i):
            return i // 2

        def prep_batch(i, par):
            return i // 2 if par else ((i + 1) // 2) % NB

        def prep_group(i, par):
            return (i % 2) * 2 + 1 if par else ((i + 1) % 2) * 2

        def out_pair(i, par):
            return ((i + 1) % 2) * 4 + 2 if par else (i % 2) * 4

        def out_slot(i, par):
            return (i + 1) // 2 if par else i // 2 + 1

        Z_LOOP = range(2, NT - 4)
        E_LOOP = range(CYCLE, SLOT_TILES - CYCLE)

        def shared_steps(engine, step):
            for t in range(-2, Z_LOOP.start):
                step(t, t % 2)
            with engine.Fori(0, len(Z_LOOP) // 2) as i:
                for j in range(2):
                    step(i * 2 + (Z_LOOP.start + j), j)
            for t in range(Z_LOOP.stop, NT):
                step(t, t % 2)

        def expert_steps(engine, step, look_up=None):
            def ahead(first):
                return () if look_up is None else (look_up(first),)

            more = ahead(0)
            for n in range(-3, E_LOOP.start):
                step(n, n % CYCLE, *more)
            with engine.Fori(0, len(E_LOOP) // CYCLE) as i:
                more = ahead(i * CYCLE + E_LOOP.start)
                for j in range(CYCLE):
                    step(i * CYCLE + (E_LOOP.start + j), j, *more)
            more = ahead(SLOT_TILES - PACK)
            for n in range(E_LOOP.stop, SLOT_TILES):
                step(n, n % CYCLE, *more)

        def modulated(b):
            return (f_h2p, 1) if b == ASIDE else (f_h2, b + 1 - (b > ASIDE))

        def static(n):
            return isinstance(n, int)

        def within(n, limit):
            return not static(n) or 0 <= n < limit

        LAST = [("ot", 1, 0), ("ot", 1, 1), ("op", 1, 0), ("op", 1, 1)]

        @block.sync
        def _(sp):
            sp.dma_start(cT_s[:], cT).then_inc(ld_a, 16)
            sp.dma_start(wmod_s[:, :, 0:2 * D], wmod[:, :, 0:2 * D]).then_inc(ld_a, 16)
            sp.dma_start(ident[:], eye).then_inc(ld_a, 16)
            for b in range(NB):
                sp.dma_start(xa[:, TB * (b + 1):TB * (b + 2), :],
                             x[SEQ * b:SEQ * (b + 1)].rearrange("(t p) d -> p t d", p=P)).then_inc(ld_x[b], 16)
            sp.dma_start(wdn_s[:], wdn).then_inc(ld_d, 16)
            sp.dma_start(wqup_s[:], wqup).then_inc(ld_c, 16)
            sp.dma_start(wkup_s[:], wkup).then_inc(ld_c, 16)
            sp.dma_start(qnw_s[:], qnw).then_inc(ld_c, 16)
            sp.dma_start(kvwb_s[:], kvw_bc).then_inc(ld_c, 16)
            half_w = KD * NG * 512 // 2
            sp.dma_start(wr_raw[:, 0:half_w], wrope[:, 0:half_w]).then_inc(ld_b, 16)

            def store_inputs(b):
                sp.wait_ge(p_hhi, b + 1)
                sp.wait_ge(p_hlo, b + 1)
                sp.dma_start(h_dram[b], h_slot(b)[:].bitcast(F32).rearrange("p a k t -> p (a k t)"))\
                    .then_inc(p_st0 if b == 0 else p_st, 16)

            store_inputs(1)
            sp.dma_start(wr_raw[:, half_w:], wrope[:, half_w:]).then_inc(ld_b, 16)
            sp.dma_start(rope[:], rope_tab).then_inc(ld_b, 16)
            store_inputs(2)
            sp.dma_start(wmod_s[:, :, 2 * D:], wmod[:, :, 2 * D:]).then_inc(ld_m, 16)
            store_inputs(3)
            sp.dma_start(wvup_s[:], wvup).then_inc(ld_v, 16)
            sp.dma_start(kvw2_s[:], kvw2).then_inc(ld_v, 16)
            sp.dma_start(wout_s, wout).then_inc(ld_v, 16)
            def stage(b):
                sp.dma_start(h_st[:].bitcast(F32).rearrange("p a k t -> p (a k t)"),
                             h_dram[bass.ds(b, 1)].rearrange("b p n -> (b p) n")).then_inc(staged, 16)
                sp.dma_start(cq_st[0:QL].bitcast(F32).rearrange("p a t -> p (a t)"),
                             cq_dram[bass.ds(b, 1)].rearrange("b p n -> (b p) n")).then_inc(staged, 16)

            def store_latents(b):
                sp.wait_ge(p_chi, b + 1)
                sp.wait_ge(p_clo, b + 1)
                sp.dma_start(cq_dram[b], cq_slot(b).bitcast(F32).rearrange("p a t -> p (a t)"))\
                    .then_inc(p_st0 if b == 0 else p_cst, 16)

            def store_modulations(b):
                sp.wait_ge(mb_ev, b + 1)
                sp.dma_start(mod_dram[b], mod_o[:, b % 2].rearrange("p a n -> p (a n)")).then_inc(mb_st[b % 2], 16)

            store_latents(1)
            store_latents(0)
            for b in range(2):
                store_modulations(b)
                store_latents(2 + b)
            store_modulations(2)
            store_modulations(3)
            store_inputs(0)
            sp.wait_ge(p_st, 16 * (NB - 1))
            sp.wait_ge(p_cst, 16 * (NB - 1))
            sp.wait_ge(p_st0, 32)
            for q in mb_st:
                sp.wait_ge(q, 32)
            last = max(k for u, k, t in aux_tasks() if t[0] in ("pr", "ab") and t[1] == 1)
            sp.wait_ge(pad_set, 3)
            with sp.Fori(0, ITERS) as i:
                sp.wait_ge(aux_done, aux_count(i, last))
                stage(((i + 1) // 2) % NB)
                sp.dma_start(slots[bass.ds(i * (PADS * P), PADS * P)].rearrange("(s p) n -> p s n", p=P),
                             pad[:].unsqueeze(1).to_broadcast([P, PADS, XW])).then_inc(padded, 16)
            sp.wait_ge(staged, 32 * ITERS)
            sp.wait_ge(s_x, 4 * ITERS + 4)
            for b in range(NB):
                if b >= 2:
                    sp.wait_ge(*modulated(b - 2))
                sp.dma_start(modb[:, b % 2].rearrange("p a n -> p (a n)"), mod_dram[b]).then_inc(mb_ld[b % 2], 16)
                if b == 0:
                    sp.wait_ge(padded, 16 * ITERS)
                    sp.dma_start(gw_s[:], wgate).then_inc(ld_f, 16)
                    sp.dma_start(tab[:], route).then_inc(ld_f, 16)
                if b == 1:
                    sp.dma_start(w_raw[:, E:], w13[:, E:]).then_inc(ld_ws, 16)
                    sp.dma_start(w2_s[:, E:], w2[:, E:]).then_inc(ld_ws2, 16)
            for e in range(0, E, 4):
                sp.dma_start(w_raw[:, e:e + 4], w13[:, e:e + 4]).then_inc(ld_w, 16)
            sp.wait_ge(f_lg, NB)
            sp.dma_start(w2_s[:, 0:E], w2[:, 0:E]).then_inc(ld_w2, 16)

            sp.wait_ge(sent, 16 * NT * TOPK)
            sp.wait_ge(z_x, NT)

            def load_slots(n, j):
                if not within(n + 3, SLOT_TILES):
                    return
                m, jm = n + 3, (j + 3) % CYCLE
                if not (static(n) and m < CYCLE):
                    sp.wait_ge(e_x, m - CYCLE + 1)
                    sp.wait_ge(e_mul, m - CYCLE + 1)
                sp.dma_start(xs[:, jm], slots[bass.ds(m * P, P)] if not static(m) else slots[m * P:(m + 1) * P])\
                    .then_inc(ld_s[jm], 16)

            expert_steps(sp, load_slots)

            for j in range(CYCLE):
                sp.wait_ge(e_put[j], 16 * (SLOT_TILES // CYCLE))
            sp.wait_ge(e_g, SLOT_TILES)
            own_parts = parts.rearrange("(t p r) d -> t p (r d)", t=NT, r=TOPK)
            for t in range(4):
                sp.dma_start(yb[:, t], own_parts[t]).then_inc(ld_y[t], 16)
            for b in range(NB):
                if b + 1 < NB:
                    for j in range(4):
                        sp.wait_ge(y_sum, 4 * b + j + 1)
                        sp.dma_start(yb[:, j], own_parts[4 * b + j + 4]).then_inc(ld_y[j], 16)
                sp.wait_ge(y_add, 4 * (b + 1))
                sp.dma_start(out[SEQ * b:SEQ * (b + 1)].rearrange("(t p) d -> p t d", p=P),
                             xa[:, TB * (b + 1):TB * (b + 2), :]).then_inc(stored, 16)
            sp.wait_ge(stored, 16 * NB)

        @block.tensor
        def _(pe):
            def mm3(dst, l_hi, l_lo, r_hi, r_lo, start, stop):
                pe.matmul(dst, l_hi, r_hi, start=start, stop=False)
                pe.matmul(dst, l_hi, r_lo, start=False, stop=False)
                return pe.matmul(dst, l_lo, r_hi, start=False, stop=stop)

            pe.wait_ge(ld_a, 48)
            pe.wait_ge(c_sil, 1)
            for w in range(2):
                for c in range(KD):
                    for k in range(KD):
                        mm = pe.matmul(aux_bank[0][:, (w * KD + c) * NB:(w * KD + c + 1) * NB],
                                       wmod_s[:, k, w * D + c * P:w * D + (c + 1) * P],
                                       csil[:, k, :], start=(k == 0), stop=(k == KD - 1))
            mm.then_inc(mod_mm, 1)

            def down(b):
                pe.wait_ge(p_h, KD * (b + 1))
                if b >= 2:
                    pe.wait_ge(p_dnev, b - 1)
                for t in range(TB):
                    for k in range(KD):
                        mm = pe.matmul(out_bank[b % 2][:, t * P:t * P + QL + KL], h_f[:, k, t * P:(t + 1) * P],
                                       wdn_s[:, k, :], start=(k == 0), stop=(k == KD - 1))
                mm.then_inc(p_dn, 1)

            def turn_latents(b):
                pe.wait_ge(p_ncq, b // 2 + 1)
                if b >= 2:
                    pe.wait_ge(p_clo, b - 1)
                for t in range(TB):
                    mm = pe.transpose(pt_bank[b % 2][0:QL, t * P:(t + 1) * P], ncq[:, b * TB + t, :], ident[:])
                mm.then_inc(p_ctr, 1)

            pe.wait_ge(mod_ev, 1)
            for b in range(NB):
                pe.wait_ge(p_xn, b + 1)
                for k in range(KD):
                    if b > 0:
                        pe.wait_ge(p_h, KD * (b - 1) + k + 1)
                    for t in range(TB):
                        mm = pe.transpose(aux_bank[k][:, t * P:(t + 1) * P], xn[:, b % 2, t, k * P:(k + 1) * P], ident[:])
                    mm.then_inc(p_tr, 1)
                if b == 0:
                    pe.wait_ge(ld_d, 16)
                down(b)
            turn_latents(0)
            turn_latents(1)

            pe.wait_ge(ld_c, 16 * 4)
            pe.wait_ge(p_dnev, NB)
            for h in range(H):
                mm = pe.matmul(out_bank[h // 8][0:QL, (h % 8) * KL:(h % 8 + 1) * KL], wqup_s[:, h, :],
                               wkup_s[:, h, :], start=True, stop=True)
                if h % 8 == 7:
                    mm.then_inc(ab_mm, 1)
            def row_modulations(b):
                for z, chunks in enumerate(((2, 5), (3, 4))):
                    if b > 0:
                        pe.wait_ge(mb_ev if z else g_ev, b)
                    for w in range(2):
                        for k in range(KD):
                            mm = pe.matmul(score_bank[z][:, w * D:(w + 1) * D], csil_bc[:, k, b, :],
                                           wmod_s[:, k, chunks[w] * D:(chunks[w] + 1) * D],
                                           start=(k == 0), stop=(k == KD - 1))
                    mm.then_inc(mb_mm if z else g_mm, 1)

            def aux(i, k, t):
                dst = aux_home(i, k)
                if t[0] == "ab":
                    pe.wait_ge(ab_l, 1)
                if i is None and k >= 2:
                    pe.wait_ge(*read_out(None, AUX_FIRST[k - 2]))
                elif i is not None and k >= 2:
                    pe.wait_ge(*read_out(i, (LAST if isinstance(i, int) else AUX_LIST)[k - 2]))
                elif i is not None:
                    kind, s = AUX_LIST[AUX_N - 2 + k]
                    pe.wait_ge(*read_out(i, (kind, s - IT_HEADS)))
                if t[0] == "pr":
                    _, par, n = t
                    g = 0 if i is None else prep_group(i, par)
                    if n == 0 and i is None:
                        pe.wait_ge(p_hlo, 1)
                        pe.wait_ge(p_hhi, 1)
                    elif n == 0 and par == 0:
                        pe.wait_ge(staged, 32 * (i + 1))
                    for c in range(KD):
                        tok = slice(n * P, (n + 1) * P)
                        mm = mm3(dst[:], h_st[:, 0, c, tok], h_st[:, 1, c, tok],
                                 wr_hi[:, c, bass.ds(g, 1), :].rearrange("p a n -> p (a n)"),
                                 wr_lo[:, c, bass.ds(g, 1), :].rearrange("p a n -> p (a n)"),
                                 c == 0, c == KD - 1)
                elif t[0] == "ab":
                    _, par, n = t
                    g = 0 if i is None else prep_group(i, par)
                    tok = slice(n * P, (n + 1) * P)
                    mm = mm3(dst[:, 0:GH * KL], cq_st[:, 0, tok], cq_st[:, 1, tok],
                             ab_hi[:, bass.ds(g * (GH * KL), GH * KL)], ab_lo[:, bass.ds(g * (GH * KL), GH * KL)],
                             True, True)
                elif t[0] in ("tq", "tk"):
                    s = t[1]
                    par, hh = (s // GH) % 2, s % GH
                    if t[0] == "tq" and hh == 0:
                        n = pr_count(i, par, TB) if i is not None else TB
                        pe.wait_ge(s_rope, n)
                        pe.wait_ge(s_ab, n)
                        pe.wait_ge(s_ck, n)
                    for n in range(TB):
                        mm = pe.transpose(dst[:, n * P:(n + 1) * P], qk_tok[:, par, n, int(t[0] == "tk"), hh, :], ident[:])
                elif t[0] == "ot":
                    _, par, n = t
                    pe.wait_ge(s_norm, IT_HEADS * i + (0 if par else GH) + 1)
                    for q in range(TB):
                        mm = pe.transpose(dst[:, q * P:(q + 1) * P], o_tok[:, par, q, n * P:(n + 1) * P], ident[:])
                else:
                    _, par, n = t
                    if n == 0:
                        pe.wait_ge(s_ol, 4 * i + (2 if par else 4))
                    g2 = out_pair(i, par)
                    for q in range(2):
                        for pp in range(2):
                            tok = slice((2 * n + q) * P, (2 * n + q + 1) * P)
                            mm = mm3(dst[:, q * D:(q + 1) * D], oT[:, par, pp, 0, tok], oT[:, par, pp, 1, tok],
                                     mout[:, 0, bass.ds(g2 + pp, 1), :].rearrange("p a n -> p (a n)"),
                                     mout[:, 1, bass.ds(g2 + pp, 1), :].rearrange("p a n -> p (a n)"), pp == 0, pp == 1)
                mm.then_inc(aux_done, 1)

            def score(i, u):
                s, q = u // TB, u % TB
                if i is None:
                    if q == 0:
                        pe.wait_ge(s_ql, 2 * (s + 1))
                    if u >= 2:
                        pe.wait_ge(s_exp, u - 1)
                else:
                    if q == 0:
                        pe.wait_ge(s_ql, 2 * IT_HEADS * i + 2 * (s + 1))
                    pe.wait_ge(s_exp, UNITS * i + u - 1)
                tok = slice(q * P, (q + 1) * P)
                mm3(score_bank[u % 2][:], qT[:, s % 2, 0, tok], qT[:, s % 2, 1, tok], kT[:, s % 2, 0, :], kT[:, s % 2, 1, :],
                    True, True).then_inc(s_score, 1)

            def transpose_probs(i, u):
                base = 0 if i is None else UNITS * i
                if i is None:
                    pe.wait_ge(s_exp, u + 1)
                for c in range(TB):
                    mm = pe.transpose(pt_bank[u % 2][:, c * P:(c + 1) * P], prob[:, u % 2, c * P:(c + 1) * P], ident[:])
                mm.then_inc(s_pt, 1)

            def weigh_values(i, u):
                s, q = u // TB, u % TB
                pe.wait_ge(s_ptc, UNITS * i + u + 1)
                if q == 0 and s > 0:
                    pe.wait_ge(s_norm, IT_HEADS * i + s)
                for c in range(TB):
                    mm = pe.matmul(out_bank[s % 2][:, q * KL:(q + 1) * KL], probT[:, u % 2, c * P:(c + 1) * P],
                                   ckv[:, bass.ds(it_batch(i) * TB + c, 1), :].rearrange("p a n -> p (a n)"),
                                   start=(c == 0), stop=(c == TB - 1))
                mm.then_inc(s_pv, 1)

            pe.wait_ge(ab_ev, 2)
            pe.wait_ge(p_clo, 1)
            pe.wait_ge(ld_m, 16)
            pe.wait_ge(c_sil, 2)
            pe.wait_ge(wr_l, 1)
            pe.wait_ge(wr_h, 1)
            pe.wait_ge(ab_h, 1)
            pe.wait_ge(ab_l, 1)
            pe.wait_ge(zeroed, 2)
            for k, t in enumerate(AUX_FIRST):
                aux(None, k, t)
                if t[0] == "ab":
                    row_modulations(t[2])
                    if t[2] < 2:
                        turn_latents(2 + t[2])
            pe.wait_ge(p_clo, NB)
            pe.wait_ge(g_ev, NB)
            pe.wait_ge(mb_ev, NB)
            for u in range(AHEAD):
                score(None, u)
            transpose_probs(None, 0)
            pe.wait_ge(ld_v, 48)
            for q in range(4):
                if q >= 2:
                    pe.wait_ge(m_ev, q - 1)
                for pr in range(2 * q, 2 * q + 2):
                    for s in range(2):
                        mm = pe.matmul(out_bank[q % 2][s * KL:(s + 1) * KL, (pr % 2) * D:(pr % 2 + 1) * D],
                                       wvup_s[:, 2 * pr + s, :], wout_s[:, 2 * pr + s, :], start=True, stop=True)
                mm.then_inc(m_mm, 1)
            pe.wait_ge(m_ev, 4)
            with pe.Fori(0, ITERS) as i:
                for u in range(UNITS):
                    score(i, u + AHEAD)
                    transpose_probs(i, u + 1)
                    weigh_values(i, u)
                    for k, t in AUX_K[u]:
                        aux(i, k, t)
            for k, t in enumerate(LAST):
                aux(ITERS, k, t)

            pe.wait_ge(s_x, 4 * ITERS + 4)
            pe.wait_ge(ld_f, 32)
            def turn_inputs(n):
                pe.wait_ge(*modulated(LOGIT_ORDER[n]))
                if n >= 2:
                    pe.wait_ge(f_h2T, n - 1)
                for k in range(KD):
                    for t in range(TB):
                        mm = pe.transpose(bank[(0, 3)[n % 2] + k][:, t * P:(t + 1) * P],
                                          h2[:, LOGIT_ORDER[n] * TB + t, k * P:(k + 1) * P], ident[:])
                mm.then_inc(f_tr, 1)

            def logits(n):
                pe.wait_ge(f_h2T, n + 1)
                if n >= 2:
                    pe.wait_ge(f_sg, n - 1)
                for t in range(TB):
                    at = (LOGIT_ORDER[n] * TB + t) * E
                    for k in range(KD):
                        mm = pe.matmul(bank[(2, 5)[n % 2]][:, at:at + E], h2T[:, n % 2, k, t * P:(t + 1) * P],
                                       gw_s[:, k, :], start=(k == 0), stop=(k == KD - 1))
                mm.then_inc(f_lg, 1)

            turn_inputs(0)
            for n in range(NB):
                if n + 1 < NB:
                    turn_inputs(n + 1)
                logits(n)

            x_bank, h_bank, g_bank, y_bank = bank[0:2], bank[2:4], bank[4:6], bank[6:8]

            def inner_products(par, h_par, w_hi_e, w_lo_e):
                for k in range(KD):
                    tok = slice(k * P, (k + 1) * P)
                    mm = mm3(h_bank[h_par][:, 0:2 * FI], x_hl[:, par, 0, tok], x_hl[:, par, 1, tok],
                             w_hi_e(k), w_lo_e(k), k == 0, k == KD - 1)
                return mm

            def turn_gated(par):
                for c in range(2):
                    mm = pe.transpose(g_bank[par][0:FC, c * P:(c + 1) * P], g_s[:, par, c * FC:(c + 1) * FC], ident[:])
                return mm

            def shared_position(t, par):
                def inner(c):
                    if not within(t + 1, NT):
                        return
                    if c == 0:
                        pe.wait_ge(z_lo, t + 2)
                    if not (static(t) and t + 1 == 0):
                        pe.wait_ge(z_g, 2 * (t + 1) + c - 1)
                    inner_products((par + 1) % 2, c, lambda k: w_hi[:, E + c, k, :], lambda k: w_lo[:, E + c, k, :])\
                        .then_inc(z_h, 1)

                def turn(u, c):
                    if not within(u, NT):
                        return
                    pe.wait_ge(z_g, 2 * u + c + 1)
                    if not (static(u) and u == 0):
                        pe.wait_ge(z_gTc, 2 * u + c - 1)
                    turn_gated(c).then_inc(z_gt, 1)

                def outer(c):
                    if not within(t, NT):
                        return
                    pe.wait_ge(z_gTc, 2 * t + c + 1)
                    if c == 0 and not (static(t) and t < 2):
                        pe.wait_ge(z_zg, t - 1)
                    for h in range(2):
                        mm = pe.matmul(y_bank[par][:, 0:D], gT[:, c, h, :], w2_s[:, E + c, h, :],
                                       start=(c == 0 and h == 0), stop=(c == 1 and h == 1))
                    if c == 1:
                        mm.then_inc(z_y, 1)

                if within(t + 2, NT):
                    pe.wait_ge(z_now, t + 3)
                    if not (static(t) and t < 0):
                        pe.wait_ge(z_lo, t + 1)
                    for k in range(KD):
                        mm = pe.transpose(x_bank[par][:, k * P:(k + 1) * P], x_now[:, k * P:(k + 1) * P], ident[:])
                    mm.then_inc(z_x, 1)
                inner(0)
                turn(t, 1)
                outer(0)
                inner(1)
                turn(t + 1, 0)
                outer(1)

            pe.wait_ge(f_sg, NB)
            pe.wait_ge(f_lg, NB)
            pe.wait_ge(w_h, 1)
            pe.wait_ge(w_l, 1)
            for t in range(-2, -1):
                shared_position(t, t % 2)
            pe.wait_ge(masked, 1)
            pe.matmul(bank[6][:, 0:NT * E], tri_s, above[:].rearrange("p t e -> p (t e)"), start=True, stop=True)
            pe.matmul(bank[6][:, NT * E:], ones[:], above[:].rearrange("p t e -> p (t e)"), start=True, stop=True)\
                .then_inc(counted, 1)
            pe.wait_ge(indexed, 1)
            pe.wait_ge(ld_ws2, 16)
            for t in range(-1, Z_LOOP.start):
                shared_position(t, t % 2)
            with pe.Fori(0, len(Z_LOOP) // 2) as i:
                for j in range(2):
                    shared_position(i * 2 + (Z_LOOP.start + j), j)
            for t in range(Z_LOOP.stop, NT):
                shared_position(t, t % 2)

            pe.wait_ge(listed, 1)
            pe.wait_ge(w_h, 1 + E)
            pe.wait_ge(w_l, 1 + E)
            pe.wait_ge(ld_w2, 16)

            def expert_numbers(first):
                packed = pe.value_load(own_i[0:1, bass.ds(first, 1)], min_val=0, max_val=E ** PACK - 1)
                return [(packed // E ** d) % E for d in range(PACK)]

            def expert_position(n, j, experts):
                if static(n):
                    place = n if n < E_LOOP.start else n - (SLOT_TILES - PACK)
                else:
                    place = j
                if within(n + 3, SLOT_TILES):
                    m, jm = n + 3, (j + 3) % CYCLE
                    pe.wait_ge(ld_s[jm], 16 * ((m // CYCLE) + 1))
                    if static(m) and m < 2:
                        pe.wait_ge(z_lo, NT)
                    else:
                        pe.wait_ge(e_lo, m - 1)
                    for k in range(KD):
                        mm = pe.transpose(x_bank[jm % 2][:, k * P:(k + 1) * P], xs[:, jm, k * P:(k + 1) * P], ident[:])
                    mm.then_inc(e_x, 1)
                if within(n + 2, SLOT_TILES):
                    m, par = n + 2, j % 2
                    expert = experts[place + 2]
                    pe.wait_ge(e_lo, m + 1)
                    if static(m) and m < 2:
                        pe.wait_ge(z_g, 2 * NT)
                    else:
                        pe.wait_ge(e_g, m - 1)
                    inner_products(par, par, lambda k: w_hi[:, bass.ds(expert, 1), k, :].rearrange("p a n -> p (a n)"),
                                   lambda k: w_lo[:, bass.ds(expert, 1), k, :].rearrange("p a n -> p (a n)")).then_inc(e_h, 1)
                if within(n + 1, SLOT_TILES):
                    m, par = n + 1, (j + 1) % 2
                    pe.wait_ge(e_g, m + 1)
                    if static(m) and m < 2:
                        pe.wait_ge(z_gTc, 2 * NT)
                    else:
                        pe.wait_ge(e_gTc, m - 1)
                    turn_gated(par).then_inc(e_gt, 1)
                if within(n, SLOT_TILES):
                    expert = experts[place]
                    pe.wait_ge(e_gTc, n + 1)
                    if static(n) and n < 2:
                        pe.wait_ge(z_zg, NT)
                    else:
                        pe.wait_ge(e_yc, n - 1)
                    for h in range(2):
                        mm = pe.matmul(y_bank[j % 2][:, 0:D], gT[:, j % 2, h, :],
                                       w2_s[:, bass.ds(expert, 1), h, :].rearrange("p a n -> p (a n)"),
                                       start=(h == 0), stop=(h == 1))
                    mm.then_inc(e_y, 1)

            expert_steps(pe, expert_position, expert_numbers)

        @block.vector
        def _(dve):
            own = [0]

            def chain(ins):
                own[0] += 1
                ins.then_inc(dve_c, 1)
                dve.wait_ge(dve_c, own[0])

            dve.wait_ge(c_exp, 1)
            chain(dve.tensor_scalar(crec[:], cexp[:], 1.0, None, ALU.add))
            chain(dve.reciprocal(cexp[:], crec[:]))
            dve.tensor_tensor(csil[:], cT_s[:], cexp[:], ALU.mult).then_inc(c_sil, 1)

            def statistics(half):
                for b in (2 * half, 2 * half + 1):
                    dve.wait_ge(ld_x[b], 16)
                    for t in range(b * TB, (b + 1) * TB):
                        ins = dve.bn_stats(bst[:, t, :], xa[:, TB + t, :])
                chain(ins)
                for t in range(2 * half * TB, 2 * (half + 1) * TB):
                    ins = dve.bn_aggr(mv[:, t, :], bst[:, t, :])
                ins.then_inc(p_stat, 1)

            def centre(b):
                if b % 2 == 0:
                    dve.wait_ge(p_rstd, b // 2 + 1)
                if b >= 2:
                    dve.wait_ge(p_tr, KD * (b - 1))
                for t in range(b * TB, (b + 1) * TB):
                    ins = dve.tensor_scalar(xn[:, b % 2, t % TB, :], xa[:, TB + t, :], mv[:, t, 0:1],
                                            rstd[:, b // 2, t % (2 * TB):t % (2 * TB) + 1], ALU.subtract, ALU.mult)
                ins.then_inc(p_xn, 1)

            def modulate(b):
                if b > 0:
                    dve.wait_ge(p_hhi, b)
                    dve.wait_ge(p_hlo, b)
                    dve.wait_ge(p_dn, b)
                for k in range(KD):
                    dve.wait_ge(p_tr, KD * b + k + 1)
                    dve.tensor_scalar(h_f[:, k, :], aux_bank[k][:], modT[:, 1, k, b:b + 1], modT[:, 0, k, b:b + 1],
                                      ALU.mult, ALU.add).then_inc(p_h, 1)

            def latents(b):
                dve.wait_ge(p_dn, b + 1)
                dve.tensor_copy(dn[:, b * TB:(b + 1) * TB, :],
                                out_bank[b % 2][:].rearrange("p (t n) -> p t n", t=TB)[:, :, 0:QL + KL]).then_inc(p_dnev, 1)

            def squares(half):
                t = slice(half * 2 * TB, (half + 1) * 2 * TB)
                dve.wait_ge(p_dnev, 2 * half + 2)
                chain(dve.tensor_tensor(dsq, dn[:, t, :], dn[:, t, :], ALU.mult))
                dve.tensor_reduce(ssq[:, half, 0, :], dsq[:, :, 0:QL], AX_X, ALU.add)
                dve.tensor_reduce(ssq[:, half, 1, :], dsq[:, :, QL:], AX_X, ALU.add).then_inc(p_ssq, 1)

            def norm_latents(half):
                t = slice(half * 2 * TB, (half + 1) * 2 * TB)
                dve.wait_ge(p_rms, half + 1)
                dve.tensor_tensor(ckv[:, t, :], dn[:, t, QL:],
                                  rms[:, half, 1, :].unsqueeze(2).to_broadcast([P, 2 * TB, KL]), ALU.mult)
                dve.tensor_tensor(ncq[:, t, :], dn[:, t, 0:QL],
                                  rms[:, half, 0, :].unsqueeze(2).to_broadcast([P, 2 * TB, QL]), ALU.mult).then_inc(p_ncq, 1)

            def split_latents(b):
                dve.wait_ge(p_chi, b + 1)
                if b > 1:
                    dve.wait_ge(p_cst, 16 * (b - 1))
                dve.tensor_tensor(cq_slot(b)[:, 1, :], pt_bank[b % 2][0:QL, :], cq_slot(b)[:, 0, :].bitcast(F32),
                                  ALU.subtract).then_inc(p_clo, 1)

            statistics(0)
            dve.wait_ge(c_sil, 1)
            dve.tensor_copy(csil_bc[:].rearrange("p k b n -> p (k b) n"), csil[:].rearrange("p k b -> p (k b)")
                            .unsqueeze(2).to_broadcast([P, KD * NB, P])).then_inc(c_sil, 1)
            dve.wait_ge(mod_mm, 1)
            m2 = aux_bank[0][:, 0:2 * KD * NB].rearrange("p (w c b) -> p w c b", w=2, c=KD)
            for w in range(2):
                ins = dve.tensor_scalar(modT[:, w], m2[:, w], float(w), None, ALU.add)
            ins.then_inc(mod_ev, 1)
            dve.wait_ge(mod_ev, 1)
            centre(0)
            centre(1)
            modulate(0)
            statistics(1)
            latents(0)
            modulate(1)
            latents(1)
            squares(0)
            centre(2)
            modulate(2)
            centre(3)
            norm_latents(0)
            latents(2)
            modulate(3)
            split_latents(0)
            latents(3)
            squares(1)
            dve.wait_ge(ld_c, 16 * 4)
            chain(dve.tensor_scalar(qnw_sc[:], qnw_s[:], SCALE, None, ALU.mult))
            for z in range(2):
                dve.wait_ge(ab_mm, z + 1)
                dve.scalar_tensor_tensor(
                    out=ab_f[:, z * 512:(z + 1) * 512].rearrange("p (h c) -> p h c", h=8),
                    in0=out_bank[z][0:QL, :].rearrange("p (h c) -> p h c", h=8), scalar=qnw_sc[:, 0:1],
                    in1=kvwb_s[:].unsqueeze(1).to_broadcast([QL, 8, KL]), op0=ALU.mult, op1=ALU.mult).then_inc(ab_ev, 1)
            dve.wait_ge(ab_h, 1)
            dve.tensor_tensor(ab_lo[0:QL], ab_f[:], ab_hi[0:QL].bitcast(F32), ALU.subtract).then_inc(ab_l, 1)
            dve.wait_ge(wr_h, 1)
            dve.tensor_tensor(wr_lo[:].rearrange("p k g n -> p (k g n)"), wr_raw,
                              wr_hi[:].bitcast(F32).rearrange("p k g n -> p (k g n)"), ALU.subtract).then_inc(wr_l, 1)
            norm_latents(1)
            split_latents(1)

            def row_modulations(b):
                g = gate[:, b + 1].rearrange("p w n -> p (w n)")
                dve.wait_ge(g_mm, b + 1)
                dve.tensor_copy(g, score_bank[0][:]).then_inc(g_ev, 1)
                dve.wait_ge(mb_mm, b + 1)
                if b >= 2:
                    dve.wait_ge(mb_st[b % 2], 16)
                dve.tensor_copy(mod_o[:, b % 2, 0], score_bank[1][:, 0:D])
                dve.tensor_scalar(mod_o[:, b % 2, 1], score_bank[1][:, D:], 1.0, None, ALU.add).then_inc(mb_ev, 1)
                dve.wait_ge(g_ev, b + 1)
                dve.tensor_scalar(gsgn, g, 0.0, 0.5, ALU.is_ge, ALU.subtract)
                chain(dve.scalar_tensor_tensor(out=gabs, in0=g, scalar=-1.0, in1=g, op0=ALU.mult, op1=ALU.max))
                chain(dve.tensor_scalar(gabs, gabs, 0.25, 2.0, ALU.max, ALU.mult))
                chain(dve.tensor_tensor(g, gabs, gsgn, ALU.mult))

            def value_weights():
                for q in range(4):
                    dve.wait_ge(m_mm, q + 1)
                    pair = slice(2 * q, 2 * q + 2)
                    dve.wait_ge(m_h, q + 1)
                    dve.scalar_tensor_tensor(out=mout[:, 1, pair, :], in0=out_bank[q % 2][:].rearrange("p (a n) -> p a n", a=2),
                                             scalar=kvw2_s[:, 0:1], in1=mout[:, 0, pair, :].bitcast(F32),
                                             op0=ALU.mult, op1=ALU.subtract).then_inc(m_ev, 1)

            dve.memset(o_tok[:, 1], 0.0).then_inc(s_norm, 1)

            def aux(i, k, t):
                src = aux_home(i, k)
                if t[0] == "pr":
                    _, par, n = t
                    dve.wait_ge(aux_done, aux_count(i, k))
                    if not (i is None and n < 2):
                        dve.wait_ge(s_rope, pr_count(i, par, n) - 1)
                    for dst, w in ((t_cos, 0), (t_sin, 1)):
                        ins = dve.tensor_tensor(dst[:, n % 2].rearrange("p (a h) c -> p a h c", a=2),
                                                src[:].rearrange("p (a h c) -> p a h c", a=2, h=GH),
                                                rope[:, n, w].unsqueeze(2).to_broadcast([P, 2, GH, RD]), ALU.mult)
                    ins.then_inc(s_sin, 1)
                elif t[0] in ("tq", "tk"):
                    s, n = t[1], (0 if i is None else 2 * IT_HEADS * i) + 2 * t[1] + (1 if t[0] == "tq" else 2)
                    dve.wait_ge(s_qk, n)
                    hl = (qT if t[0] == "tq" else kT)[:, s % 2]
                    dve.tensor_tensor(hl[:, 1, :], src[:], hl[:, 0, :].bitcast(F32), ALU.subtract).then_inc(s_ql, 1)
                elif t[0] == "ab":
                    _, par, n = t
                    dve.wait_ge(aux_done, aux_count(i, k))
                    dve.tensor_copy(qk_tok[:, par, n, 0, :, RD:], src[:, 0:GH * KL]
                                    .rearrange("p (h c) -> p h c", h=GH)).then_inc(s_ab, 1)
                elif t[0] == "ot":
                    _, par, n = t
                    dve.wait_ge(s_ot, 4 * i + (0 if par else 2) + n + 1)
                    dve.tensor_tensor(oT[:, par, n, 1, :], src[:], oT[:, par, n, 0, :].bitcast(F32), ALU.subtract)\
                        .then_inc(s_ol, 1)
                elif t[0] == "op":
                    _, par, n = t
                    dve.wait_ge(aux_done, aux_count(i, k))
                    dve.wait_ge(s_x, 4 * i + (0 if par else 2) + n + 1)
                    dve.tensor_tensor(y_gate[:, n], src[:].rearrange("p (q n) -> p q n", q=2),
                                      gate[:, bass.ds(out_slot(i, par), 1), 0, :].to_broadcast([P, 2, D]),
                                      ALU.mult).then_inc(s_yg, 1)

            def row_max(i, u):
                dve.wait_ge(s_score, (0 if i is None else UNITS * i) + u + 1)
                dve.tensor_reduce(nmax[:, u % 4:u % 4 + 1], score_bank[u % 2][:], AX_X, ALU.max, negate=True)\
                    .then_inc(s_max, 1)

            def normalise(i, s):
                dve.wait_ge(s_pv, UNITS * i + TB * (s + 1))
                dve.reciprocal(rinv[:, s % 2, :], rsum[:, s % 2, :]).then_inc(s_rinv, 1)
                dve.wait_ge(s_rinv, IT_HEADS * i + s + 1)
                hh = s % GH
                dve.tensor_tensor(o_tok[:, s // GH, :, hh * KL:(hh + 1) * KL],
                                  out_bank[s % 2][:, 0:TB * KL].rearrange("p (q c) -> p q c", q=TB),
                                  rinv[:, s % 2, :].unsqueeze(2).to_broadcast([P, TB, KL]), ALU.mult).then_inc(s_norm, 1)

            dve.wait_ge(p_hhi, NB)
            dve.wait_ge(p_hlo, NB)
            for k, t in enumerate(AUX_FIRST):
                aux(None, k, t)
                if t[0] == "ab":
                    row_modulations(t[2])
                    if t[2] < 2:
                        split_latents(2 + t[2])
            for u in range(AHEAD):
                row_max(None, u)
            for q in mb_st:
                dve.wait_ge(q, 32)
            value_weights()
            with dve.Fori(0, ITERS) as i:
                for u in range(UNITS):
                    row_max(i, u + AHEAD)
                    for k, t in AUX_K[u]:
                        aux(i, k, t)
                    if u % TB == TB - 1:
                        normalise(i, u // TB)

            def second_statistics(first_b, last_b):
                for t in range(first_b * TB, last_b * TB):
                    ins = dve.bn_stats(bst2[:, t, :], xa[:, TB + t, :])
                chain(ins)
                for t in range(first_b * TB, last_b * TB):
                    ins = dve.bn_aggr(mv2[:, t, :], bst2[:, t, :])
                ins.then_inc(f_stat, 1)

            dve.wait_ge(s_x, 4 * ITERS + 2)
            second_statistics(0, NB - 1)
            for k, t in enumerate(LAST):
                aux(ITERS, k, t)

            dve.wait_ge(s_x, 4 * ITERS + 4)
            dve.wait_ge(s_norm, IT_HEADS * ITERS + 1)
            second_statistics(NB - 1, NB)
            for b in range(NB):
                dve.wait_ge(f_rstd, 2 if b == NB - 1 else 1)
                rows = h2[:, b * TB:(b + 1) * TB, 0:D]
                for t in range(b * TB, (b + 1) * TB):
                    ins = dve.tensor_scalar(h2[:, t, 0:D], xa[:, TB + t, :], mv2[:, t, 0:1], rstd2[:, t:t + 1],
                                            ALU.subtract, ALU.mult)
                if b == ASIDE:
                    ins.then_inc(f_centred, 1)
                    continue
                chain(ins)
                dve.wait_ge(mb_ld[b % 2], 16 * (b // 2 + 1))
                chain(dve.tensor_tensor(rows, rows, modb[:, b % 2, 1:2, :].to_broadcast([P, TB, D]), ALU.mult))
                dve.tensor_tensor(rows, rows, modb[:, b % 2, 0:1, :].to_broadcast([P, TB, D]), ALU.add).then_inc(f_h2, 1)
            dve.wait_ge(w_h, 1)
            dve.tensor_tensor(w_lo[:, E:], w_raw[:, E:], w_hi[:, E:].bitcast(F32), ALU.subtract).then_inc(w_l, 1)

            dve.wait_ge(f_sg, NB)
            chain(dve.tensor_scalar(sg[:], sg[:], 1.0, None, ALU.add))
            chain(dve.reciprocal(sg[:], sg[:]))
            chain(dve.tensor_reduce(gm[:], sg[:].rearrange("p t (g e) -> p t g e", g=EG), AX_X, ALU.max))
            rival = gm[:].unsqueeze(2).to_broadcast([P, NT, EG, EG])
            me = gm[:].unsqueeze(3).to_broadcast([P, NT, EG, EG])
            dve.tensor_tensor(gtm, rival, me, ALU.is_gt)
            chain(dve.tensor_tensor(gem, rival, me, ALU.is_equal))
            chain(dve.tensor_tensor(gem.rearrange("p t a b -> p t (a b)"), gem.rearrange("p t a b -> p t (a b)"),
                                    early_s[:].rearrange("p a b -> p (a b)").unsqueeze(1).to_broadcast([P, NT, EG * EG]),
                                    ALU.mult))
            chain(dve.tensor_tensor(gtm, gtm, gem, ALU.add))
            chain(dve.tensor_reduce(gsel[:], gtm, AX_X, ALU.add))
            chain(dve.tensor_scalar(gsel[:], gsel[:], float(TOPG), None, ALU.is_lt))
            chain(dve.tensor_tensor(msk[:].rearrange("p t (g e) -> p (t g) e", g=EG), sg[:].rearrange("p t (g e) -> p (t g) e", g=EG),
                                    gsel[:].rearrange("p t g -> p (t g)").unsqueeze(2).to_broadcast([P, NT * EG, E // EG]),
                                    ALU.mult))
            for t in range(NT):
                ins = dve.max(top[:, t, :], msk[:, t, :])
            chain(ins)
            least = top[:, :, TOPK - 1:TOPK].to_broadcast([P, NT, E])
            dve.tensor_tensor(above[:], msk[:], least, ALU.is_gt)
            chain(dve.tensor_tensor(equal[:], msk[:], least, ALU.is_equal))
            chain(dve.tensor_reduce(quota[:], above[:], AX_X, ALU.add))
            chain(dve.tensor_scalar(quota[:], quota[:], -1.0, float(TOPK), ALU.mult, ALU.add))
            src, n, step = equal[:], 0, 1
            while step < E:
                dst = pre[:, n % 2]
                dve.tensor_copy(dst[:, :, 0:step], src[:, :, 0:step])
                chain(dve.tensor_tensor(dst[:, :, step:], src[:, :, step:], src[:, :, 0:E - step], ALU.add))
                src, n, step = dst, n + 1, 2 * step
            chain(dve.tensor_tensor(src, src, quota[:].unsqueeze(2).to_broadcast([P, NT, E]), ALU.is_le))
            chain(dve.tensor_tensor(src, src, equal[:], ALU.mult))
            chain(dve.tensor_tensor(above[:], src, above[:], ALU.add))
            chosen = above[:]
            dve.memset(ones[:], 1.0).then_inc(masked, 1)
            weights = h2[:, :, X_W:X_W + E]
            chain(dve.tensor_tensor(equal[:], chosen, sg[:], ALU.mult))
            chain(dve.tensor_reduce(den[:], equal[:], AX_X, ALU.add))
            chain(dve.reciprocal(den[:], den[:]))
            dve.tensor_tensor(weights, equal[:], den[:].unsqueeze(2).to_broadcast([P, NT, E]), ALU.mult)
            src, n, step = chosen, 0, 1
            while step < E:
                dst = pre[:, n % 2]
                dve.tensor_copy(dst[:, :, 0:step], src[:, :, 0:step])
                chain(dve.tensor_tensor(dst[:, :, step:], src[:, :, step:], src[:, :, 0:E - step], ALU.add))
                src, n, step = dst, n + 1, 2 * step
            chain(dve.tensor_tensor(msk[:], src, chosen, ALU.mult))
            chain(dve.tensor_scalar(msk[:], msk[:], -1.0, None, ALU.add))
            rank = msk[:]
            dve.tensor_tensor(h2[:, :, X_DEST:], rank, token_s.unsqueeze(2).to_broadcast([P, NT, E]), ALU.add).then_inc(extended, 1)
            dve.wait_ge(counted, 1)
            within_tile = bank[6][:, 0:NT * E].rearrange("p (t e) -> p t e", t=NT)
            in_tile = bank[6][:, NT * E:].rearrange("p (t e) -> p t e", t=NT)
            dve.memset(pre[:, 0, 0:1, :], 0.0)
            chain(dve.tensor_copy(pre[:, 0, 1:, :], in_tile[:, 0:NT - 1, :]))
            src, n, step = pre[:, 0], 1, 1
            while step < NT:
                dst = pre[:, n % 2]
                dve.tensor_copy(dst[:, 0:step, :], src[:, 0:step, :])
                chain(dve.tensor_tensor(dst[:, step:, :], src[:, step:, :], src[:, 0:NT - step, :], ALU.add))
                src, n, step = dst, n + 1, 2 * step
            before, other = src, pre[:, n % 2]
            chain(dve.tensor_tensor(loads[:].unsqueeze(1), before[:, NT - 1:NT, :], in_tile[:, NT - 1:NT, :], ALU.add))
            chain(dve.tensor_tensor(other, loads[:].unsqueeze(2).to_broadcast([P, E, NT]),
                                    full_s.unsqueeze(1).to_broadcast([P, E, NT]), ALU.is_gt))
            dve.memset(tiles_of[:, 0, 0:1], 0.0)
            chain(dve.tensor_reduce(tiles_of[:, 0, 1:], other, AX_X, ALU.add))
            n, step = 0, 1
            while step < E:
                a, z = tiles_of[:, n % 2], tiles_of[:, (n + 1) % 2]
                dve.tensor_copy(z[:, 0:step], a[:, 0:step])
                chain(dve.tensor_tensor(z[:, step:], a[:, step:], a[:, 0:E + 1 - step], ALU.add))
                n, step = n + 1, 2 * step
            first_tile = tiles_of[:, n % 2]
            scaled = tiles_of[:, (n + 1) % 2]
            chain(dve.tensor_scalar(scaled, first_tile, float(P), None, ALU.mult))
            chain(dve.tensor_tensor(other, before, within_tile, ALU.add))
            chain(dve.tensor_tensor(other, other, scaled[:, 0:E].unsqueeze(1).to_broadcast([P, NT, E]), ALU.add))
            for r in range(TOPK):
                ins = dve.scalar_tensor_tensor(out=picked[:, :, r, :], in0=rank, scalar=float(r), in1=other,
                                               op0=ALU.is_equal, op1=ALU.mult)
            chain(ins)
            chain(dve.tensor_reduce(slot_f[:], picked, AX_X, ALU.add))
            dve.tensor_copy(slot_i[:], slot_f[:]).then_inc(indexed, 1)
            chain(dve.memset(first_tile[:, E:], float(2 * SLOT_TILES)))
            half = SLOT_TILES // 2
            for z in range(2):
                part = slice(z * half, (z + 1) * half)
                chain(dve.tensor_tensor(started, first_tile.unsqueeze(1).to_broadcast([P, half, E + 1]),
                                        tile_s[:, part].unsqueeze(2).to_broadcast([P, half, E + 1]), ALU.is_le))
                dve.tensor_tensor(owner[:, part, :], started[:, :, 0:E], started[:, :, 1:], ALU.subtract)
                chain(dve.tensor_reduce(own_f[:, part], started[:, :, 0:E], AX_X, ALU.add))
            chain(dve.tensor_scalar(own_f, own_f, -1.0, None, ALU.add))
            digits = SLOT_TILES - PACK + 1
            src = own_f[:, PACK - 1:SLOT_TILES]
            for d in range(PACK - 2, -1, -1):
                dst = packed_f[:, d % 2, :]
                chain(dve.scalar_tensor_tensor(out=dst, in0=src, scalar=float(E), in1=own_f[:, d:d + digits],
                                               op0=ALU.mult, op1=ALU.add))
                src = dst
            dve.tensor_copy(own_i[:, 0:digits], src).then_inc(listed, 1)

            x_bank, h_bank, g_bank, y_bank = bank[0:2], bank[2:4], bank[4:6], bank[6:8]

            def shared_position(t, par):
                if within(t + 2, NT):
                    dve.wait_ge(z_hi, t + 3)
                    if not (static(t) and t < 0):
                        dve.wait_ge(z_h, 2 * (t + 1))
                    dve.tensor_tensor(x_hl[:, par, 1, :], x_bank[par][:, 0:D], x_hl[:, par, 0, :].bitcast(F32),
                                      ALU.subtract).then_inc(z_lo, 1)

                def gate_half(c):
                    if not within(t + 1, NT):
                        return
                    dve.wait_ge(z_sl, 2 * (t + 1) + c + 1)
                    if not (static(t) and t + 1 == 0):
                        dve.wait_ge(z_gt, 2 * (t + 1) + c - 1)
                    dve.tensor_tensor(g_s[:, c, :], h_bank[c][:, FI:2 * FI], sl[:, c, :], ALU.mult).then_inc(z_g, 1)

                def copy_turned(u, c):
                    if not within(u, NT):
                        return
                    dve.wait_ge(z_gt, 2 * u + c + 1)
                    dve.tensor_copy(gT[:, c].rearrange("p c t -> p (c t)"), g_bank[c][0:FC, 0:2 * P]).then_inc(z_gTc, 1)

                gate_half(0)
                copy_turned(t, 1)
                gate_half(1)
                copy_turned(t + 1, 0)
                if within(t, NT):
                    dve.wait_ge(z_y, t + 1)
                    slot = t // TB + 1
                    g2 = gate[:, slot, 1, :] if static(t) else gate[:, bass.ds(slot, 1), 1, :].rearrange("p a n -> p (a n)")
                    dve.tensor_tensor(zg, y_bank[par][:, 0:D], g2, ALU.mult).then_inc(z_zg, 1)
                    dve.wait_ge(w_h, t + 2)
                    dve.tensor_tensor(w_lo[:, bass.ds(t, 1)].rearrange("p a k n -> p (a k n)"),
                                      w_raw[:, bass.ds(t, 1)].rearrange("p a k n -> p (a k n)"),
                                      w_hi[:, bass.ds(t, 1)].bitcast(F32).rearrange("p a k n -> p (a k n)"),
                                      ALU.subtract).then_inc(w_l, 1)
                    dve.wait_ge(z_zg, t + 1)
                    row = xa[:, bass.ds(t + TB, 1), :].rearrange("p a n -> p (a n)")
                    dve.tensor_tensor(row, row, zg, ALU.add)

            shared_steps(dve, shared_position)

            def expert_position(n, j):
                if within(n + 3, SLOT_TILES):
                    m, jm = n + 3, (j + 3) % CYCLE
                    dve.wait_ge(ld_s[jm], 16 * ((m // CYCLE) + 1))
                    dve.tensor_tensor(chosen_by[:, jm], xs[:, jm, X_W:].rearrange("p (a e) -> p a e", a=2),
                                      owner[:, bass.ds(m, 1), :].to_broadcast([P, 2, E]), ALU.mult).then_inc(e_mul, 1)
                    dve.wait_ge(e_hi, m + 1)
                    if not (static(m) and m < 2):
                        dve.wait_ge(e_h, m - 1)
                    dve.tensor_tensor(x_hl[:, jm % 2, 1, :], x_bank[jm % 2][:, 0:D], x_hl[:, jm % 2, 0, :].bitcast(F32),
                                      ALU.subtract).then_inc(e_lo, 1)
                    dve.wait_ge(e_mul, m + 1)
                    dve.tensor_reduce(sel[:, jm], chosen_by[:, jm], AX_X, ALU.add).then_inc(e_sel, 1)
                if within(n + 2, SLOT_TILES):
                    m, jm, par = n + 2, (j + 2) % CYCLE, j % 2
                    dve.wait_ge(e_sl, m + 1)
                    if static(m) and m < 2:
                        dve.wait_ge(z_gt, 2 * NT)
                    else:
                        dve.wait_ge(e_gt, m - 1)
                    dve.wait_ge(e_sel, m + 1)
                    dve.scalar_tensor_tensor(out=g_s[:, par, :], in0=h_bank[par][:, FI:2 * FI], scalar=sel[:, jm, 0:1],
                                             in1=sl[:, par, :], op0=ALU.mult, op1=ALU.mult).then_inc(e_g, 1)
                    if not (static(m) and m < CYCLE):
                        dve.wait_ge(e_put[jm], 16 * (m // CYCLE))
                    dve.tensor_copy(sel_i[:, jm:jm + 1], sel[:, jm, 1:2]).then_inc(e_idx, 1)
                if within(n + 1, SLOT_TILES):
                    m, par = n + 1, (j + 1) % 2
                    dve.wait_ge(e_gt, m + 1)
                    if not (static(m) and m < 2):
                        dve.wait_ge(e_y, m - 1)
                    dve.tensor_copy(gT[:, par].rearrange("p c t -> p (c t)"), g_bank[par][0:FC, 0:2 * P]).then_inc(e_gTc, 1)

            expert_steps(dve, expert_position)

            for t in range(NT):
                dve.wait_ge(ld_y[t % 4], 16 * (t // 4 + 1))
                if t >= 2:
                    dve.wait_ge(y_gat, t - 1)
                dve.tensor_reduce(ysum[:, t % 2], yb[:, t % 4].rearrange("p (r d) -> p d r", r=TOPK), AX_X, ALU.add)\
                    .then_inc(y_sum, 1)
                dve.wait_ge(y_sum, t + 1)
                if t >= 2:
                    dve.wait_ge(y_add, t - 1)
                dve.tensor_tensor(ygate[:, t % 2], ysum[:, t % 2], gate[:, t // TB + 1, 1, :], ALU.mult).then_inc(y_gat, 1)

        @block.scalar
        def _(act):
            act.wait_ge(ld_a, 48)
            act.activation(cexp[:], cT_s[:], ACT.Exp, scale=-1.0).then_inc(c_exp, 1)
            def split_latents(b):
                act.wait_ge(p_ctr, b + 1)
                if b > 1:
                    act.wait_ge(p_cst, 16 * (b - 1))
                act.activation(cq_slot(b)[:, 0], pt_bank[b % 2][0:QL, :], ACT.Copy).then_inc(p_chi, 1)

            for b in range(NB):
                act.wait_ge(p_h, KD * (b + 1))
                if b > 1:
                    act.wait_ge(p_st, 16 * (b - 1))
                act.activation(h_slot(b)[:, 0], h_f[:], ACT.Copy).then_inc(p_hhi, 1)
            act.wait_ge(zeroed, 2)
            split_latents(0)
            act.wait_ge(ld_b, 48)
            act.activation(wr_hi[:].rearrange("p k g n -> p (k g n)"), wr_raw, ACT.Copy).then_inc(wr_h, 1)
            act.wait_ge(ab_ev, 2)
            act.activation(ab_hi[0:QL], ab_f[:], ACT.Copy).then_inc(ab_h, 1)
            act.wait_ge(p_st, 16 * (NB - 1))
            split_latents(1)
            split_latents(2)
            split_latents(3)

            def aux(i, k, t):
                if t[0] in ("tq", "tk"):
                    s = t[1]
                    act.wait_ge(aux_done, aux_count(i, k))
                    act.activation((qT if t[0] == "tq" else kT)[:, s % 2, 0, :], aux_home(i, k)[:], ACT.Copy).then_inc(s_qk, 1)
                elif t[0] == "ot":
                    act.wait_ge(aux_done, aux_count(i, k))
                    act.activation(oT[:, t[1], t[2], 0, :], aux_home(i, k)[:], ACT.Copy).then_inc(s_ot, 1)

            def copy_probs(i, u):
                act.wait_ge(s_pt, (0 if i is None else UNITS * i) + u + 1)
                act.activation(probT[:, u % 2, :], pt_bank[u % 2][:], ACT.Copy).then_inc(s_ptc, 1)

            def exponentials(i, u):
                act.wait_ge(s_max, (0 if i is None else UNITS * i) + u + 1)
                s, q = (u // TB) % 2, u % TB
                act.activation(prob[:, u % 2, :], score_bank[u % 2][:], ACT.Exp, bias=nmax[:, u % 4:u % 4 + 1],
                               accum_out=rsum[:, s, q:q + 1]).then_inc(s_exp, 1)

            act.wait_ge(p_cst, 16 * (NB - 1))
            for k, t in enumerate(AUX_FIRST):
                aux(None, k, t)
            for u in range(2):
                exponentials(None, u)
            copy_probs(None, 0)
            exponentials(None, 2)
            for q in mb_st:
                act.wait_ge(q, 32)
            for q in range(4):
                act.wait_ge(m_mm, q + 1)
                act.activation(mout[:, 0, 2 * q:2 * q + 2, :], out_bank[q % 2][:].rearrange("p (a n) -> p a n", a=2),
                               ACT.Copy, scale=kvw2_s[:, 0:1]).then_inc(m_h, 1)
            with act.Fori(0, ITERS) as i:
                for u in range(UNITS):
                    copy_probs(i, u + 1)
                    exponentials(i, u + AHEAD)
                    for k, t in AUX_K[u]:
                        aux(i, k, t)
            for k, t in enumerate(LAST):
                aux(ITERS, k, t)

            def gate_exponentials(n):
                b = LOGIT_ORDER[n]
                act.wait_ge(f_lg, n + 1)
                act.activation(sg[:, b * TB:(b + 1) * TB, :], bank[(2, 5)[n % 2]][:, b * TB * E:(b + 1) * TB * E]
                               .rearrange("p (t e) -> p t e", t=TB), ACT.Exp, scale=-1.0).then_inc(f_sg, 1)

            for n in range(NB):
                act.wait_ge(f_tr, n + 1)
                if n >= 2:
                    act.wait_ge(f_lg, n - 1)
                for k in range(KD):
                    ins = act.activation(h2T[:, n % 2, k, :], bank[(0, 3)[n % 2] + k][:], ACT.Copy)
                ins.then_inc(f_h2T, 1)
                if n > 0:
                    gate_exponentials(n - 1)
            gate_exponentials(NB - 1)
            act.wait_ge(ld_ws, 16)
            act.activation(w_hi[:, E:], w_raw[:, E:], ACT.Copy).then_inc(w_h, 1)

            x_bank, h_bank, g_bank, y_bank = bank[0:2], bank[2:4], bank[4:6], bank[6:8]

            act.wait_ge(f_h2, NB - 1)
            act.wait_ge(f_h2p, 1)

            def fetch(t):
                act.activation(x_now[:], h2[:, bass.ds(t, 1), 0:D].rearrange("p a n -> p (a n)"), ACT.Copy).then_inc(z_now, 1)

            fetch(0)

            def shared_position(t, par):
                if within(t + 2, NT):
                    act.wait_ge(z_x, t + 3)
                    if not (static(t) and t < 0):
                        act.wait_ge(z_h, 2 * (t + 1))
                    act.activation(x_hl[:, par, 0, :], x_bank[par][:, 0:D], ACT.Copy).then_inc(z_hi, 1)
                if within(t + 3, NT):
                    fetch(t + 3)
                if within(t + 1, NT):
                    for c in range(2):
                        act.wait_ge(z_h, 2 * (t + 1) + c + 1)
                        if not (static(t) and t + 1 == 0):
                            act.wait_ge(z_g, 2 * (t + 1) + c - 1)
                        act.activation(sl[:, c, :], h_bank[c][:, 0:FI], ACT.Silu).then_inc(z_sl, 1)
                if within(t, NT):
                    if static(t) and t == 0:
                        act.wait_ge(ld_w, 64)
                    act.activation(w_hi[:, bass.ds(t, 1)].rearrange("p a k n -> p (a k n)"),
                                   w_raw[:, bass.ds(t, 1)].rearrange("p a k n -> p (a k n)"), ACT.Copy).then_inc(w_h, 1)

            shared_steps(act, shared_position)

            def expert_position(n, j):
                if within(n + 3, SLOT_TILES):
                    m, par = n + 3, (j + 3) % 2
                    act.wait_ge(e_x, m + 1)
                    if static(m) and m < 2:
                        act.wait_ge(z_h, 2 * NT)
                    else:
                        act.wait_ge(e_h, m - 1)
                    act.activation(x_hl[:, par, 0, :], x_bank[par][:, 0:D], ACT.Copy).then_inc(e_hi, 1)
                if within(n + 2, SLOT_TILES):
                    m, par = n + 2, j % 2
                    act.wait_ge(e_h, m + 1)
                    if static(m) and m < 2:
                        act.wait_ge(z_g, 2 * NT)
                    else:
                        act.wait_ge(e_g, m - 1)
                    act.activation(sl[:, par, :], h_bank[par][:, 0:FI], ACT.Silu).then_inc(e_sl, 1)
                if within(n, SLOT_TILES):
                    act.wait_ge(e_y, n + 1)
                    if not (static(n) and n < CYCLE):
                        act.wait_ge(e_put[j], 16 * (n // CYCLE))
                    act.activation(ys[:, j], y_bank[j % 2][:, 0:D], ACT.Copy).then_inc(e_yc, 1)

            expert_steps(act, expert_position)

        @block.gpsimd
        def _(pool):
            own = [0]

            def chain(ins):
                own[0] += 1
                ins.then_inc(pool_c, 1)
                pool.wait_ge(pool_c, own[0])

            pool.memset(xa[:, 0:TB, :], 0.0).then_inc(s_x, 1)
            pool.memset(idle[:, 0:1], 0.0).then_inc(s_x, 1)
            pool.memset(pad[:, 0:X_W], 0.0).then_inc(pad_set, 1)
            pool.memset(pad[:, X_W:X_DEST], 0.0).then_inc(pad_set, 1)
            pool.memset(pad[:, X_DEST:], float(NOWHERE)).then_inc(pad_set, 1)
            pool.memset(gate[:, 0], 0.0).then_inc(zeroed, 1)
            chain(pool.memset(mhalf[:], -0.5))
            pool.memset(ab_hi[:].bitcast(F32), 0.0)
            pool.memset(ab_lo[:].bitcast(F32), 0.0)
            pool.memset(cq_st[:].bitcast(F32), 0.0).then_inc(zeroed, 1)
            def inverse_deviations(half):
                pool.wait_ge(p_stat, half + 1)
                chain(pool.tensor_scalar(ve[:, half, 0, :], mv[:, half * 2 * TB:(half + 1) * 2 * TB, 1], EPS_LN, None, ALU.add))
                pool.tensor_tensor(rstd[:, half], ve[:, half, 0, :], mhalf[:, 0:2 * TB], ALU.pow).then_inc(p_rstd, 1)

            def split_inputs(b):
                pool.wait_ge(p_hhi, b + 1)
                if b > 1:
                    pool.wait_ge(p_st, 16 * (b - 1))
                pool.tensor_tensor(h_slot(b)[:, 1].rearrange("p k t -> p (k t)"), h_f[:].rearrange("p k t -> p (k t)"),
                                   h_slot(b)[:, 0].bitcast(F32).rearrange("p k t -> p (k t)"), ALU.subtract).then_inc(p_hlo, 1)

            def inverse_norms(half):
                pool.wait_ge(p_ssq, half + 1)
                pool.tensor_scalar(ve[:, half, 1, :], ssq[:, half, 0, :], 1.0 / QL, EPS_RMS, ALU.mult, ALU.add)
                chain(pool.tensor_scalar(ve[:, half, 2, :], ssq[:, half, 1, :], 1.0 / KL, EPS_RMS, ALU.mult, ALU.add))
                pool.tensor_tensor(rms[:, half].rearrange("p a t -> p (a t)"), ve[:, half, 1:3, :].rearrange("p a t -> p (a t)"),
                                   mhalf[:], ALU.pow).then_inc(p_rms, 1)

            inverse_deviations(0)
            split_inputs(0)
            inverse_deviations(1)
            split_inputs(1)
            inverse_norms(0)
            split_inputs(2)
            split_inputs(3)
            inverse_norms(1)

            def aux(i, k, t):
                if t[0] == "pr":
                    _, par, n = t
                    pool.wait_ge(s_sin, pr_count(i, par, n) + 1)
                    dst = qk_tok[:, par, n].rearrange("p a h c -> p (a h) c")
                    half = RD // 2
                    pool.tensor_tensor(dst[:, :, 0:half], t_cos[:, n % 2, :, 0:half], t_sin[:, n % 2, :, half:],
                                       ALU.subtract)
                    pool.tensor_tensor(dst[:, :, half:RD], t_cos[:, n % 2, :, half:], t_sin[:, n % 2, :, 0:half],
                                       ALU.add).then_inc(s_rope, 1)
                    tile = n if i is None else prep_batch(i, par) * TB + n
                    pool.tensor_copy(qk_tok[:, par, n, 1, :, RD:],
                                     ckv[:, bass.ds(tile, 1), :].to_broadcast([P, GH, KL])).then_inc(s_ck, 1)
                elif t[0] == "op":
                    _, par, n = t
                    c = 4 * i + (0 if par else 2) + n
                    pool.wait_ge(s_yg, c + 1)
                    pool.wait_ge(s_x, c + 2)
                    rows = xa[:, bass.ds(out_slot(i, par) * TB + 2 * n, 2), :]
                    pool.tensor_tensor(rows, rows, y_gate[:, n], ALU.add).then_inc(s_x, 1)

            for k, t in enumerate(AUX_FIRST):
                aux(None, k, t)
            with pool.Fori(0, ITERS) as i:
                for u in range(UNITS):
                    for k, t in AUX_K[u]:
                        aux(i, k, t)

            def second_deviations(n, tiles):
                pool.wait_ge(f_stat, n + 1)
                chain(pool.tensor_scalar(ve2[:, tiles], mv2[:, tiles, 1], EPS_LN, None, ALU.add))
                pool.tensor_tensor(rstd2[:, tiles], ve2[:, tiles], mhalf[:, 0:tiles.stop - tiles.start], ALU.pow).then_inc(f_rstd, 1)

            second_deviations(0, slice(0, (NB - 1) * TB))
            for k, t in enumerate(LAST):
                aux(ITERS, k, t)

            second_deviations(1, slice((NB - 1) * TB, NT))
            rows = h2[:, ASIDE * TB:(ASIDE + 1) * TB, 0:D]
            pool.wait_ge(mb_ld[ASIDE % 2], 16)
            pool.wait_ge(f_centred, 1)
            chain(pool.tensor_tensor(rows, rows, modb[:, ASIDE % 2, 1:2, :].to_broadcast([P, TB, D]), ALU.mult))
            pool.tensor_tensor(rows, rows, modb[:, ASIDE % 2, 0:1, :].to_broadcast([P, TB, D]), ALU.add).then_inc(f_h2p, 1)
            pool.wait_ge(padded, 16 * ITERS)
            pool.wait_ge(indexed, 1)
            pool.wait_ge(extended, 1)
            pool.wait_ge(f_h2, NB - 1)
            pool.wait_ge(f_h2p, 1)
            for t in range(NT):
                for r in range(TOPK):
                    pool.indirect_dma_start(slots, bass.IndirectOffsetOnAxis(ap=slot_i[:, t, r:r + 1], axis=0),
                                            h2[:, t, :], None).then_inc(sent, 16)

            last_part = pool.to_reg(NOWHERE - 1)

            def expert_position(n, j):
                if within(n, SLOT_TILES):
                    pool.wait_ge(e_yc, n + 1)
                    pool.wait_ge(e_idx, n + 1)
                    if not (static(n) and n == 0):
                        pool.wait_ge(e_go, n)
                    pool.tensor_tensor(idle[:, 1:2], mhalf[:, 0:1], mhalf[:, 0:1], ALU.add).then_inc(e_go, 1)
                    pool.indirect_dma_start(parts, bass.IndirectOffsetOnAxis(ap=sel_i[:, j:j + 1], axis=0),
                                            ys[:, j], None, bounds_check=last_part, oob_is_err=False).then_inc(e_put[j], 16)

            expert_steps(pool, expert_position)

            for t in range(NT):
                pool.wait_ge(y_gat, t + 1)
                row = xa[:, t + TB, :]
                pool.tensor_tensor(row, row, ygate[:, t % 2], ALU.add).then_inc(y_add, 1)


def route_constants():
    tab = np.zeros((P, R_ALL), np.float32)
    tab[:, R_EARLY:R_TRI] = np.tril(np.ones((EG, EG), np.float32), -1).reshape(1, -1)
    tab[:, R_TRI:R_FULL] = np.triu(np.ones((P, P), np.float32), 1)
    tab[:, R_FULL:R_TILE] = P * np.arange(NT, dtype=np.float32)
    tab[:, R_TILE:R_TOKEN] = np.arange(SLOT_TILES, dtype=np.float32)
    tab[:, R_TOKEN:R_ALL] = TOPK * np.arange(NT * P, dtype=np.float32).reshape(NT, P).T
    return tab


def rope_constants():
    freqs = (1.0 / 10000.0 ** (np.arange(0, RD, 2, dtype=np.float32) / np.float32(RD))).astype(np.float32)
    ang = np.outer(np.arange(SEQ, dtype=np.float32), freqs).astype(np.float32)
    t = np.stack([np.cos(ang), np.sin(ang)]).astype(np.float32)
    t = np.concatenate([t, t], axis=-1)
    t = np.stack([t * np.float32(SCALE), t], axis=1)
    return np.ascontiguousarray(t.reshape(2, 2, TB, P, RD).transpose(3, 2, 0, 1, 4))


def lay_out(inputs):
    a = {k: np.asarray(v) for k, v in inputs.items()}

    def rows(w, n):
        return w.reshape(n, P, -1).transpose(1, 0, 2)

    def heads(w, r):
        return w.reshape(r, H, HD).transpose(2, 1, 0)

    def rotary(w):
        return w.reshape(D, NG, 1, GH, RD // 2, 2).transpose(0, 1, 2, 3, 5, 4)

    r = np.concatenate([rotary(a["L0_attn_Wq_rope"]), rotary(a["L0_attn_Wk_rope"])], axis=2).reshape(D, NG * 512)
    out = {
        "x": a["L0_attn_x"].reshape(NT * P, D),
        "cT": rows(a["L0_c"].T, KD),
        "wmod": rows(a["L0_wmod"], KD),
        "wdn": rows(np.concatenate([a["L0_attn_Wq_down"], a["L0_attn_Wkv_down"]], axis=1), KD),
        "wqup": heads(a["L0_attn_Wq_up"], QL),
        "wkup": heads(a["L0_attn_Wk_up"], KL),
        "wvup": heads(a["L0_attn_Wv_up"], KL),
        "wout": a["L0_attn_Wout"].reshape(H, HD, D).transpose(1, 0, 2),
        "wrope": rows(r, KD).reshape(P, -1),
        "rope_tab": rope_constants(),
        "eye": np.eye(P, dtype=np.float32),
        "qnw": a["L0_attn_q_norm_w"].reshape(QL, 1),
        "kvw_bc": np.broadcast_to(a["L0_attn_kv_norm_w"], (QL, KL)),
        "kvw2": np.concatenate([a["L0_attn_kv_norm_w"]] * 2).reshape(P, 1),
    }

    def experts(w, ws):
        return np.concatenate([w, ws.reshape(2, FI, D)]).transpose(0, 2, 1)

    w13 = np.concatenate([experts(a["L0_ffn_W1"], a["L0_ffn_Ws1"]), experts(a["L0_ffn_W3"], a["L0_ffn_Ws3"])], axis=2)
    w2 = np.concatenate([a["L0_ffn_W2"].transpose(0, 2, 1), a["L0_ffn_Ws2"].T.reshape(2, FI, D)])
    out["wgate"] = rows(a["L0_ffn_gate_w"].T, KD)
    out["w13"] = w13.reshape(ES, KD, P, 2 * FI).transpose(2, 0, 1, 3)
    out["w2"] = w2.reshape(ES, 2, FC, D).transpose(2, 0, 1, 3)
    out["route"] = route_constants()
    return {k: np.ascontiguousarray(v) for k, v in out.items()}


def kernel(**inputs):
    import concourse.bacc as _bacc
    from concourse.bass_utils import run_bass_kernel_spmd as _run

    nc = _bacc.Bacc("TRN2", target_bir_lowering=False, num_devices=1)
    arrays = lay_out(inputs)
    args = {n: nc.dram_tensor(f"in_{n}", a.shape, mybir.dt.from_np(a.dtype), kind="ExternalInput").ap()
            for n, a in arrays.items()}
    args["out"] = nc.dram_tensor("out_x", (NT * P, D), F32, kind="ExternalOutput").ap()
    program(nc, **args)
    r = _run(nc, [{f"in_{n}": a for n, a in arrays.items()}], core_ids=[0])
    return r.results[0]["out_x"].reshape(NB, SEQ, D)
```
